# Optimizing a Trainium2 kernel written in Bass

```python
import numpy as np
import jax
import jax.numpy as jnp

def _softmax(x, axis=-1):
    return jax.nn.softmax(x, axis=axis)

def _gelu(x):
    return jax.nn.gelu(x, approximate=True)

def _silu(x):
    return jax.nn.silu(x)

def _sigmoid(x):
    return jax.nn.sigmoid(x)

def _layernorm(x, axis=-1, eps=1e-05):
    m = jnp.mean(x, axis=axis, keepdims=True)
    v = jnp.var(x, axis=axis, keepdims=True)
    return (x - m) / jnp.sqrt(v + eps)

def _scatter_add(tgt, idx, src, axis=0):
    return tgt.at[idx].add(src)

def _segment_sum(src, seg, n):
    return jax.ops.segment_sum(src, seg, n)
kernel_name = 'mk_hybrid_d1_jaxref_r8_a858be'

def setup_inputs(seed: int=0):
    np.random.seed(seed)
    _w = jnp.asarray

    def _L0_attn_a_setup():
        import jax, jax.numpy as jnp
        import numpy as np
        HID = 256
        H = 8
        DK = 128
        DV = 32
        KD = H * DK
        VD = H * DV
        CH = 64
        SC = 16
        GLN = 16.0
        LRD = 16
        EPS = 1e-05

        def _gla_forward(hidden_states, Wq, Wk, Wv, Wg, Wgk1, Wgk2, bgk2, Wo, ln_w, ln_b):
            B, T, _ = hidden_states.shape
            q = (hidden_states @ Wq).reshape(B, T, H, DK)
            k = (hidden_states @ Wk).reshape(B, T, H, DK)
            v = (hidden_states @ Wv).reshape(B, T, H, DV)
            gk = (hidden_states @ Wgk1 @ Wgk2 + bgk2).reshape(B, T, H, DK)
            gk = jax.nn.log_sigmoid(gk) / GLN
            NC = T // CH
            NS = CH // SC

            def chunked(x):
                return x.reshape(B, NC, CH, H, x.shape[-1]).transpose(1, 0, 2, 3, 4)
            qc, kc, vc, gc = (chunked(q), chunked(k), chunked(v), chunked(gk))
            tril = jnp.tril(jnp.ones((SC, SC), bool))

            def step(S, inp):
                bq, bk, bv, bg = inp
                Bc = jnp.cumsum(bg, axis=1)
                Blast = Bc[:, -1]
                eBlast = jnp.exp(Blast)
                q_exp = bq * eBlast[:, None]
                k_exp = bk * jnp.exp(Blast[:, None] - Bc)
                S_new = eBlast[..., None] * S + jnp.einsum('bchd,bche->bhde', k_exp, bv)
                O_inter = jnp.einsum('bchd,bhde->bche', q_exp, S_new)
                sq = bq.reshape(B, NS, SC, H, DK)
                sk = bk.reshape(B, NS, SC, H, DK)
                sv = bv.reshape(B, NS, SC, H, DV)
                sb = Bc.reshape(B, NS, SC, H, DK)
                P = jnp.einsum('bjmhd,bjnhd->bjmnh', sq * jnp.exp(sb), sk * jnp.exp(-sb))
                P = jnp.where(tril[None, None, :, :, None], P, 0.0)
                colsum = P.sum(axis=2)
                intra = colsum[..., None] * sv
                return (S_new, O_inter + intra.reshape(B, CH, H, DV))
            S0 = jnp.zeros((B, H, DK, DV), hidden_states.dtype)
            _, O = jax.lax.scan(step, S0, (qc, kc, vc, gc))
            o = O.transpose(1, 0, 2, 3, 4).reshape(B, T, H, DV)
            g = (hidden_states @ Wg).reshape(B, T, H, DV)
            x = o + g
            mu = x.mean(-1, keepdims=True)
            var = jnp.mean((x - mu) ** 2, axis=-1, keepdims=True)
            x = (x - mu) * jax.lax.rsqrt(var + EPS) * ln_w + ln_b
            return jax.nn.silu(x).reshape(B, T, VD) @ Wo
        key = jax.random.key(seed)
        ks = jax.random.split(key, 8)
        B, T = (2, 256)
        s = 0.02
        return {'hidden_states': jax.random.normal(ks[0], (B, T, HID), jnp.float32), 'Wq': jax.random.normal(ks[1], (HID, KD), jnp.float32) * s, 'Wk': jax.random.normal(ks[2], (HID, KD), jnp.float32) * s, 'Wv': jax.random.normal(ks[3], (HID, VD), jnp.float32) * s, 'Wg': jax.random.normal(ks[4], (HID, VD), jnp.float32) * s, 'Wgk1': jax.random.normal(ks[5], (HID, LRD), jnp.float32) * s, 'Wgk2': jax.random.normal(ks[6], (LRD, KD), jnp.float32) * s, 'bgk2': jnp.zeros((KD,), jnp.float32), 'Wo': jax.random.normal(ks[7], (VD, HID), jnp.float32) * s, 'ln_w': jnp.ones((DV,), jnp.float32), 'ln_b': jnp.zeros((DV,), jnp.float32)}
    _L0_attn_a_in = _L0_attn_a_setup()

    def _L0_attn_b_setup():
        import jax, jax.numpy as jnp
        import numpy as np
        import math
        DIM = 256
        N_HEADS = 16
        N_KV_HEADS = 8
        HEAD_DIM = DIM // N_HEADS
        N_REP = N_HEADS // N_KV_HEADS
        BLOCK = 128
        TOPK = 8
        NEG_INF = -10000.0
        SEQ = 512
        BS = 1

        def _rope_tables(seq_len, head_dim, base=10000.0):
            inv_freq = 1.0 / base ** (jnp.arange(0, head_dim, 2, dtype=jnp.float32) / head_dim)
            ang = jnp.arange(seq_len, dtype=jnp.float32)[:, None] * inv_freq[None, :]
            return (jnp.cos(ang), jnp.sin(ang))

        def _apply_rope(t, cos, sin):
            t1 = t[..., 0::2]
            t2 = t[..., 1::2]
            c = cos[None, :, None, :]
            s = sin[None, :, None, :]
            out_even = t1 * c - t2 * s
            out_odd = t1 * s + t2 * c
            out = jnp.stack([out_even, out_odd], axis=-1)
            return out.reshape(t.shape)
        key = jax.random.key(seed)
        ks = jax.random.split(key, 5)
        scale = 1.0 / math.sqrt(DIM)
        x = jax.random.normal(ks[0], (BS, SEQ, DIM), dtype=jnp.float32)
        wq = jax.random.normal(ks[1], (DIM, N_HEADS * HEAD_DIM), dtype=jnp.float32) * scale
        wk = jax.random.normal(ks[2], (DIM, N_KV_HEADS * HEAD_DIM), dtype=jnp.float32) * scale
        wv = jax.random.normal(ks[3], (DIM, N_KV_HEADS * HEAD_DIM), dtype=jnp.float32) * scale
        wo = jax.random.normal(ks[4], (DIM, DIM), dtype=jnp.float32) * scale
        return {'x': x, 'wq': wq, 'wk': wk, 'wv': wv, 'wo': wo}
    _L0_attn_b_in = _L0_attn_b_setup()

    def _L0_ffn_setup():
        import jax, jax.numpy as jnp
        import numpy as np
        EPS = 1e-08

        def _quantize(w):
            gamma = jnp.mean(jnp.abs(w))
            return jnp.clip(jnp.round(w / (gamma + EPS)), -1.0, 1.0)

        def _bitlinear(x, w):
            return jnp.matmul(x, _quantize(w).T)
        key = jax.random.key(seed)
        k1, k2, k3, k4 = jax.random.split(key, 4)
        d, h = (256, 704)
        x = jax.random.normal(k1, (4, 256, d), dtype=jnp.float32)
        w1 = jax.random.normal(k2, (h, d), dtype=jnp.float32)
        w2 = jax.random.normal(k3, (h, d), dtype=jnp.float32)
        w3 = jax.random.normal(k4, (d, h), dtype=jnp.float32)
        return {'x': x, 'w1': w1, 'w2': w2, 'w3': w3}
    _L0_ffn_in = _L0_ffn_setup()
    _d = {'L0_attn_a_hidden_states': _L0_attn_a_in['hidden_states'], 'L0_attn_a_Wq': _L0_attn_a_in['Wq'], 'L0_attn_a_Wk': _L0_attn_a_in['Wk'], 'L0_attn_a_Wv': _L0_attn_a_in['Wv'], 'L0_attn_a_Wg': _L0_attn_a_in['Wg'], 'L0_attn_a_Wgk1': _L0_attn_a_in['Wgk1'], 'L0_attn_a_Wgk2': _L0_attn_a_in['Wgk2'], 'L0_attn_a_bgk2': _L0_attn_a_in['bgk2'], 'L0_attn_a_Wo': _L0_attn_a_in['Wo'], 'L0_attn_a_ln_w': _L0_attn_a_in['ln_w'], 'L0_attn_a_ln_b': _L0_attn_a_in['ln_b'], 'L0_attn_b_wq': _L0_attn_b_in['wq'], 'L0_attn_b_wk': _L0_attn_b_in['wk'], 'L0_attn_b_wv': _L0_attn_b_in['wv'], 'L0_attn_b_wo': _L0_attn_b_in['wo'], 'L0_ffn_w1': _L0_ffn_in['w1'], 'L0_ffn_w2': _L0_ffn_in['w2'], 'L0_ffn_w3': _L0_ffn_in['w3']}
    _x0 = _d['L0_attn_a_hidden_states']
    _d['L0_attn_a_hidden_states'] = jax.random.normal(jax.random.fold_in(jax.random.key(seed), 1), (4, 256, 256), dtype=_x0.dtype)
    del _x0
    return _d

def reference(L0_attn_a_hidden_states, L0_attn_a_Wq, L0_attn_a_Wk, L0_attn_a_Wv, L0_attn_a_Wg, L0_attn_a_Wgk1, L0_attn_a_Wgk2, L0_attn_a_bgk2, L0_attn_a_Wo, L0_attn_a_ln_w, L0_attn_a_ln_b, L0_attn_b_wq, L0_attn_b_wk, L0_attn_b_wv, L0_attn_b_wo, L0_ffn_w1, L0_ffn_w2, L0_ffn_w3):

    def _L0_attn_a_ref(hidden_states, Wq, Wk, Wv, Wg, Wgk1, Wgk2, bgk2, Wo, ln_w, ln_b):
        import jax, jax.numpy as jnp
        import numpy as np
        HID = 256
        H = 8
        DK = 128
        DV = 32
        KD = H * DK
        VD = H * DV
        CH = 64
        SC = 16
        GLN = 16.0
        LRD = 16
        EPS = 1e-05

        def _gla_forward(hidden_states, Wq, Wk, Wv, Wg, Wgk1, Wgk2, bgk2, Wo, ln_w, ln_b):
            B, T, _ = hidden_states.shape
            q = (hidden_states @ Wq).reshape(B, T, H, DK)
            k = (hidden_states @ Wk).reshape(B, T, H, DK)
            v = (hidden_states @ Wv).reshape(B, T, H, DV)
            gk = (hidden_states @ Wgk1 @ Wgk2 + bgk2).reshape(B, T, H, DK)
            gk = jax.nn.log_sigmoid(gk) / GLN
            NC = T // CH
            NS = CH // SC

            def chunked(x):
                return x.reshape(B, NC, CH, H, x.shape[-1]).transpose(1, 0, 2, 3, 4)
            qc, kc, vc, gc = (chunked(q), chunked(k), chunked(v), chunked(gk))
            tril = jnp.tril(jnp.ones((SC, SC), bool))

            def step(S, inp):
                bq, bk, bv, bg = inp
                Bc = jnp.cumsum(bg, axis=1)
                Blast = Bc[:, -1]
                eBlast = jnp.exp(Blast)
                q_exp = bq * eBlast[:, None]
                k_exp = bk * jnp.exp(Blast[:, None] - Bc)
                S_new = eBlast[..., None] * S + jnp.einsum('bchd,bche->bhde', k_exp, bv)
                O_inter = jnp.einsum('bchd,bhde->bche', q_exp, S_new)
                sq = bq.reshape(B, NS, SC, H, DK)
                sk = bk.reshape(B, NS, SC, H, DK)
                sv = bv.reshape(B, NS, SC, H, DV)
                sb = Bc.reshape(B, NS, SC, H, DK)
                P = jnp.einsum('bjmhd,bjnhd->bjmnh', sq * jnp.exp(sb), sk * jnp.exp(-sb))
                P = jnp.where(tril[None, None, :, :, None], P, 0.0)
                colsum = P.sum(axis=2)
                intra = colsum[..., None] * sv
                return (S_new, O_inter + intra.reshape(B, CH, H, DV))
            S0 = jnp.zeros((B, H, DK, DV), hidden_states.dtype)
            _, O = jax.lax.scan(step, S0, (qc, kc, vc, gc))
            o = O.transpose(1, 0, 2, 3, 4).reshape(B, T, H, DV)
            g = (hidden_states @ Wg).reshape(B, T, H, DV)
            x = o + g
            mu = x.mean(-1, keepdims=True)
            var = jnp.mean((x - mu) ** 2, axis=-1, keepdims=True)
            x = (x - mu) * jax.lax.rsqrt(var + EPS) * ln_w + ln_b
            return jax.nn.silu(x).reshape(B, T, VD) @ Wo
        return _gla_forward(hidden_states, Wq, Wk, Wv, Wg, Wgk1, Wgk2, bgk2, Wo, ln_w, ln_b)

    def _L0_attn_b_ref(x, wq, wk, wv, wo):
        import jax, jax.numpy as jnp
        import numpy as np
        import math
        DIM = 256
        N_HEADS = 16
        N_KV_HEADS = 8
        HEAD_DIM = DIM // N_HEADS
        N_REP = N_HEADS // N_KV_HEADS
        BLOCK = 128
        TOPK = 8
        NEG_INF = -10000.0
        SEQ = 512
        BS = 1

        def _rope_tables(seq_len, head_dim, base=10000.0):
            inv_freq = 1.0 / base ** (jnp.arange(0, head_dim, 2, dtype=jnp.float32) / head_dim)
            ang = jnp.arange(seq_len, dtype=jnp.float32)[:, None] * inv_freq[None, :]
            return (jnp.cos(ang), jnp.sin(ang))

        def _apply_rope(t, cos, sin):
            t1 = t[..., 0::2]
            t2 = t[..., 1::2]
            c = cos[None, :, None, :]
            s = sin[None, :, None, :]
            out_even = t1 * c - t2 * s
            out_odd = t1 * s + t2 * c
            out = jnp.stack([out_even, out_odd], axis=-1)
            return out.reshape(t.shape)
        bs, S, _ = x.shape
        inv_sqrt_d = 1.0 / math.sqrt(HEAD_DIM)
        q = (x @ wq).reshape(bs, S, N_HEADS, HEAD_DIM)
        k = (x @ wk).reshape(bs, S, N_KV_HEADS, HEAD_DIM)
        v = (x @ wv).reshape(bs, S, N_KV_HEADS, HEAD_DIM)
        cos, sin = _rope_tables(S, HEAD_DIM)
        q = _apply_rope(q, cos, sin)
        k = _apply_rope(k, cos, sin)
        q = jnp.transpose(q, (0, 2, 1, 3))
        k = jnp.transpose(k, (0, 2, 1, 3))
        v = jnp.transpose(v, (0, 2, 1, 3))
        k_e = jnp.repeat(k, N_REP, axis=1)
        v_e = jnp.repeat(v, N_REP, axis=1)
        num_blocks = S // BLOCK
        k_blocks = k_e.reshape(bs, N_HEADS, num_blocks, BLOCK, HEAD_DIM)
        block_means = k_blocks.mean(axis=3)
        gating = jnp.einsum('bhsd,bhnd->bhsn', q, block_means) * inv_sqrt_d
        q_block_idx = jnp.arange(S) // BLOCK
        future_block = q_block_idx[:, None] < jnp.arange(num_blocks)[None, :]
        gating = jnp.where(future_block[None, None], NEG_INF, gating)
        curr_k = min(TOPK, num_blocks)
        _, sel_idx = jax.lax.top_k(gating, curr_k)
        selected = jnp.sum(jax.nn.one_hot(sel_idx, num_blocks, dtype=jnp.float32), axis=-2) > 0
        token_keep = jnp.repeat(selected, BLOCK, axis=-1)[..., :S]
        token_mask = jnp.where(token_keep, 0.0, NEG_INF)
        scores = jnp.einsum('bhsd,bhtd->bhst', q, k_e) * inv_sqrt_d
        causal = jnp.triu(jnp.ones((S, S), dtype=jnp.float32), k=1)
        final_mask = jnp.maximum(token_mask, causal[None, None] * NEG_INF)
        scores = scores + final_mask
        probs = jax.nn.softmax(scores.astype(jnp.float32), axis=-1).astype(scores.dtype)
        out = jnp.einsum('bhst,bhtd->bhsd', probs, v_e)
        out = jnp.transpose(out, (0, 2, 1, 3)).reshape(bs, S, N_HEADS * HEAD_DIM)
        return out @ wo

    def _L0_ffn_ref(x, w1, w2, w3):
        import jax, jax.numpy as jnp
        import numpy as np
        EPS = 1e-08

        def _quantize(w):
            gamma = jnp.mean(jnp.abs(w))
            return jnp.clip(jnp.round(w / (gamma + EPS)), -1.0, 1.0)

        def _bitlinear(x, w):
            return jnp.matmul(x, _quantize(w).T)
        x1 = _bitlinear(x, w1)
        x2 = _bitlinear(x, w2)
        hidden = jax.nn.sigmoid(x1) * x2
        return _bitlinear(hidden, w3)
    x = L0_attn_a_hidden_states
    x = x + _L0_attn_a_ref(_layernorm(x, axis=-1), L0_attn_a_Wq, L0_attn_a_Wk, L0_attn_a_Wv, L0_attn_a_Wg, L0_attn_a_Wgk1, L0_attn_a_Wgk2, L0_attn_a_bgk2, L0_attn_a_Wo, L0_attn_a_ln_w, L0_attn_a_ln_b)
    x = x + _L0_ffn_ref(_layernorm(x, axis=-1), L0_ffn_w1, L0_ffn_w2, L0_ffn_w3)
    x = x + _L0_attn_b_ref(_layernorm(x, axis=-1), L0_attn_b_wq, L0_attn_b_wk, L0_attn_b_wv, L0_attn_b_wo)
    x = x + _L0_ffn_ref(_layernorm(x, axis=-1), L0_ffn_w1, L0_ffn_w2, L0_ffn_w3)
    return x

_drawn_inputs = setup_inputs


def setup_inputs(seed=0):
    import zlib

    import numpy as np

    out = dict(_drawn_inputs(seed))
    spreads = {'L0_attn_a_bgk2': (0.0, 0.357), 'L0_attn_a_ln_w': (1.0, 0.2), 'L0_attn_a_ln_b': (0.0, 0.1)}
    factors = {'L0_attn_a_Wgk1': 8.0,
     'L0_attn_a_Wgk2': 8.0,
     'L0_attn_b_wq': 8.0,
     'L0_attn_b_wk': 8.0,
     'L0_attn_b_wv': 8.0,
     'L0_attn_b_wo': 8.0}
    for name, (base, spread) in spreads.items():
        noise = np.random.default_rng([zlib.crc32(name.encode()), seed]).standard_normal(out[name].shape)
        drawn = base * np.exp(spread * noise) if base else spread * noise
        out[name] = jnp.asarray(drawn.astype(out[name].dtype))
    for name, factor in factors.items():
        out[name] = (out[name] * factor).astype(out[name].dtype)
    return out
```

```python
from contextlib import ExitStack

import numpy as np

import concourse.bass as bass
from concourse import mybir

F32 = mybir.dt.float32
F16 = mybir.dt.float16
BF16 = mybir.dt.bfloat16
I32 = mybir.dt.int32
ALU = mybir.AluOpType
ACT = mybir.ActivationFunctionType
AX_X = mybir.AxisListType.X

P = 128
B, T, D = 4, 256, 256
KC = D // P
TT = T // P
NT = B * TT
NTOK = NT * P
HT = NTOK // 2
HTT = HT // P
LN_EPS = 1e-5

H, DK, DV = 8, 128, 32
KD, VD = H * DK, H * DV
CH, SC, LOW = 64, 16, 16
GATE = 1.0 / 16.0
ONE_ROW, UK = 32, 64
HH = H // 2

F = 704
FT = -(-F // P)
QEPS = 1e-8
XS, HS = 2048.0, 128.0

QH, VH, HD = 16, 8, 16
QK = (QH + VH) * HD
PARTS = 6
SK = PARTS * HD
VW = 3 * HD + 1
PSHIFT = 9.0

ORDER = [0, 2, 1, 3, 4, 6, 5, 7]


def build(nc, x, wq, wk, wv, wg, wgk1, wgk2, bgk2, wo, ln_w, ln_b, w1t, w2t, w3t,
          bwq, bwk, bwv, bwo, const_f, out):
    ctx = ExitStack()
    with ctx:
        def sb(name, shape, dt=F32):
            return ctx.enter_context(nc.sbuf_tensor(name, shape, dt))

        sems = {}

        def sem(name):
            sems[name] = ctx.enter_context(nc.semaphore(name))
            return sems[name]

        Wq = sb("Wq", [P, KC, KD])
        Wk = sb("Wk", [P, KC, KD])
        Wvg = sb("Wvg", [P, KC, 2 * VD])
        Wg1 = sb("Wg1", [P, KC, LOW])
        Wg2 = sb("Wg2", [UK, KD])
        Wo = sb("Wo", [P, KC, D])
        lnw = sb("lnw", [P, DV])
        lnb = sb("lnb", [P, DV])
        RAW = 2 * KC * F + FT * D
        region = sb("region", [P, (QH + VH) * NTOK // 2])
        raw1 = region[:, 0:KC * F].rearrange("p (k n) -> p k n", k=KC)
        raw2 = region[:, KC * F:2 * KC * F].rearrange("p (k n) -> p k n", k=KC)
        raw3 = region[:, 2 * KC * F:RAW].rearrange("p (k n) -> p k n", k=FT)
        qtmp = region[:, RAW:RAW + KC * F]
        junk = region[:, RAW + KC * F:RAW + 2 * KC * F]
        HID = FT * NTOK // 2
        hTh = region[:, 0:HID].bitcast(F16).rearrange("p (m t) -> p m t", m=FT)
        hTl = region[:, HID:2 * HID].bitcast(F16).rearrange("p (m t) -> p m t", m=FT)
        qkT = region[0:SK, :].bitcast(BF16).rearrange("p (h t) -> p h t", t=NTOK)
        W1 = sb("W1", [P, KC, F], F16)
        W2 = sb("W2", [P, KC, F], F16)
        W3 = sb("W3", [P, FT, D], F16)
        Wqkv = sb("Wqkv", [P, KC, QK + VH * HD])
        Wob = sb("Wob", [P, KC, D])
        cf = sb("cf", [P, 3 * P + 2 * TT * HD])
        ident = cf[:, 0:P]
        tril = cf[:, P:2 * P]
        submask = cf[:, 2 * P:3 * P]
        cosT = cf[:, 3 * P:3 * P + TT * HD].rearrange("p (t d) -> p t d", t=TT)
        sinT = cf[:, 3 * P + TT * HD:3 * P + 2 * TT * HD].rearrange("p (t d) -> p t d", t=TT)
        identb = sb("identb", [P, P], BF16)
        sel = sb("sel", [3 * QH, QH, P], BF16)[:, :, :]
        ones = sb("ones", [P, P])
        asum = sb("asum", [P, 4])
        thr = sb("thr", [P, 6])
        shift = sb("shift", [P, 1])
        eps = sb("eps", [P, 1])

        Xe, Xo = sb("Xe", [P, NT, D]), sb("Xo", [P, NT, D])
        X = [Xe, Xo, Xe, Xo, Xe]
        xn = sb("xn", [P, NT, D])
        xnT = sb("xnT", [P, KC, NTOK])
        xh = xnT[:, 0, :].bitcast(F16).rearrange("p (k t) -> p k t", k=KC)
        xl = xnT[:, 1, :].bitcast(F16).rearrange("p (k t) -> p k t", k=KC)
        st6 = sb("st6", [P, NT, 6])
        mv = sb("mv", [P, NT, 2])
        nv = sb("nv", [P, HTT])
        nh = sb("nh", [P, HTT], I32)
        ny = sb("ny", [P, HTT])
        na = sb("na", [P, HTT])
        uT = sb("uT", [UK, NTOK])
        scratch = sb("scratch", [P, 10, KD])
        absb, expb, gS = scratch[:, 0, :], scratch[:, 1, :], scratch[:, 2, :]

        def heads(j):
            return scratch[:, j, :].rearrange("p (h t) -> p h t", t=P)

        eN, eB, kk, qq, qS, kkT, pm = (heads(j) for j in range(3, 10))
        prob = scratch[:, 0:2, :].rearrange("p s (k h q) -> p s k h q", k=TT, h=2)
        prob_h = scratch[:, 2:4, :].rearrange("p a n -> p (a n)").bitcast(F16)[:, 0:3 * TT * 2 * T]
        prob_h = prob_h.rearrange("p (s k h q) -> p s k h q", s=3, k=TT, h=2)
        prob_l = scratch[:, 4:6, :].rearrange("p a n -> p (a n)").bitcast(F16)[:, 0:3 * TT * 2 * T]
        prob_l = prob_l.rearrange("p (s k h q) -> p s k h q", s=3, k=TT, h=2)
        sg = scratch[:, 6, :].rearrange("p (s t) -> p s t", s=2)
        hf = scratch[:, 7, :].rearrange("p (s t) -> p s t", s=2)
        qk = scratch[:, 8, 0:QK].rearrange("p (h d) -> p h d", d=HD)
        ra = scratch[:, 8, QK:2 * QK].rearrange("p (h d) -> p h d", d=HD)
        osum = scratch[:, 8, 2 * QK:2 * QK + D].rearrange("p (t h d) -> p t h d", t=TT, d=HD)
        oS = scratch[:, 9, 0:TT * D].rearrange("p (t n) -> p t n", t=TT)
        oT = scratch[:, 9, TT * D:2 * TT * D].rearrange("p (t k q) -> p t k q", t=TT, k=KC)
        eL = sb("eL", [P, H, 2])
        cs = sb("cs", [P, H])
        vgS = sb("vgS", [P, 2 * VD])
        vbd = sb("vbd", [P, H, 2, DV])
        y0 = sb("y0", [P, H, DV])
        y1 = sb("y1", [P, H, DV])
        S = [sb(f"S{b}", [P, H, DV]) for b in range(2)]
        su = sb("su", [P, H, DV])
        eS = sb("eS", [P, H, 2, DV])
        ya = sb("ya", [P, H, DV])
        yb = sb("yb", [P, H, DV])
        ysq = sb("ysq", [P, H, DV])
        yS = sb("yS", [P, H, DV])
        hm = sb("hm", [P, H])
        hv = sb("hv", [P, H])
        hl = sb("hl", [P, H])
        hy = sb("hy", [P, H])
        yT = sb("yT", [P, KC, P])
        rb = sb("rb", [P, QH + VH, HD])
        stk = sb("stk", [P, QH + VH, PARTS, HD], BF16)
        vf = sb("vf", [P, NT, VH, HD])
        vr = sb("vr", [P, VH, HD])
        v3 = sb("v3", [P, NT, VH, VW], BF16)
        nmx = sb("nmx", [P, NT, QH])
        nmr = sb("nmr", [P, TT, QH])
        nm3 = sb("nm3", [P, TT, 3, QH], BF16)
        mT = sb("mT", [3 * QH, B, T], BF16)
        rden = sb("rden", [P, TT, QH // 2])

        bank = ctx.enter_context(nc.psum_tensor("bank", [P, 8, 512], F32))

        w_gate = sem("w_gate")
        w_k = sem("w_k")
        w_q = sem("w_q")
        w_vg = sem("w_vg")
        w_gla = sem("w_gla")
        w_const = sem("w_const")
        identity_b = sem("identity_b")
        fills = sem("fills")
        w_ffn = sem("w_ffn")
        w_att = sem("w_att")
        padded = sem("padded")
        summed = sem("summed")
        totals = sem("totals")
        thresholds = sem("thresholds")
        ternary = sem("ternary")
        sel_step = sem("sel_step")
        stored = sem("stored")

        for n in ("x_in0 x_in1 x_in2 x_in3 x_in4 vec xnT_ps xnT_in u_ps u_in gk_ps abs_in expg_in lng_in g_in bt_ps en_in eb_in "
                  "eb_used kt_ps kk_in qt_ps q_in qq_in vg_ps vg_in tr_ps kkT_in p_ps cs_in vbd_in y1_in "
                  "u_state es_in o_ps o_used ycen_in ysq_in var_in lv_in root_in silu_step z_in ez_in ys_in ytr_ps yT_in wo_ps pool_step "
                  "qkv_ps qk_in v_in rope_a rope_b rope_used rot_in hi_in mid_in lo_in stk_in stk_ps qkT_in "
                  "row_ps max_in nm3_in mT_ps mT_in sc_ps prob_in ph_in pl_in vs_in pv_ps oS_in oT_ps oT_in bo_ps").split():
            sem(n)
        for s in (1, 2, 3, 4):
            for n in ("xn_in", "res_in"):
                sem(f"{n}{s}")
        for s in (2, 4):
            for n in ("xT_ps", "xh_in", "xl_in", "up_ps", "sig_in", "hid_in", "hh_in", "hl_in", "down_ps"):
                sem(f"{n}{s}")
        sem("xT3_ps")
        sem("xT3_in")

        def after(eng, name, value):
            eng.wait_ge(sems[name], value)

        def rsqrt(link, v, half, y, a):
            link(nc.vector.tensor_scalar(half, v.bitcast(I32), 1, None, ALU.logical_shift_right))
            link(nc.vector.tensor_scalar(y.bitcast(I32), half, -1.0, float(0x5F3759DF), ALU.mult, ALU.add))
            for _ in range(3):
                link(nc.vector.tensor_tensor(a, y, y, ALU.mult))
                link(nc.vector.scalar_tensor_tensor(out=a, in0=a, scalar=-0.5, in1=v, op0=ALU.mult, op1=ALU.mult))
                link(nc.vector.scalar_tensor_tensor(out=y, in0=a, scalar=1.5, in1=y, op0=ALU.add, op1=ALU.mult))

        x_v = x.rearrange("b (t p) d -> p (b t) d", p=P)
        out_v = out.rearrange("b (t p) d -> p (b t) d", p=P)
        FULL = (FT - 1) * P
        raw_parts = ((raw1, W1, P, 0, KC * F), (raw2, W2, P, 0, KC * F),
                     (raw3, W3, P, 0, (FT - 1) * D), (raw3, W3, F - FULL, (FT - 1) * D, FT * D))

        def rows_of(m):
            return min(P, F - m * P)

        TURN_BANK = {(2, 0): 0, (2, 1): 0, (4, 0): 4, (4, 1): 0}

        block = ctx.enter_context(nc.Block())

        @block.sync
        def _(sp):
            def chunks(w):
                return w.rearrange("(k p) n -> p k n", p=P)

            for t in range(HTT):
                sp.dma_start(X[0][:, t, :], x_v[:, t, :]).then_inc(sems[f"x_in{t}"], 16)
            sp.dma_start(cf[:, :], const_f).then_inc(w_const, 16)
            sp.dma_start(Wg1[:, :, :], chunks(wgk1)).then_inc(w_gate, 16)
            sp.wait_ge(padded, 1)
            sp.dma_start(Wg2[0:LOW, :], wgk2).then_inc(w_gate, 16)
            sp.dma_start(Wg2[ONE_ROW:ONE_ROW + 1, :], bgk2.rearrange("(a n) -> a n", a=1)).then_inc(w_gate, 16)
            sp.dma_start(X[0][:, HTT:, :], x_v[:, HTT:, :]).then_inc(sems[f"x_in{HTT}"], 16)
            sp.dma_start(Wk[:, :, :], chunks(wk)).then_inc(w_k, 16)
            sp.dma_start(Wq[:, :, :], chunks(wq)).then_inc(w_q, 16)
            sp.dma_start(Wvg[:, :, 0:VD], chunks(wv)).then_inc(w_vg, 16)
            sp.dma_start(Wvg[:, :, VD:], chunks(wg)).then_inc(w_vg, 16)
            sp.dma_start(Wo[:, :, :], chunks(wo)).then_inc(w_gla, 16)
            sp.dma_start(lnw[:, :], ln_w.partition_broadcast(P)).then_inc(w_gla, 16)
            sp.dma_start(lnb[:, :], ln_b.partition_broadcast(P)).then_inc(w_gla, 16)
            sp.dma_start(raw1, chunks(w1t)).then_inc(w_ffn, 16)
            sp.dma_start(raw2, chunks(w2t)).then_inc(w_ffn, 16)
            sp.dma_start(raw3[:, 0:FT - 1, :], chunks(w3t[0:FULL, :])).then_inc(w_ffn, 16)
            sp.dma_start(raw3[0:F - FULL, FT - 1, :], w3t[FULL:F, :]).then_inc(w_ffn, 16)
            for w, a, b in ((bwq, 0, QH * HD), (bwk, QH * HD, QK), (bwv, QK, QK + VH * HD)):
                sp.dma_start(Wqkv[:, :, a:b], chunks(w)).then_inc(w_att, 16)
            sp.dma_start(Wob[:, :, :], chunks(bwo)).then_inc(w_att, 16)
            for t in range(NT):
                after(sp, "res_in4", t + 1)
                sp.dma_start(out_v[:, t, :], X[4][:, t, :]).then_inc(stored, 16)
            sp.wait_ge(stored, 16 * NT)

        @block.tensor
        def _(pe):
            def turn(s, c, b0, name):
                for t in range(HTT):
                    after(pe, f"xn_in{s}", c * HTT + t + 1)
                    for k in range(KC):
                        last = nc.tensor.transpose(bank[:, b0 + k, t * P:(t + 1) * P],
                                                   xn[:, c * HTT + t, k * P:(k + 1) * P], ident)
                last.then_inc(sems[name], 1)

            def low_rank(c, b):
                after(pe, "xnT_in", KC * (c + 1))
                for k in range(KC):
                    last = nc.tensor.matmul(bank[0:LOW, b, :], Wg1[:, k, :], xnT[:, k, c * HT:(c + 1) * HT],
                                            start=(k == 0), stop=(k == KC - 1))
                last.then_inc(sems["u_ps"], 1)

            def gate(n):
                t = ORDER[n]
                after(pe, "u_in", n // HTT + 1)
                if n:
                    after(pe, "g_in", n)
                for j in range(2):
                    last = nc.tensor.matmul(bank[:, j, :], uT[:, t * P:(t + 1) * P], Wg2[:, j * 512:(j + 1) * 512],
                                            start=True, stop=True)
                last.then_inc(sems["gk_ps"], 1)

            def cumsum(n):
                after(pe, "g_in", n + 1)
                if n:
                    after(pe, "cs_in", n)
                for h in range(H):
                    last = nc.tensor.matmul(bank[:, 2 + h // HH, (h % HH) * P:(h % HH + 1) * P],
                                            gS[:, h * DK:(h + 1) * DK], tril, start=True, stop=True)
                last.then_inc(sems["bt_ps"], 1)

            def project(n, w, hb, done):
                t = ORDER[n]
                for h in range(hb * HH, hb * HH + HH):
                    for k in range(KC):
                        last = nc.tensor.matmul(bank[:, 4 + hb, (h % HH) * P:(h % HH + 1) * P],
                                                w[:, k, h * DK:(h + 1) * DK], xnT[:, k, t * P:(t + 1) * P],
                                                start=(k == 0), stop=(k == KC - 1))
                last.then_inc(sems[done], 1)

            def read_state(n):
                after(pe, "es_in", n + 1)
                if n:
                    after(pe, "res_in1", n)
                else:
                    pe.wait_ge(thresholds, 1)
                for h in range(H):
                    last = nc.tensor.matmul(bank[:, 7, h * 2 * DV:(h + 1) * 2 * DV], qS[:, h, :],
                                            eS[:, h, :, :].rearrange("p c e -> p (c e)"), start=True, stop=True)
                last.then_inc(sems["o_ps"], 1)

            def turn_y(n):
                after(pe, "ys_in", n + 1)
                yf = yS[:, :, :].rearrange("p h e -> p (h e)")
                for k in range(KC):
                    last = nc.tensor.transpose(bank[:, 7, k * P:(k + 1) * P], yf[:, k * P:(k + 1) * P], ident)
                last.then_inc(sems["ytr_ps"], 1)

            def project_y(n):
                after(pe, "yT_in", n + 1)
                for k in range(KC):
                    last = nc.tensor.matmul(bank[:, 7, 0:D], yT[:, k, :], Wo[:, k, :],
                                            start=(k == 0), stop=(k == KC - 1))
                last.then_inc(sems["wo_ps"], 1)

            pe.wait_ge(w_const, 16)
            turn(1, 0, 4, "xnT_ps")
            pe.wait_ge(w_gate, 48)
            pe.wait_ge(padded, 2)
            low_rank(0, 6)
            gate(0)
            turn(1, 1, 2, "xnT_ps")
            low_rank(1, 7)
            pe.wait_ge(w_k, 16)
            pe.wait_ge(w_q, 16)
            pe.wait_ge(w_vg, 32)
            pe.wait_ge(w_gla, 48)
            for n in range(NT):
                t = ORDER[n]
                if n + 1 < NT:
                    gate(n + 1)
                cumsum(n)
                if n == 1:
                    pe.wait_ge(summed, len(raw_parts))
                    after(pe, "u_in", 2)
                    nc.tensor.matmul(bank[:, 7, 0:4], ones[:, :], asum[:, :], start=True, stop=True).then_inc(totals, 1)
                if n >= 2:
                    turn_y(n - 2)
                if n:
                    after(pe, "kkT_in", 2 * n - 1)
                project(n, Wk, 0, "kt_ps")
                if n >= 2:
                    project_y(n - 2)
                if n:
                    after(pe, "kkT_in", 2 * n)
                project(n, Wk, 1, "kt_ps")
                if n:
                    after(pe, "es_in", n)
                for k in range(KC):
                    last = nc.tensor.matmul(bank[:, 6, :], xnT[:, k, t * P:(t + 1) * P], Wvg[:, k, :],
                                            start=(k == 0), stop=(k == KC - 1))
                last.then_inc(sems["vg_ps"], 1)
                if n:
                    read_state(n - 1)
                for hb in range(2):
                    after(pe, "kk_in", 2 * n + hb + 1)
                    project(n, Wq, hb, "qt_ps")
                for hb in range(2):
                    after(pe, "q_in", 2 * n + hb + 1)
                    for h in range(hb * HH, hb * HH + HH):
                        last = nc.tensor.transpose(bank[:, 4 + hb, (h % HH) * P:(h % HH + 1) * P], kk[:, h, :], ident)
                    last.then_inc(sems["tr_ps"], 1)
                after(pe, "qq_in", 2 * n + 2)
                after(pe, "eb_in", n + 1)
                for h in range(H):
                    last = nc.tensor.matmul(bank[:, 2 + h // HH, (h % HH) * P:(h % HH + 1) * P],
                                            kk[:, h, :], qq[:, h, :], start=True, stop=True)
                last.then_inc(sems["p_ps"], 1)
                after(pe, "vg_in", n + 1)
                after(pe, "vbd_in", n + 1)
                after(pe, "kkT_in", 2 * n + 2)
                for h in range(H):
                    last = nc.tensor.matmul(bank[:, 6, h * 2 * DV:(h + 1) * 2 * DV], kkT[:, h, :],
                                            vbd[:, h, :, :].rearrange("p c e -> p (c e)"), start=True, stop=True)
                last.then_inc(sems["u_state"], 1)

            def up(s, c, m):
                g = c * FT + m
                r = rows_of(m)
                after(pe, f"xl_in{s}", KC * (c + 1))
                if g >= 2:
                    after(pe, f"hid_in{s}", g - 1)
                for j, w in enumerate((W1, W2)):
                    for k in range(KC):
                        for part, xp in enumerate((xh, xl)):
                            last = nc.tensor.matmul(bank[0:r, 2 + 2 * (g % 2) + j, :],
                                                    w[:, k, m * P:m * P + r], xp[:, k, c * HT:(c + 1) * HT],
                                                    start=(k == 0 and part == 0), stop=(k == KC - 1 and part == 1))
                last.then_inc(sems[f"up_ps{s}"], 1)

            def down(s, t):
                after(pe, f"hl_in{s}", FT * (t // HTT + 1))
                if t >= 2:
                    after(pe, f"res_in{s}", t - 1)
                for m in range(FT):
                    r = rows_of(m)
                    for part, hp in enumerate((hTh, hTl)):
                        last = nc.tensor.matmul(bank[:, 6 + t % 2, 0:D], hp[0:r, m, t * P:(t + 1) * P],
                                                W3[0:r, m, :], start=(m == 0 and part == 0),
                                                stop=(m == FT - 1 and part == 1))
                last.then_inc(sems[f"down_ps{s}"], 1)

            def rest_of_ffn(s):
                turn(s, 1, TURN_BANK[s, 1], f"xT_ps{s}")
                for t in range(HTT):
                    down(s, t)
                for m in range(FT):
                    up(s, 1, m)
                for t in range(HTT, NT):
                    down(s, t)

            turn_y(NT - 2)
            turn(2, 0, TURN_BANK[2, 0], "xT_ps2")
            project_y(NT - 2)
            read_state(NT - 1)
            pe.wait_ge(ternary, len(raw_parts))
            up(2, 0, 0)
            up(2, 0, 1)
            turn_y(NT - 1)
            project_y(NT - 1)
            for m in range(2, FT):
                up(2, 0, m)
            rest_of_ffn(2)

            def qkv(t):
                after(pe, "xT3_in", KC * (t // HTT + 1))
                if t >= 2:
                    after(pe, "v_in", t - 1)
                for k in range(KC):
                    last = nc.tensor.matmul(bank[:, 2 + t % 2, :], xnT[:, k, t * P:(t + 1) * P], Wqkv[:, k, :],
                                            start=(k == 0), stop=(k == KC - 1))
                last.then_inc(sems["qkv_ps"], 1)

            def turn_stack(t):
                after(pe, "stk_in", t + 1)
                for j in range(3):
                    if t:
                        after(pe, "qkT_in", 3 * (t - 1) + j + 1)
                    pb = bank[0:SK, 4 + j, :].bitcast(BF16)
                    for h in range(8):
                        last = nc.tensor.transpose(
                            pb[:, h * P:(h + 1) * P],
                            stk[:, 8 * j + h, :, :].rearrange("p s d -> p (s d)"), identb[:, :])
                    last.then_inc(sems["stk_ps"], 1)

            turn(3, 0, 0, "xT3_ps")
            pe.wait_ge(w_att, 64)
            pe.wait_ge(identity_b, 1)
            qkv(0)
            for t in range(NT):
                if t == 1:
                    after(pe, "xT3_in", KC)
                    turn(3, 1, 0, "xT3_ps")
                if t + 1 < NT:
                    qkv(t + 1)
                turn_stack(t)

            def row_scores(a):
                b, qt, g = a // 16, a // 8 % 2, a % 8
                if a >= 2:
                    after(pe, "max_in", a - 1)
                k0 = b * T
                after(pe, "qkT_in", 3 * TT * (b + 1))
                for h2 in range(2):
                    last = nc.tensor.matmul(bank[:, a % 2, h2 * T:(h2 + 1) * T],
                                            qkT[:, 2 * g + h2, k0 + qt * P:k0 + (qt + 1) * P],
                                            qkT[:, QH + g, k0:k0 + T], start=True, stop=True)
                last.then_inc(sems["row_ps"], 1)

            def turn_max(b):
                after(pe, "nm3_in", b + 1)
                pb = bank[0:3 * QH, 0, :].bitcast(BF16)
                for qt in range(TT):
                    last = nc.tensor.transpose(pb[:, qt * P:(qt + 1) * P],
                                               nm3[:, qt, :, :].rearrange("p s h -> p (s h)"), identb[:, :])
                last.then_inc(sems["mT_ps"], 1)

            def scores(u):
                b, g = u // VH, u % VH
                after(pe, "mT_in", b + 1)
                if u >= 2:
                    after(pe, "prob_in", u - 1)
                k0 = b * T
                for kt in range(TT):
                    dst = bank[:, 2 + 2 * (u % 2) + kt, :].rearrange("p (h q) -> p h q", h=2)
                    nc.tensor.matmul(dst, qkT[:, QH + g, k0 + kt * P:k0 + (kt + 1) * P],
                                     qkT[:, 2 * g:2 * g + 2, k0:k0 + T], start=True, stop=False)
                    for h2 in range(2):
                        last = nc.tensor.matmul(dst[:, h2, :], sel[:, 2 * g + h2, :], mT[:, b, :],
                                                start=False, stop=(h2 == 1))
                last.then_inc(sems["sc_ps"], 1)

            def values(u):
                b, g = u // VH, u % VH
                after(pe, "pl_in", u + 1)
                after(pe, "vs_in", TT * (b + 1))
                if u >= VH // 2 and g % (VH // 2) == 0:
                    after(pe, "oS_in", u // (VH // 2))
                for h2 in range(2):
                    c = (2 * (g % (VH // 2)) + h2) * VW
                    for qt in range(TT):
                        for kt in range(TT):
                            for part, pr in enumerate((prob_h, prob_l)):
                                last = nc.tensor.matmul(bank[:, 6 + qt, c:c + VW],
                                                        pr[:, u % 3, kt, h2, qt * P:(qt + 1) * P],
                                                        v3[:, b * TT + kt, g, :], start=(kt == 0 and part == 0),
                                                        stop=(kt == TT - 1 and part == 1))
                last.then_inc(sems["pv_ps"], 1)

            def turn_o(b):
                after(pe, "oS_in", 2 * b + 2)
                after(pe, "max_in", min(NT * 8, 16 * (b + 2) + 8))
                for qt in range(TT):
                    for k in range(KC):
                        last = nc.tensor.transpose(bank[:, 0, (qt * KC + k) * P:(qt * KC + k + 1) * P],
                                                   oS[:, qt, k * P:(k + 1) * P], ident)
                last.then_inc(sems["oT_ps"], 1)

            def project_o(b):
                after(pe, "oT_in", b + 1)
                for qt in range(TT):
                    for k in range(KC):
                        last = nc.tensor.matmul(bank[:, 1, qt * D:(qt + 1) * D], oT[:, qt, k, :], Wob[:, k, :],
                                                start=(k == 0), stop=(k == KC - 1))
                last.then_inc(sems["bo_ps"], 1)

            for a in range(16):
                row_scores(a)
            turn_max(0)
            for u in range(B * VH):
                b, g = u // VH, u % VH
                scores(u)
                nxt = 16 * (b + 1) + 2 * g
                if b and g == 4:
                    project_o(b - 1)
                if b + 1 < B:
                    if b and g == 4:
                        after(pe, "oT_in", b)
                    row_scores(nxt)
                if u:
                    values(u - 1)
                if b + 1 < B:
                    if b and g == 4:
                        after(pe, "res_in3", TT * b)
                    row_scores(nxt + 1)
                if b and g == 3:
                    turn_o(b - 1)
                if g == VH - 1 and b + 1 < B:
                    turn_max(b + 1)
            values(B * VH - 1)
            turn(4, 0, TURN_BANK[4, 0], "xT_ps4")
            after(pe, "prob_in", B * VH)
            turn_o(B - 1)
            up(4, 0, 0)
            after(pe, "res_in3", TT * (B - 1))
            project_o(B - 1)
            for m in range(1, FT):
                up(4, 0, m)
            rest_of_ffn(4)

        @block.scalar
        def _(act):
            def turned(ps, done, c, b0):
                after(act, ps, c + 1)
                for k in range(KC):
                    nc.scalar.activation(xnT[:, k, c * HT:(c + 1) * HT], bank[:, b0 + k, :],
                                         ACT.Copy).then_inc(sems[done], 1)

            def turned_low(c, b):
                after(act, "u_ps", c + 1)
                nc.scalar.activation(uT[0:LOW, c * HT:(c + 1) * HT], bank[0:LOW, b, :], ACT.Copy).then_inc(sems["u_in"], 1)

            def magnitude(n):
                after(act, "gk_ps", n + 1)
                if n:
                    after(act, "g_in", n)
                nc.scalar.activation(absb, bank[:, 0:2, :].rearrange("p a n -> p (a n)"),
                                     ACT.Abs).then_inc(sems["abs_in"], 1)

            def decay(n):
                after(act, "abs_in", n + 1)
                nc.scalar.activation(expb, absb, ACT.Exp, scale=-1.0).then_inc(sems["expg_in"], 1)
                after(act, "expg_in", n + 1)
                nc.scalar.activation(absb, expb, ACT.Ln, bias=1.0).then_inc(sems["lng_in"], 1)

            def turned_y(n):
                after(act, "ytr_ps", n + 1)
                nc.scalar.activation(yT[:, :, :].rearrange("p k t -> p (k t)"), bank[:, 7, 0:D],
                                     ACT.Copy).then_inc(sems["yT_in"], 1)

            def square_y(n):
                after(act, "ycen_in", n + 1)
                nc.scalar.activation(ysq[:, :, :], yb[:, :, :], ACT.Square).then_inc(sems["ysq_in"], 1)

            def root_y(n):
                after(act, "var_in", n + 1)
                nc.scalar.activation(hl[:, :], hv[:, :], ACT.Ln, scale=1.0 / DV, bias=eps[:, :]).then_inc(sems["lv_in"], 1)
                after(act, "lv_in", n + 1)
                nc.scalar.activation(hy[:, :], hl[:, :], ACT.Exp, scale=-0.5).then_inc(sems["root_in"], 1)

            def gate_y(n):
                after(act, "z_in", n + 1)
                nc.scalar.activation(ysq[:, :, :], ya[:, :, :], ACT.Exp, scale=-1.0).then_inc(sems["silu_step"], 1)
                after(act, "silu_step", 2 * n + 1)
                nc.scalar.activation(ysq[:, :, :], ysq[:, :, :], ACT.Ln, bias=1.0).then_inc(sems["silu_step"], 1)
                after(act, "silu_step", 2 * n + 2)
                nc.scalar.activation(ysq[:, :, :], ysq[:, :, :], ACT.Exp, scale=-1.0).then_inc(sems["ez_in"], 1)

            act.preload_act_table_set("natural_log_exp_and_others")
            turned("xnT_ps", "xnT_in", 0, 4)
            act.wait_ge(padded, 3)
            turned_low(0, 6)
            magnitude(0)
            decay(0)
            turned("xnT_ps", "xnT_in", 1, 2)
            turned_low(1, 7)
            act.wait_ge(fills, 2)
            for n in range(NT):
                if n + 1 < NT:
                    magnitude(n + 1)
                after(act, "bt_ps", n + 1)
                if n:
                    after(act, "eb_used", n)
                cum = bank[:, 2:4, :].rearrange("p a (h t) -> p (a h) t", t=P)
                nc.scalar.activation(eN, cum, ACT.Exp, scale=-1.0).then_inc(sems["en_in"], 1)
                if n >= 2:
                    turned_y(n - 2)
                nc.scalar.activation(eB, cum, ACT.Exp).then_inc(sems["eb_in"], 1)
                if n + 1 < NT:
                    decay(n + 1)
                after(act, "vg_ps", n + 1)
                if n:
                    after(act, "y1_in", n)
                nc.scalar.activation(vgS[:, :], bank[:, 6, :], ACT.Copy).then_inc(sems["vg_in"], 1)
                if n:
                    square_y(n - 1)
                for hb in range(2):
                    after(act, "qt_ps", 2 * n + hb + 1)
                    nc.scalar.activation(qS[:, hb * HH:(hb + 1) * HH, :].rearrange("p h t -> p (h t)"),
                                         bank[:, 4 + hb, :], ACT.Copy).then_inc(sems["q_in"], 1)
                if n:
                    root_y(n - 1)
                for hb in range(2):
                    after(act, "tr_ps", 2 * n + hb + 1)
                    nc.scalar.activation(kkT[:, hb * HH:(hb + 1) * HH, :].rearrange("p h t -> p (h t)"),
                                         bank[:, 4 + hb, :], ACT.Copy).then_inc(sems["kkT_in"], 1)
                if n:
                    gate_y(n - 1)
                if n == 0:
                    act.wait_ge(w_ffn, 64)
                    for j, (raw, _w, rows, a, b) in enumerate(raw_parts):
                        if j:
                            act.wait_ge(summed, j)
                        nc.scalar.activation(junk[0:rows, 0:b - a], raw.rearrange("p k n -> p (k n)")[0:rows, a:b],
                                             ACT.Abs, accum_out=asum[0:rows, j:j + 1]).then_inc(summed, 1)

            def part_high(s, c):
                after(act, f"xT_ps{s}", c + 1)
                for k in range(KC):
                    nc.scalar.activation(xh[:, k, c * HT:(c + 1) * HT], bank[:, TURN_BANK[s, c] + k, :],
                                         ACT.Copy).then_inc(sems[f"xh_in{s}"], 1)

            def sigmoid(s, c, m):
                g, r = c * FT + m, rows_of(m)
                after(act, f"up_ps{s}", g + 1)
                if g >= 2:
                    after(act, f"hid_in{s}", g - 1)
                nc.scalar.activation(sg[0:r, g % 2, :], bank[0:r, 2 + 2 * (g % 2), :], ACT.Sigmoid,
                                     scale=1.0 / XS).then_inc(sems[f"sig_in{s}"], 1)

            def high(s, c, m):
                g, r = c * FT + m, rows_of(m)
                after(act, f"hid_in{s}", g + 1)
                nc.scalar.activation(hTh[0:r, m, c * HT:(c + 1) * HT], hf[0:r, g % 2, :],
                                     ACT.Copy).then_inc(sems[f"hh_in{s}"], 1)

            def rest_of_ffn(s, m0):
                for m in range(m0, FT):
                    sigmoid(s, 0, m)
                    high(s, 0, m - 1)
                high(s, 0, FT - 1)
                part_high(s, 1)
                for m in range(FT):
                    sigmoid(s, 1, m)
                    if m:
                        high(s, 1, m - 1)
                high(s, 1, FT - 1)

            turned_y(NT - 2)
            part_high(2, 0)
            square_y(NT - 1)
            root_y(NT - 1)
            gate_y(NT - 1)
            turned_y(NT - 1)
            sigmoid(2, 0, 0)
            rest_of_ffn(2, 1)

            turned("xT3_ps", "xT3_in", 0, 0)
            for t in range(NT):
                if t == 1:
                    turned("xT3_ps", "xT3_in", 1, 0)
                after(act, "qkv_ps", t + 1)
                if t:
                    after(act, "rope_used", t)
                    after(act, "rope_b", t)
                src = bank[:, 2 + t % 2, :]
                nc.scalar.activation(qk[:, :, :].rearrange("p h d -> p (h d)"), src[:, 0:QK],
                                     ACT.Copy).then_inc(sems["qk_in"], 1)
                nc.scalar.activation(vf[:, t, :, :], src[:, QK:].rearrange("p (h d) -> p h d", d=HD),
                                     ACT.Copy).then_inc(sems["v_in"], 1)
                after(act, "rot_in", t + 1)
                if t:
                    after(act, "stk_ps", 3 * t)
                nc.scalar.activation(stk[:, 0:QH, 0:3, :], ra[:, 0:QH, None, :].broadcast_to([P, QH, 3, HD]), ACT.Copy)
                nc.scalar.activation(stk[:, QH:, 0:4:3, :], ra[:, QH:, None, :].broadcast_to([P, VH, 2, HD]), ACT.Copy)
                nc.scalar.activation(stk[:, QH:, 5, :], ra[:, QH:, :], ACT.Copy).then_inc(sems["hi_in"], 1)
                after(act, "mid_in", t + 1)
                nc.scalar.activation(stk[:, 0:QH, 3:5, :], rb[:, 0:QH, None, :].broadcast_to([P, QH, 2, HD]), ACT.Copy)
                nc.scalar.activation(stk[:, QH:, 1:5:3, :], rb[:, QH:, None, :].broadcast_to([P, VH, 2, HD]),
                                     ACT.Copy).then_inc(sems["lo_in"], 1)
                after(act, "stk_ps", 3 * t + 1)
                nc.scalar.activation(qkT[:, 0:8, t * P:(t + 1) * P],
                                     bank[0:SK, 4, :].bitcast(BF16).rearrange("p (h q) -> p h q", q=P),
                                     ACT.Copy).then_inc(sems["qkT_in"], 1)

            def turned_o(b):
                after(act, "oT_ps", b + 1)
                nc.scalar.activation(oT[:, :, :, :].rearrange("p a k t -> p (a k t)"), bank[:, 0, :],
                                     ACT.Copy).then_inc(sems["oT_in"], 1)

            for u in range(B * VH):
                b, g = u // VH, u % VH
                after(act, "sc_ps", u + 1)
                if u >= 2:
                    after(act, "pl_in", u - 1)
                b0 = 2 + 2 * (u % 2)
                nc.scalar.activation(prob[:, u % 2, :, :, :].rearrange("p k h q -> p (k h q)"),
                                     bank[:, b0:b0 + 2, :].rearrange("p a n -> p (a n)"), ACT.Exp,
                                     bias=shift[:, :], scale=HD ** -0.5).then_inc(sems["prob_in"], 1)
                if u >= 3:
                    after(act, "pv_ps", u - 2)
                after(act, "prob_in", u + 1)
                nc.scalar.activation(prob_h[:, u % 3, :, :, :].rearrange("p k h q -> p (k h q)"),
                                     prob[:, u % 2, :, :, :].rearrange("p k h q -> p (k h q)"),
                                     ACT.Copy).then_inc(sems["ph_in"], 1)
                if b and g == 3:
                    turned_o(b - 1)
            part_high(4, 0)
            turned_o(B - 1)
            sigmoid(4, 0, 0)
            rest_of_ffn(4, 1)

        @block.vector
        def _(dve):
            links = [0]

            def link(ins):
                links[0] += 1
                ins.then_inc(sems["vec"], 1)
                after(dve, "vec", links[0])

            def layer_norm(s, c, scale=1.0):
                src = X[s - 1]
                tiles = range(c * HTT, (c + 1) * HTT)
                for t in tiles:
                    if s == 1:
                        after(dve, f"x_in{min(t, HTT)}", 16)
                    elif s == 2:
                        after(dve, "res_in1", ORDER.index(t) + 1)
                    else:
                        after(dve, f"res_in{s - 1}", t + 1)
                    last = nc.vector.bn_stats(st6[:, t, :], src[:, t, :])
                link(last)
                for t in tiles:
                    last = nc.vector.bn_aggr(mv[:, t, :], st6[:, t, :])
                link(last)
                link(nc.vector.tensor_scalar(nv[:, :], mv[:, c * HTT:(c + 1) * HTT, 1], LN_EPS, None, ALU.add))
                rsqrt(link, nv[:, :], nh[:, :], ny[:, :], na[:, :])
                if scale != 1.0:
                    link(nc.vector.tensor_scalar(ny[:, :], ny[:, :], scale, None, ALU.mult))
                for t in tiles:
                    nc.vector.tensor_scalar(xn[:, t, :], src[:, t, :], mv[:, t, 0:1], ny[:, t % HTT:t % HTT + 1],
                                            ALU.subtract, ALU.mult).then_inc(sems[f"xn_in{s}"], 1)

            def log_gate(n):
                after(dve, "lng_in", n + 1)
                if n:
                    after(dve, "bt_ps", n)
                nc.vector.scalar_tensor_tensor(out=gS, in0=bank[:, 0:2, :].rearrange("p a n -> p (a n)"),
                                               scalar=0.0, in1=absb, op0=ALU.min,
                                               op1=ALU.subtract).then_inc(sems["g_in"], 1)

            def residual_y(n):
                after(dve, "wo_ps", n + 1)
                t = ORDER[n]
                nc.vector.tensor_tensor(X[1][:, t, :], bank[:, 7, 0:D], X[0][:, t, :],
                                        ALU.add).then_inc(sems["res_in1"], 1)

            def head_bc(v):
                return v[:, :, None].broadcast_to([P, H, DV])

            def add_state(n):
                after(dve, "o_ps", n + 1)
                after(dve, "y1_in", n + 1)
                o = bank[:, 7, :].rearrange("p (h c e) -> p h c e", h=H, c=2)
                for c in range(2):
                    r = slice(c * CH, (c + 1) * CH)
                    last = nc.vector.tensor_tensor(ya[r, :, :], o[r, :, c, :], y1[r, :, :], ALU.add)
                last.then_inc(sems["o_used"], 1)
                after(dve, "o_used", n + 1)

            def centre_y(n):
                link(nc.vector.tensor_reduce(hm[:, :], ya[:, :, :], AX_X, ALU.add))
                nc.vector.scalar_tensor_tensor(out=yb[:, :, :], in0=head_bc(hm), scalar=-1.0 / DV, in1=ya[:, :, :],
                                               op0=ALU.mult, op1=ALU.add).then_inc(sems["ycen_in"], 1)

            def variance_y(n):
                after(dve, "ysq_in", n + 1)
                nc.vector.tensor_reduce(hv[:, :], ysq[:, :, :], AX_X, ALU.add).then_inc(sems["var_in"], 1)

            def scale_y(n):
                after(dve, "root_in", n + 1)
                link(nc.vector.tensor_tensor(yb[:, :, :], yb[:, :, :], head_bc(hy), ALU.mult))
                link(nc.vector.tensor_tensor(yb[:, :, :], yb[:, :, :],
                                             lnw[:, None, :].broadcast_to([P, H, DV]), ALU.mult))
                nc.vector.tensor_tensor(ya[:, :, :], yb[:, :, :],
                                        lnb[:, None, :].broadcast_to([P, H, DV]), ALU.add).then_inc(sems["z_in"], 1)

            def silu_y(n):
                after(dve, "ez_in", n + 1)
                nc.vector.tensor_tensor(yS[:, :, :], ya[:, :, :], ysq[:, :, :], ALU.mult).then_inc(sems["ys_in"], 1)
                after(dve, "ys_in", n + 1)

            def state(n):
                after(dve, "u_state", n + 1)
                if n:
                    after(dve, "o_ps", n)
                u = bank[:, 6, :].rearrange("p (h c e) -> p h c e", h=H, c=2)
                Sb = S[n % 2]
                for c in range(2):
                    el = head_bc(eL[:, :, c])
                    if n % 4 < 2 and c == 0:
                        link(nc.vector.tensor_tensor(Sb[:, :, :], u[:, :, c, :], el, ALU.mult))
                    else:
                        link(nc.vector.tensor_tensor(su[:, :, :], u[:, :, c, :], Sb[:, :, :], ALU.add))
                        link(nc.vector.tensor_tensor(Sb[:, :, :], su[:, :, :], el, ALU.mult))
                    last = nc.vector.tensor_tensor(eS[:, :, c, :], Sb[:, :, :], el, ALU.mult)
                last.then_inc(sems["es_in"], 1)
                after(dve, "es_in", n + 1)

            def thresholds_of_weights():
                dve.wait_ge(totals, 1)
                for k in range(6):
                    s = -0.5 if k > 2 else 0.5
                    last = nc.vector.tensor_scalar(thr[:, k:k + 1], bank[:, 7, k % 3:k % 3 + 1], s / (F * D), s * QEPS,
                                                   ALU.mult, ALU.add)
                link(last)
                for k in (2, 5):
                    s = -0.5 if k > 2 else 0.5
                    last = nc.vector.scalar_tensor_tensor(
                        out=thr[:, k:k + 1], in0=bank[:, 7, 3:4], scalar=s / (F * D),
                        in1=thr[:, k:k + 1], op0=ALU.mult, op1=ALU.add)
                last.then_inc(thresholds, 1)
                dve.wait_ge(thresholds, 1)

            def quantise(j):
                raw, w, rows, a, b = raw_parts[j]
                k = min(j, 2)
                r = raw.rearrange("p k n -> p (k n)")[0:rows, a:b]
                q = w[:, :, :].rearrange("p k n -> p (k n)")[0:rows, a:b]
                below = qtmp[0:rows, 0:b - a]
                link(nc.vector.tensor_scalar(below, r, thr[0:rows, 3 + k:4 + k], None, ALU.is_lt))
                nc.vector.scalar_tensor_tensor(out=q, in0=r, scalar=thr[0:rows, k:k + 1], in1=below,
                                               op0=ALU.is_gt, op1=ALU.subtract).then_inc(ternary, 1)
                dve.wait_ge(ternary, j + 1)

            layer_norm(1, 0)
            layer_norm(1, 1)
            dve.wait_ge(w_const, 16)
            nc.vector.tensor_copy(identb[:, :], ident).then_inc(identity_b, 1)
            nc.vector.memset(shift[:, :], PSHIFT).then_inc(fills, 1)
            nc.vector.memset(eps[:, :], LN_EPS).then_inc(fills, 1)
            log_gate(0)
            dve.wait_ge(w_gla, 48)
            for n in range(NT):
                after(dve, "en_in", n + 1)
                if n:
                    after(dve, "p_ps", n)
                for hb in range(2):
                    after(dve, "kt_ps", 2 * n + hb + 1)
                    r = slice(hb * HH, (hb + 1) * HH)
                    nc.vector.tensor_tensor(kk[:, r, :], bank[:, 4 + hb, :].rearrange("p (h t) -> p h t", t=P),
                                            eN[:, r, :], ALU.mult).then_inc(sems["kk_in"], 1)
                    if n >= 2 and hb == 0:
                        residual_y(n - 2)
                if n == 1:
                    thresholds_of_weights()
                if n + 1 < NT:
                    log_gate(n + 1)
                if n:
                    add_state(n - 1)
                    centre_y(n - 1)
                after(dve, "eb_in", n + 1)
                for hb in range(2):
                    after(dve, "q_in", 2 * n + hb + 1)
                    r = slice(hb * HH, (hb + 1) * HH)
                    nc.vector.tensor_tensor(qq[:, r, :], qS[:, r, :], eB[:, r, :], ALU.mult).then_inc(sems["qq_in"], 1)
                    if n and hb == 0:
                        variance_y(n - 1)
                nc.vector.tensor_copy(eL[:, :, :], eB[:, :, CH - 1:P:CH]).then_inc(sems["eb_used"], 1)
                after(dve, "eb_used", n + 1)
                if n:
                    scale_y(n - 1)
                after(dve, "p_ps", n + 1)
                link(nc.vector.tensor_tensor(pm, bank[:, 2:4, :].rearrange("p a (h t) -> p (a h) t", t=P),
                                             submask[:, None, :].broadcast_to([P, H, P]), ALU.mult))
                if n:
                    after(dve, "y1_in", n)
                nc.vector.tensor_reduce(cs[:, :], pm, AX_X, ALU.add).then_inc(sems["cs_in"], 1)
                after(dve, "cs_in", n + 1)
                if n:
                    silu_y(n - 1)
                state(n)
                if 1 <= n <= len(raw_parts):
                    quantise(n - 1)
                if n == NT - 2:
                    layer_norm(2, 0, XS)

            def part_low(s, c):
                for k in range(KC):
                    after(dve, f"xh_in{s}", KC * c + k + 1)
                    tok = slice(c * HT, (c + 1) * HT)
                    nc.vector.tensor_tensor(xl[:, k, tok], bank[:, TURN_BANK[s, c] + k, :], xh[:, k, tok],
                                            ALU.subtract).then_inc(sems[f"xl_in{s}"], 1)

            def hidden(s, c, m):
                g, r = c * FT + m, rows_of(m)
                after(dve, f"sig_in{s}", g + 1)
                if g >= 2:
                    after(dve, f"hl_in{s}", g - 1)
                nc.vector.scalar_tensor_tensor(
                    out=hf[0:r, g % 2, :], in0=bank[0:r, 3 + 2 * (g % 2), :], scalar=HS / XS,
                    in1=sg[0:r, g % 2, :], op0=ALU.mult, op1=ALU.mult).then_inc(sems[f"hid_in{s}"], 1)

            def low(s, c, m):
                g, r = c * FT + m, rows_of(m)
                after(dve, f"hh_in{s}", g + 1)
                tok = slice(c * HT, (c + 1) * HT)
                nc.vector.tensor_tensor(hTl[0:r, m, tok], hf[0:r, g % 2, :], hTh[0:r, m, tok],
                                        ALU.subtract).then_inc(sems[f"hl_in{s}"], 1)

            def residual(s, t):
                after(dve, f"down_ps{s}", t + 1)
                nc.vector.scalar_tensor_tensor(
                    out=X[s][:, t, :], in0=bank[:, 6 + t % 2, 0:D], scalar=1.0 / HS,
                    in1=X[s - 1][:, t, :], op0=ALU.mult, op1=ALU.add).then_inc(sems[f"res_in{s}"], 1)

            def rest_of_ffn(s):
                for m in range(FT):
                    hidden(s, 0, m)
                    if m:
                        low(s, 0, m - 1)
                    if m == 2:
                        layer_norm(s, 1, XS)
                low(s, 0, FT - 1)
                part_low(s, 1)
                for t in range(HTT):
                    residual(s, t)
                for m in range(FT):
                    hidden(s, 1, m)
                    if m:
                        low(s, 1, m - 1)
                    if m == 2 and s == 2:
                        layer_norm(3, 0)
                low(s, 1, FT - 1)
                for t in range(HTT, NT):
                    residual(s, t)

            residual_y(NT - 2)
            part_low(2, 0)
            add_state(NT - 1)
            centre_y(NT - 1)
            variance_y(NT - 1)
            scale_y(NT - 1)
            silu_y(NT - 1)
            residual_y(NT - 1)
            rest_of_ffn(2)
            layer_norm(3, 1)

            for t in range(NT):
                after(dve, "qk_in", t + 1)
                if t:
                    after(dve, "stk_in", t)
                nc.vector.tensor_tensor(ra[:, :, :], qk[:, :, :],
                                        cosT[:, t % TT, None, :].broadcast_to([P, QH + VH, HD]),
                                        ALU.mult).then_inc(sems["rope_used"], 1)
                after(dve, "rope_used", t + 1)
                after(dve, "rope_b", t + 1)
                nc.vector.tensor_tensor(ra[:, :, :], ra[:, :, :], rb[:, :, :], ALU.add).then_inc(sems["rot_in"], 1)
                after(dve, "v_in", t + 1)
                if t == 0:
                    dve.wait_ge(padded, 3)
                vt = vf[:, t, :, :]
                link(nc.vector.tensor_copy(v3[:, t, :, 0:HD], vt))
                link(nc.vector.tensor_tensor(vr[:, :, :], vt, v3[:, t, :, 0:HD], ALU.subtract))
                link(nc.vector.tensor_copy(v3[:, t, :, HD:2 * HD], vr[:, :, :]))
                nc.vector.tensor_tensor(v3[:, t, :, 2 * HD:3 * HD], vr[:, :, :], v3[:, t, :, HD:2 * HD],
                                        ALU.subtract).then_inc(sems["vs_in"], 1)
                after(dve, "vs_in", t + 1)
                after(dve, "hi_in", t + 1)
                nc.vector.tensor_tensor(rb[:, 0:QH, :], ra[:, 0:QH, :], stk[:, 0:QH, 0, :], ALU.subtract)
                nc.vector.tensor_tensor(rb[:, QH:, :], ra[:, QH:, :], stk[:, QH:, 0, :],
                                        ALU.subtract).then_inc(sems["mid_in"], 1)
                after(dve, "mid_in", t + 1)
                after(dve, "lo_in", t + 1)
                nc.vector.tensor_tensor(stk[:, 0:QH, 5, :], rb[:, 0:QH, :], stk[:, 0:QH, 3, :], ALU.subtract)
                nc.vector.tensor_tensor(stk[:, QH:, 2, :], rb[:, QH:, :], stk[:, QH:, 1, :],
                                        ALU.subtract).then_inc(sems["stk_in"], 1)
                for j in (1, 2):
                    after(dve, "stk_ps", 3 * t + j + 1)
                    after(dve, "qkT_in", 3 * t + j)
                    nc.vector.tensor_copy(qkT[:, 8 * j:8 * j + 8, t * P:(t + 1) * P],
                                          bank[0:SK, 4 + j, :].bitcast(BF16).rearrange("p (h q) -> p h q", q=P)
                                          ).then_inc(sems["qkT_in"], 1)

            def row_max(a):
                g = a % 8
                after(dve, "row_ps", a + 1)
                nc.vector.tensor_reduce(nmx[:, a // 8, 2 * g:2 * g + 2],
                                        bank[:, a % 2, :].rearrange("p (h k) -> p h k", h=2), AX_X, ALU.max,
                                        negate=True).then_inc(sems["max_in"], 1)

            def split_max(b):
                after(dve, "max_in", 16 * (b + 1))
                src = nmx[:, b * TT:(b + 1) * TT, :]
                if b:
                    after(dve, "mT_ps", b)
                link(nc.vector.tensor_copy(nm3[:, :, 0, :], src))
                link(nc.vector.tensor_tensor(nmr[:, :, :], src, nm3[:, :, 0, :], ALU.subtract))
                link(nc.vector.tensor_copy(nm3[:, :, 1, :], nmr[:, :, :]))
                nc.vector.tensor_tensor(nm3[:, :, 2, :], nmr[:, :, :], nm3[:, :, 1, :],
                                        ALU.subtract).then_inc(sems["nm3_in"], 1)

            def turned_max(b):
                after(dve, "mT_ps", b + 1)
                nc.vector.tensor_copy(mT[:, b, :], bank[0:3 * QH, 0, :].bitcast(BF16)[:, 0:T]).then_inc(sems["mT_in"], 1)

            def normalise(w):
                b, hw = w // 2, w % 2
                after(dve, "pv_ps", VH // 2 * (w + 1))
                if b and hw == 0:
                    after(dve, "oT_ps", b)
                ov = bank[:, 6:8, 0:QH // 2 * VW].rearrange("p a (h e) -> p a h e", e=VW)
                nc.vector.reciprocal(rden[:, :, :], ov[:, :, :, VW - 1])
                for qt in range(TT):
                    last = nc.vector.tensor_reduce(
                        osum[:, qt, :, :], ov[:, qt, :, 0:3 * HD].rearrange("p h (s e) -> p h e s", s=3), AX_X, ALU.add)
                link(last)
                for qt in range(TT):
                    last = nc.vector.tensor_tensor(
                        oS[:, qt, hw * D // 2:(hw + 1) * D // 2].rearrange("p (h e) -> p h e", e=HD),
                        osum[:, qt, :, :], rden[:, qt, :, None].broadcast_to([P, QH // 2, HD]), ALU.mult)
                last.then_inc(sems["oS_in"], 1)
                after(dve, "oS_in", w + 1)

            def prob_low(u):
                after(dve, "ph_in", u + 1)
                nc.vector.tensor_tensor(prob_l[:, u % 3, :, :, :].rearrange("p k h q -> p (k h q)"),
                                        prob[:, u % 2, :, :, :].rearrange("p k h q -> p (k h q)"),
                                        prob_h[:, u % 3, :, :, :].rearrange("p k h q -> p (k h q)"),
                                        ALU.subtract).then_inc(sems["pl_in"], 1)

            def residual_o(b):
                after(dve, "bo_ps", b + 1)
                for qt in range(TT):
                    t = b * TT + qt
                    nc.vector.tensor_tensor(X[3][:, t, :], bank[:, 1, qt * D:(qt + 1) * D], X[2][:, t, :],
                                            ALU.add).then_inc(sems["res_in3"], 1)

            for a in range(16):
                row_max(a)
            split_max(0)
            turned_max(0)
            for u in range(B * VH):
                b, g = u // VH, u % VH
                nxt = 16 * (b + 1) + 2 * g
                if u and u % 4 == 0:
                    normalise(u // 4 - 1)
                if b and g == 4:
                    residual_o(b - 1)
                if b + 1 < B:
                    row_max(nxt)
                prob_low(u)
                if b + 1 < B:
                    row_max(nxt + 1)
                if g == VH - 1 and b + 1 < B:
                    split_max(b + 1)
                    turned_max(b + 1)
                if u == B * VH - 4:
                    layer_norm(4, 0, XS)
            normalise(2 * B - 1)
            part_low(4, 0)
            residual_o(B - 1)
            rest_of_ffn(4)

        @block.gpsimd
        def _(gp):
            nc.gpsimd.memset(Wg2[:, :], 0.0).then_inc(padded, 1)
            nc.gpsimd.memset(uT[:, :], 0.0)
            nc.gpsimd.memset(asum[:, :], 0.0)
            nc.gpsimd.memset(ones[:, :], 1.0)
            nc.gpsimd.memset(vbd[:, :, :, :], 0.0).then_inc(padded, 1)
            gp.wait_ge(padded, 2)
            nc.gpsimd.memset(uT[ONE_ROW:ONE_ROW + 1, :], 1.0).then_inc(padded, 1)
            gp.wait_ge(padded, 3)

            for n in range(NT):
                after(gp, "vg_in", n + 1)
                if n:
                    after(gp, "u_state", n)
                v = vgS[:, 0:VD].rearrange("p (h e) -> p h e", h=H)
                g = vgS[:, VD:].rearrange("p (h e) -> p h e", h=H)
                for c in range(2):
                    r = slice(c * CH, (c + 1) * CH)
                    last = nc.gpsimd.tensor_copy(vbd[r, :, c, :], v[r, :, :])
                last.then_inc(sems["vbd_in"], 1)
                after(gp, "vbd_in", n + 1)
                after(gp, "cs_in", n + 1)
                if n:
                    after(gp, "y1_in", n)
                nc.gpsimd.tensor_tensor(y0[:, :, :], v, cs[:, :, None].broadcast_to([P, H, DV]),
                                        ALU.mult).then_inc(sems["pool_step"], 1)
                after(gp, "pool_step", n + 1)
                if n:
                    after(gp, "o_used", n)
                nc.gpsimd.tensor_tensor(y1[:, :, :], y0[:, :, :], g, ALU.add).then_inc(sems["y1_in"], 1)
                if n == 0:
                    after(gp, "y1_in", 1)
                    nc.gpsimd.memset(v3[:, :, :, :], 1.0)
                    nc.gpsimd.memset(sel, 0.0).then_inc(sel_step, 1)
                    gp.wait_ge(sel_step, 1)
                    for part in range(3):
                        nc.gpsimd.affine_select(out=sel, in_=sel, compare_op=ALU.not_equal, fill=1.0,
                                                base=-part * QH, pattern=[[-1, QH], [0, P]],
                                                channel_multiplier=1).then_inc(sel_step, 1)
                        gp.wait_ge(sel_step, part + 2)
            gp.wait_ge(w_const, 16)
            for t in range(NT):
                after(gp, "qk_in", t + 1)
                if t:
                    after(gp, "stk_in", t)
                for e in range(2):
                    last = nc.gpsimd.tensor_tensor(
                        rb[:, :, e:HD:2], qk[:, :, 1 - e:HD:2],
                        sinT[:, t % TT, None, e:HD:2].broadcast_to([P, QH + VH, HD // 2]), ALU.mult)
                last.then_inc(sems["rope_b"], 1)


def constants():
    r, c = np.arange(P)[:, None], np.arange(P)[None, :]
    tril = ((c >= r) & (c // CH == r // CH)).astype(np.float32) * np.float32(GATE)
    sub = ((c >= r) & (c // SC == r // SC)).astype(np.float32)
    inv = (1.0 / np.float32(10000.0) ** (np.arange(0, HD, 2, dtype=np.float32) / np.float32(HD))).astype(np.float32)
    ang = np.arange(T, dtype=np.float32)[:, None] * inv[None, :]
    cos = np.repeat(np.cos(ang), 2, axis=1).reshape(TT, P, HD).transpose(1, 0, 2).reshape(P, TT * HD)
    sin = np.stack([-np.sin(ang), np.sin(ang)], -1).reshape(TT, P, HD).transpose(1, 0, 2).reshape(P, TT * HD)
    eye = np.eye(P, dtype=np.float32)
    cf = np.concatenate([eye, tril, sub, cos, sin], axis=1).astype(np.float32)
    return cf


def kernel(**inputs):
    import numpy as _np
    import concourse.bacc as _bacc
    from concourse import mybir as _mybir
    from concourse.bass_utils import run_bass_kernel_spmd as _run

    nc = _bacc.Bacc("TRN2", target_bir_lowering=False, num_devices=1)
    a = {k: _np.ascontiguousarray(v) for k, v in inputs.items()}
    cf = constants()
    p, q, f = "L0_attn_a_", "L0_attn_b_", "L0_ffn_"
    arrays = {
        "x": a[p + "hidden_states"], "wq": a[p + "Wq"], "wk": a[p + "Wk"], "wv": a[p + "Wv"], "wg": a[p + "Wg"],
        "wgk1": a[p + "Wgk1"], "wgk2": a[p + "Wgk2"], "bgk2": a[p + "bgk2"], "wo": a[p + "Wo"],
        "ln_w": a[p + "ln_w"], "ln_b": a[p + "ln_b"],
        "w1t": _np.ascontiguousarray(a[f + "w1"].T), "w2t": _np.ascontiguousarray(a[f + "w2"].T),
        "w3t": _np.ascontiguousarray(a[f + "w3"].T),
        "bwq": a[q + "wq"], "bwk": a[q + "wk"], "bwv": a[q + "wv"], "bwo": a[q + "wo"],
        "const_f": cf,
    }
    args = [nc.dram_tensor(f"in_{n}", v.shape, _mybir.dt.from_np(v.dtype), kind="ExternalInput").ap()
            for n, v in arrays.items()]
    y = nc.dram_tensor("out_0", a[p + "hidden_states"].shape, _mybir.dt.float32, kind="ExternalOutput").ap()
    build(nc, *args, y)
    r = _run(nc, [{f"in_{n}": v for n, v in arrays.items()}], core_ids=[0])
    return r.results[0]["out_0"]
```

```python
from contextlib import ExitStack

import numpy as np

import concourse.bass as bass
from concourse import mybir

F32 = mybir.dt.float32
F16 = mybir.dt.float16
BF16 = mybir.dt.bfloat16
I32 = mybir.dt.int32
ALU = mybir.AluOpType
ACT = mybir.ActivationFunctionType
AX_X = mybir.AxisListType.X

P = 128
B, T, D = 4, 256, 256
KC = D // P
TT = T // P
NT = B * TT
NTOK = NT * P
HT = NTOK // 2
HTT = HT // P
LN_EPS = 1e-5

H, DK, DV = 8, 128, 32
KD, VD = H * DK, H * DV
CH, SC, LOW = 64, 16, 16
GATE = 1.0 / 16.0
ONE_ROW, UK = 32, 64
HH = H // 2

F = 704
FT = -(-F // P)
QEPS = 1e-8
XS, HS = 2048.0, 128.0

QH, VH, HD = 16, 8, 16
QK = (QH + VH) * HD
PARTS = 6
SK = PARTS * HD
VW = 3 * HD + 1
PSHIFT = 9.0

ORDER = [0, 2, 1, 3, 4, 6, 5, 7]


def build(nc, x, wq, wk, wv, wg, wgk1, wgk2, bgk2, wo, ln_w, ln_b, w1t, w2t, w3t,
          bwq, bwk, bwv, bwo, const_f, out):
    ctx = ExitStack()
    with ctx:
        def sb(name, shape, dt=F32):
            return ctx.enter_context(nc.sbuf_tensor(name, shape, dt))

        sems = {}

        def sem(name):
            sems[name] = ctx.enter_context(nc.semaphore(name))
            return sems[name]

        Wq = sb("Wq", [P, KC, KD])
        Wk = sb("Wk", [P, KC, KD])
        Wvg = sb("Wvg", [P, KC, 2 * VD])
        Wg1 = sb("Wg1", [P, KC, LOW])
        Wg2 = sb("Wg2", [UK, KD])
        Wo = sb("Wo", [P, KC, D])
        lnw = sb("lnw", [P, DV])
        lnb = sb("lnb", [P, DV])
        RAW = 2 * KC * F + FT * D
        region = sb("region", [P, (QH + VH) * NTOK // 2])
        raw1 = region[:, 0:KC * F].rearrange("p (k n) -> p k n", k=KC)
        raw2 = region[:, KC * F:2 * KC * F].rearrange("p (k n) -> p k n", k=KC)
        raw3 = region[:, 2 * KC * F:RAW].rearrange("p (k n) -> p k n", k=FT)
        qtmp = region[:, RAW:RAW + KC * F]
        junk = region[:, RAW + KC * F:RAW + 2 * KC * F]
        HID = FT * NTOK // 2
        hTh = region[:, 0:HID].bitcast(F16).rearrange("p (m t) -> p m t", m=FT)
        hTl = region[:, HID:2 * HID].bitcast(F16).rearrange("p (m t) -> p m t", m=FT)
        qkT = region[0:SK, :].bitcast(BF16).rearrange("p (h t) -> p h t", t=NTOK)
        W1 = sb("W1", [P, KC, F], F16)
        W2 = sb("W2", [P, KC, F], F16)
        W3 = sb("W3", [P, FT, D], F16)
        Wqkv = sb("Wqkv", [P, KC, QK + VH * HD])
        Wob = sb("Wob", [P, KC, D])
        cf = sb("cf", [P, 3 * P + 2 * TT * HD])
        ident = cf[:, 0:P]
        tril = cf[:, P:2 * P]
        submask = cf[:, 2 * P:3 * P]
        cosT = cf[:, 3 * P:3 * P + TT * HD].rearrange("p (t d) -> p t d", t=TT)
        sinT = cf[:, 3 * P + TT * HD:3 * P + 2 * TT * HD].rearrange("p (t d) -> p t d", t=TT)
        identb = sb("identb", [P, P], BF16)
        sel = sb("sel", [3 * QH, QH, P], BF16)[:, :, :]
        ones = sb("ones", [P, P])
        asum = sb("asum", [P, 4])
        thr = sb("thr", [P, 6])
        shift = sb("shift", [P, 1])
        eps = sb("eps", [P, 1])

        Xe, Xo = sb("Xe", [P, NT, D]), sb("Xo", [P, NT, D])
        X = [Xe, Xo, Xe, Xo, Xe]
        xn = sb("xn", [P, NT, D])
        xnT = sb("xnT", [P, KC, NTOK])
        xh = xnT[:, 0, :].bitcast(F16).rearrange("p (k t) -> p k t", k=KC)
        xl = xnT[:, 1, :].bitcast(F16).rearrange("p (k t) -> p k t", k=KC)
        st6 = sb("st6", [P, NT, 6])
        mv = sb("mv", [P, NT, 2])
        nv = sb("nv", [P, HTT])
        nh = sb("nh", [P, HTT], I32)
        ny = sb("ny", [P, HTT])
        na = sb("na", [P, HTT])
        uT = sb("uT", [UK, NTOK])
        scratch = sb("scratch", [P, 10, KD])
        absb, expb, gS = scratch[:, 0, :], scratch[:, 1, :], scratch[:, 2, :]

        def heads(j):
            return scratch[:, j, :].rearrange("p (h t) -> p h t", t=P)

        eN, eB, kk, qq, qS, kkT, pm = (heads(j) for j in range(3, 10))
        prob = scratch[:, 0:2, :].rearrange("p s (k h q) -> p s k h q", k=TT, h=2)
        prob_h = scratch[:, 2:4, :].rearrange("p a n -> p (a n)").bitcast(F16)[:, 0:3 * TT * 2 * T]
        prob_h = prob_h.rearrange("p (s k h q) -> p s k h q", s=3, k=TT, h=2)
        prob_l = scratch[:, 4:6, :].rearrange("p a n -> p (a n)").bitcast(F16)[:, 0:3 * TT * 2 * T]
        prob_l = prob_l.rearrange("p (s k h q) -> p s k h q", s=3, k=TT, h=2)
        sg = scratch[:, 6, :].rearrange("p (s t) -> p s t", s=2)
        hf = scratch[:, 3, :].rearrange("p (s t) -> p s t", s=2)
        stk = scratch[:, 0:3, :].rearrange("p a n -> p (a n)").bitcast(BF16)[:, 0:2 * PARTS * QK]
        stk = stk.rearrange("p (a h s d) -> p a h s d", a=2, s=PARTS, d=HD)
        qk, ra, rb = (scratch[:, j, 0:2 * QK].rearrange("p (a h d) -> p a h d", a=2, d=HD) for j in (3, 4, 5))
        osum = scratch[:, 8, 0:D].rearrange("p (t h d) -> p t h d", t=TT, d=HD)
        oS = scratch[:, 9, 0:TT * D].rearrange("p (t n) -> p t n", t=TT)
        oT = scratch[:, 9, TT * D:2 * TT * D].rearrange("p (t k q) -> p t k q", t=TT, k=KC)
        eL = sb("eL", [P, H, 2])
        cs = sb("cs", [P, H])
        vgS = sb("vgS", [P, 2 * VD])
        vbd = sb("vbd", [P, H, 2, DV])
        y0 = sb("y0", [P, H, DV])
        y1 = sb("y1", [P, H, DV])
        S = [sb(f"S{b}", [P, H, DV]) for b in range(2)]
        su = sb("su", [P, H, DV])
        eS = sb("eS", [P, H, 2, DV])
        ya = sb("ya", [P, H, DV])
        yb = sb("yb", [P, H, DV])
        ysq = sb("ysq", [P, H, DV])
        yS = sb("yS", [P, H, DV])
        hm = sb("hm", [P, H])
        hv = sb("hv", [P, H])
        hl = sb("hl", [P, H])
        hh = hl[:, :].bitcast(I32)
        ha = sb("ha", [P, H])
        hy = sb("hy", [P, H])
        yT = sb("yT", [P, KC, P])
        vf = sb("vf", [P, 2, VH, HD])
        vr = sb("vr", [P, VH, HD])
        v3 = sb("v3", [P, NT, VH, VW], BF16)
        nmx = sb("nmx", [P, NT, QH])
        nmr = sb("nmr", [P, TT, QH])
        nm3 = sb("nm3", [P, TT, 3, QH], BF16)
        mT = sb("mT", [3 * QH, B, T], BF16)
        rden = sb("rden", [P, TT, QH // 2])

        bank = ctx.enter_context(nc.psum_tensor("bank", [P, 8, 512], F32))

        w_gate = sem("w_gate")
        w_k = sem("w_k")
        w_q = sem("w_q")
        w_vg = sem("w_vg")
        w_gla = sem("w_gla")
        w_const = sem("w_const")
        identity_b = sem("identity_b")
        fills = sem("fills")
        w_ffn = sem("w_ffn")
        w_att = sem("w_att")
        padded = sem("padded")
        summed = sem("summed")
        totals = sem("totals")
        thresholds = sem("thresholds")
        ternary = sem("ternary")
        sel_step = sem("sel_step")
        stored = sem("stored")

        for n in ("x_in0 x_in1 x_in2 x_in3 x_in4 vec xnT_ps xnT_in u_ps u_in gk_ps abs_in expg_in lng_in g_in bt_ps en_in eb_in "
                  "eb_used kt_ps kk_in qt_ps q_in qq_in vg_ps vg_in tr_ps kkT_in p_ps cs_in vbd_in y1_in "
                  "u_state es_in o_ps o_used ycen_in ysq_in var_in lv_in root_in silu_step z_in ez_in ys_in ytr_ps yT_in wo_ps pool_step "
                  "qkv_ps qk_in v_in rope_a rope_b rope_used rot_in qT_in hi_in mid_in lo_in stk_in stk_ps qkT_in "
                  "row_ps max_in nm3_in mT_ps mT_in sc_ps prob_in ph_in pl_in vs_in pv_ps oS_in oT_ps oT_in bo_ps").split():
            sem(n)
        for s in (1, 2, 3, 4):
            for n in ("xn_in", "res_in"):
                sem(f"{n}{s}")
        for s in (2, 4):
            for n in ("xT_ps", "xh_in", "xl_in", "up_ps", "sig_in", "hid_in", "hh_in", "hl_in", "down_ps"):
                sem(f"{n}{s}")
        sem("xT3_ps")
        sem("xT3_in")

        def rsqrt(link, v, half, y, a):
            link(nc.vector.tensor_scalar(half, v.bitcast(I32), 1, None, ALU.logical_shift_right))
            link(nc.vector.tensor_scalar(y.bitcast(I32), half, -1.0, float(0x5F3759DF), ALU.mult, ALU.add))
            for _ in range(3):
                link(nc.vector.tensor_tensor(a, y, y, ALU.mult))
                link(nc.vector.scalar_tensor_tensor(out=a, in0=a, scalar=-0.5, in1=v, op0=ALU.mult, op1=ALU.mult))
                link(nc.vector.scalar_tensor_tensor(out=y, in0=a, scalar=1.5, in1=y, op0=ALU.add, op1=ALU.mult))

        x_v = x.rearrange("b (t p) d -> p (b t) d", p=P)
        out_v = out.rearrange("b (t p) d -> p (b t) d", p=P)
        FULL = (FT - 1) * P
        raw_parts = ((raw1, W1, P, 0, KC * F), (raw2, W2, P, 0, KC * F),
                     (raw3, W3, P, 0, (FT - 1) * D), (raw3, W3, F - FULL, (FT - 1) * D, FT * D))

        def rows_of(m):
            return min(P, F - m * P)

        UNITS = B * VH
        ROWS = TT * VH
        ROWS_EARLY = ROWS + 4
        TURN_AT = UNITS - 3

        def rows_at(t):
            return range(4 * (t - 3), 4 * (t - 2)) if t >= 3 else ()

        def next_row(u):
            return min(B * ROWS, ROWS_EARLY + 2 * u)

        NORM_STEPS = 2 * HTT + 13
        UPS = 2 * FT

        def up_bank(g):
            return 4 - 2 * (g % 2)

        block = ctx.enter_context(nc.Block())

        @block.sync
        def _(sp):
            def chunks(w):
                return w.rearrange("(k p) n -> p k n", p=P)

            for t in range(HTT):
                sp.dma_start(X[0][:, t, :], x_v[:, t, :]).then_inc(sems[f"x_in{t}"], 16)
            sp.dma_start(cf[:, :], const_f).then_inc(w_const, 16)
            sp.dma_start(Wg1[:, :, :], chunks(wgk1)).then_inc(w_gate, 16)
            sp.wait_ge(padded, 1)
            sp.dma_start(Wg2[0:LOW, :], wgk2).then_inc(w_gate, 16)
            sp.dma_start(Wg2[ONE_ROW:ONE_ROW + 1, :], bgk2.rearrange("(a n) -> a n", a=1)).then_inc(w_gate, 16)
            sp.dma_start(X[0][:, HTT:, :], x_v[:, HTT:, :]).then_inc(sems[f"x_in{HTT}"], 16)
            sp.dma_start(Wk[:, :, :], chunks(wk)).then_inc(w_k, 16)
            sp.dma_start(Wq[:, :, :], chunks(wq)).then_inc(w_q, 16)
            sp.dma_start(Wvg[:, :, 0:VD], chunks(wv)).then_inc(w_vg, 16)
            sp.dma_start(Wvg[:, :, VD:], chunks(wg)).then_inc(w_vg, 16)
            sp.dma_start(Wo[:, :, :], chunks(wo)).then_inc(w_gla, 16)
            sp.dma_start(lnw[:, :], ln_w.partition_broadcast(P)).then_inc(w_gla, 16)
            sp.dma_start(lnb[:, :], ln_b.partition_broadcast(P)).then_inc(w_gla, 16)
            sp.dma_start(raw1, chunks(w1t)).then_inc(w_ffn, 16)
            sp.dma_start(raw2, chunks(w2t)).then_inc(w_ffn, 16)
            sp.dma_start(raw3[:, 0:FT - 1, :], chunks(w3t[0:FULL, :])).then_inc(w_ffn, 16)
            sp.dma_start(raw3[0:F - FULL, FT - 1, :], w3t[FULL:F, :]).then_inc(w_ffn, 16)
            for w, a, b in ((bwq, 0, QH * HD), (bwk, QH * HD, QK), (bwv, QK, QK + VH * HD)):
                sp.dma_start(Wqkv[:, :, a:b], chunks(w)).then_inc(w_att, 16)
            sp.dma_start(Wob[:, :, :], chunks(bwo)).then_inc(w_att, 16)
            for t in range(NT):
                sp.wait_ge(sems["res_in4"], t + 1)
                sp.dma_start(out_v[:, t, :], X[4][:, t, :]).then_inc(stored, 16)
            sp.wait_ge(stored, 16 * NT)

        @block.tensor
        def _(pe):
            def turn(s, c, b0, name):
                for t in range(HTT):
                    pe.wait_ge(sems[f"xn_in{s}"], c * HTT + t + 1)
                    for k in range(KC):
                        last = nc.tensor.transpose(bank[:, b0 + k, t * P:(t + 1) * P],
                                                   xn[:, c * HTT + t, k * P:(k + 1) * P], ident)
                last.then_inc(sems[name], 1)

            def low_rank(c, b):
                pe.wait_ge(sems["xnT_in"], KC * (c + 1))
                for k in range(KC):
                    last = nc.tensor.matmul(bank[0:LOW, b, :], Wg1[:, k, :], xnT[:, k, c * HT:(c + 1) * HT],
                                            start=(k == 0), stop=(k == KC - 1))
                last.then_inc(sems["u_ps"], 1)

            def gate(n):
                t = ORDER[n]
                pe.wait_ge(sems["u_in"], n // HTT + 1)
                if n:
                    pe.wait_ge(sems["g_in"], n)
                for j in range(2):
                    last = nc.tensor.matmul(bank[:, j, :], uT[:, t * P:(t + 1) * P], Wg2[:, j * 512:(j + 1) * 512],
                                            start=True, stop=True)
                last.then_inc(sems["gk_ps"], 1)

            def cumsum(n):
                pe.wait_ge(sems["g_in"], n + 1)
                if n:
                    pe.wait_ge(sems["cs_in"], n)
                for h in range(H):
                    last = nc.tensor.matmul(bank[:, 2 + h // HH, (h % HH) * P:(h % HH + 1) * P],
                                            gS[:, h * DK:(h + 1) * DK], tril, start=True, stop=True)
                last.then_inc(sems["bt_ps"], 1)

            def project(n, w, hb, done):
                t = ORDER[n]
                for h in range(hb * HH, hb * HH + HH):
                    for k in range(KC):
                        last = nc.tensor.matmul(bank[:, 4 + hb, (h % HH) * P:(h % HH + 1) * P],
                                                w[:, k, h * DK:(h + 1) * DK], xnT[:, k, t * P:(t + 1) * P],
                                                start=(k == 0), stop=(k == KC - 1))
                last.then_inc(sems[done], 1)

            def read_state(n):
                pe.wait_ge(sems["es_in"], n + 1)
                if n:
                    pe.wait_ge(sems["res_in1"], n)
                else:
                    pe.wait_ge(thresholds, 1)
                for h in range(H):
                    last = nc.tensor.matmul(bank[:, 7, h * 2 * DV:(h + 1) * 2 * DV], qS[:, h, :],
                                            eS[:, h, :, :].rearrange("p c e -> p (c e)"), start=True, stop=True)
                last.then_inc(sems["o_ps"], 1)

            def turn_y(n):
                pe.wait_ge(sems["ys_in"], n + 1)
                yf = yS[:, :, :].rearrange("p h e -> p (h e)")
                for k in range(KC):
                    last = nc.tensor.transpose(bank[:, 7, k * P:(k + 1) * P], yf[:, k * P:(k + 1) * P], ident)
                last.then_inc(sems["ytr_ps"], 1)

            def project_y(n):
                pe.wait_ge(sems["yT_in"], n + 1)
                for k in range(KC):
                    last = nc.tensor.matmul(bank[:, 7, 0:D], yT[:, k, :], Wo[:, k, :],
                                            start=(k == 0), stop=(k == KC - 1))
                last.then_inc(sems["wo_ps"], 1)

            pe.wait_ge(w_const, 16)
            turn(1, 0, 4, "xnT_ps")
            pe.wait_ge(w_gate, 48)
            pe.wait_ge(padded, 2)
            low_rank(0, 6)
            gate(0)
            turn(1, 1, 2, "xnT_ps")
            low_rank(1, 7)
            pe.wait_ge(w_k, 16)
            pe.wait_ge(w_q, 16)
            pe.wait_ge(w_vg, 32)
            pe.wait_ge(w_gla, 48)
            for n in range(NT):
                t = ORDER[n]
                if n + 1 < NT:
                    gate(n + 1)
                cumsum(n)
                if n == NT - 1:
                    turn(2, 0, 0, "xT_ps2")
                if n == 1:
                    pe.wait_ge(summed, len(raw_parts))
                    pe.wait_ge(sems["u_in"], 2)
                    nc.tensor.matmul(bank[:, 7, 0:4], ones[:, :], asum[:, :], start=True, stop=True).then_inc(totals, 1)
                if n >= 2:
                    turn_y(n - 2)
                if n:
                    pe.wait_ge(sems["kkT_in"], 2 * n - 1)
                project(n, Wk, 0, "kt_ps")
                if n >= 2:
                    project_y(n - 2)
                if n:
                    pe.wait_ge(sems["kkT_in"], 2 * n)
                project(n, Wk, 1, "kt_ps")
                if n:
                    pe.wait_ge(sems["es_in"], n)
                for k in range(KC):
                    last = nc.tensor.matmul(bank[:, 6, :], xnT[:, k, t * P:(t + 1) * P], Wvg[:, k, :],
                                            start=(k == 0), stop=(k == KC - 1))
                last.then_inc(sems["vg_ps"], 1)
                if n:
                    read_state(n - 1)
                for hb in range(2):
                    pe.wait_ge(sems["kk_in"], 2 * n + hb + 1)
                    project(n, Wq, hb, "qt_ps")
                for hb in range(2):
                    pe.wait_ge(sems["q_in"], 2 * n + hb + 1)
                    for h in range(hb * HH, hb * HH + HH):
                        last = nc.tensor.transpose(bank[:, 4 + hb, (h % HH) * P:(h % HH + 1) * P], kk[:, h, :], ident)
                    last.then_inc(sems["tr_ps"], 1)
                pe.wait_ge(sems["qq_in"], 2 * n + 2)
                pe.wait_ge(sems["eb_in"], n + 1)
                for h in range(H):
                    last = nc.tensor.matmul(bank[:, 2 + h // HH, (h % HH) * P:(h % HH + 1) * P],
                                            kk[:, h, :], qq[:, h, :], start=True, stop=True)
                last.then_inc(sems["p_ps"], 1)
                pe.wait_ge(sems["vg_in"], n + 1)
                pe.wait_ge(sems["vbd_in"], n + 1)
                pe.wait_ge(sems["kkT_in"], 2 * n + 2)
                for h in range(H):
                    last = nc.tensor.matmul(bank[:, 6, h * 2 * DV:(h + 1) * 2 * DV], kkT[:, h, :],
                                            vbd[:, h, :, :].rearrange("p c e -> p (c e)"), start=True, stop=True)
                last.then_inc(sems["u_state"], 1)

            def up(s, g):
                c, m = g // FT, g % FT
                r = rows_of(m)
                pe.wait_ge(sems[f"xl_in{s}"], KC * (c + 1))
                if g >= 2:
                    pe.wait_ge(sems[f"hid_in{s}"], g - 1)
                for j, w in enumerate((W1, W2)):
                    for k in range(KC):
                        for part, xp in enumerate((xh, xl)):
                            last = nc.tensor.matmul(bank[0:r, up_bank(g) + j, :],
                                                    w[:, k, m * P:m * P + r], xp[:, k, c * HT:(c + 1) * HT],
                                                    start=(k == 0 and part == 0), stop=(k == KC - 1 and part == 1))
                last.then_inc(sems[f"up_ps{s}"], 1)

            def down(s, t):
                pe.wait_ge(sems[f"hl_in{s}"], FT * (t // HTT + 1))
                if t >= 2:
                    pe.wait_ge(sems[f"res_in{s}"], t - 1)
                for m in range(FT):
                    r = rows_of(m)
                    for part, hp in enumerate((hTh, hTl)):
                        last = nc.tensor.matmul(bank[:, 6 + t % 2, 0:D], hp[0:r, m, t * P:(t + 1) * P],
                                                W3[0:r, m, :], start=(m == 0 and part == 0),
                                                stop=(m == FT - 1 and part == 1))
                last.then_inc(sems[f"down_ps{s}"], 1)

            pe.wait_ge(ternary, len(raw_parts))
            up(2, 0)
            turn_y(NT - 2)
            project_y(NT - 2)
            pe.wait_ge(sems["cs_in"], NT)
            up(2, 1)
            read_state(NT - 1)
            up(2, 2)
            up(2, 3)
            turn_y(NT - 1)
            up(2, 4)
            project_y(NT - 1)
            up(2, 5)
            pe.wait_ge(sems["res_in1"], NT)
            down(2, 0)
            down(2, 1)
            turn(2, 1, 0, "xT_ps2")
            down(2, 2)
            down(2, 3)
            for g in range(FT, UPS):
                up(2, g)

            def qkv(t):
                pe.wait_ge(sems["xT3_in"], KC * (t // HTT + 1))
                if t >= 2:
                    pe.wait_ge(sems["v_in"], t - 1)
                else:
                    pe.wait_ge(sems["hid_in2"], UPS)
                for k in range(KC):
                    last = nc.tensor.matmul(bank[:, 2 + t % 2, :], xnT[:, k, t * P:(t + 1) * P], Wqkv[:, k, :],
                                            start=(k == 0), stop=(k == KC - 1))
                last.then_inc(sems["qkv_ps"], 1)

            def turn_stack(t):
                pe.wait_ge(sems["stk_in"], t + 1)
                if t == 0:
                    pe.wait_ge(sems["res_in2"], NT)
                for j in range(3):
                    if t and j == 0:
                        pe.wait_ge(sems["qT_in"], t)
                    elif t:
                        pe.wait_ge(sems["qkT_in"], 2 * (t - 1) + j)
                    pb = bank[0:SK, 4 + j, :].bitcast(BF16)
                    for h in range(8):
                        last = nc.tensor.transpose(
                            pb[:, h * P:(h + 1) * P],
                            stk[:, t % 2, 8 * j + h, :, :].rearrange("p s d -> p (s d)"), identb[:, :])
                    last.then_inc(sems["stk_ps"], 1)

            def row_scores(a):
                b, qt, g = a // 16, a // 8 % 2, a % 8
                if a >= 2:
                    pe.wait_ge(sems["max_in"], a - 1)
                else:
                    pe.wait_ge(sems["xT3_in"], 2 * KC)
                if a and a % ROWS == 0:
                    pe.wait_ge(sems["mT_in"], a // ROWS)
                k0 = b * T
                pe.wait_ge(sems["qT_in"], TT * (b + 1))
                pe.wait_ge(sems["qkT_in"], 2 * TT * (b + 1))
                for h2 in range(2):
                    last = nc.tensor.matmul(bank[:, a % 2, h2 * T:(h2 + 1) * T],
                                            qkT[:, 2 * g + h2, k0 + qt * P:k0 + (qt + 1) * P],
                                            qkT[:, QH + g, k0:k0 + T], start=True, stop=True)
                last.then_inc(sems["row_ps"], 1)

            def turn_max(b):
                pe.wait_ge(sems["nm3_in"], b + 1)
                pb = bank[0:3 * QH, 0, :].bitcast(BF16)
                for qt in range(TT):
                    last = nc.tensor.transpose(pb[:, qt * P:(qt + 1) * P],
                                               nm3[:, qt, :, :].rearrange("p s h -> p (s h)"), identb[:, :])
                last.then_inc(sems["mT_ps"], 1)

            def scores(u):
                b, g = u // VH, u % VH
                pe.wait_ge(sems["mT_in"], b + 1)
                if u >= 2:
                    pe.wait_ge(sems["prob_in"], u - 1)
                k0 = b * T
                for kt in range(TT):
                    dst = bank[:, 2 + 2 * (u % 2) + kt, :].rearrange("p (h q) -> p h q", h=2)
                    nc.tensor.matmul(dst, qkT[:, QH + g, k0 + kt * P:k0 + (kt + 1) * P],
                                     qkT[:, 2 * g:2 * g + 2, k0:k0 + T], start=True, stop=False)
                    for h2 in range(2):
                        last = nc.tensor.matmul(dst[:, h2, :], sel[:, 2 * g + h2, :], mT[:, b, :],
                                                start=False, stop=(h2 == 1))
                last.then_inc(sems["sc_ps"], 1)

            def values(u):
                b, g = u // VH, u % VH
                pe.wait_ge(sems["pl_in"], u + 1)
                pe.wait_ge(sems["vs_in"], TT * (b + 1))
                if u >= VH // 2 and g % (VH // 2) == 0:
                    pe.wait_ge(sems["oS_in"], u // (VH // 2))
                for h2 in range(2):
                    c = (2 * (g % (VH // 2)) + h2) * VW
                    for qt in range(TT):
                        for kt in range(TT):
                            for part, pr in enumerate((prob_h, prob_l)):
                                last = nc.tensor.matmul(bank[:, 6 + qt, c:c + VW],
                                                        pr[:, u % 3, kt, h2, qt * P:(qt + 1) * P],
                                                        v3[:, b * TT + kt, g, :], start=(kt == 0 and part == 0),
                                                        stop=(kt == TT - 1 and part == 1))
                last.then_inc(sems["pv_ps"], 1)

            def turn_o(b, rows):
                pe.wait_ge(sems["oS_in"], 2 * b + 2)
                pe.wait_ge(sems["max_in"], rows)
                for qt in range(TT):
                    for k in range(KC):
                        last = nc.tensor.transpose(bank[:, 0, (qt * KC + k) * P:(qt * KC + k + 1) * P],
                                                   oS[:, qt, k * P:(k + 1) * P], ident)
                last.then_inc(sems["oT_ps"], 1)

            def project_o(b):
                pe.wait_ge(sems["oT_in"], b + 1)
                for qt in range(TT):
                    for k in range(KC):
                        last = nc.tensor.matmul(bank[:, 1, qt * D:(qt + 1) * D], oT[:, qt, k, :], Wob[:, k, :],
                                                start=(k == 0), stop=(k == KC - 1))
                last.then_inc(sems["bo_ps"], 1)

            turn(3, 0, 0, "xT3_ps")
            down(2, 4)
            down(2, 5)
            pe.wait_ge(w_att, 64)
            pe.wait_ge(identity_b, 1)
            qkv(0)
            down(2, 6)
            down(2, 7)
            for t in range(NT):
                if t == 2:
                    pe.wait_ge(sems["xT3_in"], KC)
                    turn(3, 1, 0, "xT3_ps")
                if t + 1 < NT:
                    qkv(t + 1)
                for a in rows_at(t):
                    if a == ROWS:
                        turn_max(0)
                    row_scores(a)
                turn_stack(t)
            pe.wait_ge(sems["qT_in"], NT)
            pe.wait_ge(sems["qkT_in"], 2 * NT)
            for u in range(UNITS):
                b, g = u // VH, u % VH
                scores(u)
                if b and g == 4:
                    project_o(b - 1)
                    if next_row(u) < B * ROWS:
                        pe.wait_ge(sems["oT_in"], b)
                        pe.wait_ge(sems["res_in3"], TT * b)
                if next_row(u) < B * ROWS:
                    row_scores(next_row(u))
                if u:
                    values(u - 1)
                if next_row(u) < B * ROWS:
                    row_scores(next_row(u) + 1)
                    if next_row(u + 1) % ROWS == 0:
                        turn_max(next_row(u) // ROWS)
                if b and g == 3:
                    turn_o(b - 1, next_row(u + 1))
                if u == TURN_AT:
                    pe.wait_ge(sems["oT_in"], B - 1)
                    pe.wait_ge(sems["res_in3"], TT * (B - 1))
                    turn(4, 0, 0, "xT_ps4")
            values(UNITS - 1)
            pe.wait_ge(sems["prob_in"], UNITS)
            up(4, 0)
            pe.wait_ge(sems["xl_in4"], KC)
            turn_o(B - 1, B * ROWS)
            up(4, 1)
            project_o(B - 1)
            for g in range(2, FT - 1):
                up(4, g)
            pe.wait_ge(sems["res_in3"], NT)
            turn(4, 1, 0, "xT_ps4")
            for g in range(FT - 1, UPS):
                up(4, g)
                if FT + 1 <= g < FT + 3:
                    if g == FT + 1:
                        pe.wait_ge(sems["oS_in"], 2 * B)
                    down(4, g - FT - 1)
            for t in range(2, NT):
                down(4, t)

        @block.scalar
        def _(act):
            def turned(ps, done, c, b0):
                act.wait_ge(sems[ps], c + 1)
                for k in range(KC):
                    nc.scalar.activation(xnT[:, k, c * HT:(c + 1) * HT], bank[:, b0 + k, :],
                                         ACT.Copy).then_inc(sems[done], 1)

            def turned_low(c, b):
                act.wait_ge(sems["u_ps"], c + 1)
                nc.scalar.activation(uT[0:LOW, c * HT:(c + 1) * HT], bank[0:LOW, b, :], ACT.Copy).then_inc(sems["u_in"], 1)

            def magnitude(n):
                act.wait_ge(sems["gk_ps"], n + 1)
                if n:
                    act.wait_ge(sems["g_in"], n)
                nc.scalar.activation(absb, bank[:, 0:2, :].rearrange("p a n -> p (a n)"),
                                     ACT.Abs).then_inc(sems["abs_in"], 1)

            def decay(n):
                act.wait_ge(sems["abs_in"], n + 1)
                nc.scalar.activation(expb, absb, ACT.Exp, scale=-1.0).then_inc(sems["expg_in"], 1)
                act.wait_ge(sems["expg_in"], n + 1)
                nc.scalar.activation(absb, expb, ACT.Ln, bias=1.0).then_inc(sems["lng_in"], 1)

            def turned_y(n):
                act.wait_ge(sems["ytr_ps"], n + 1)
                nc.scalar.activation(yT[:, :, :].rearrange("p k t -> p (k t)"), bank[:, 7, 0:D],
                                     ACT.Copy).then_inc(sems["yT_in"], 1)

            def part_high(s, c):
                act.wait_ge(sems[f"xT_ps{s}"], c + 1)
                for k in range(KC):
                    nc.scalar.activation(xh[:, k, c * HT:(c + 1) * HT], bank[:, k, :],
                                         ACT.Copy, scale=XS).then_inc(sems[f"xh_in{s}"], 1)

            def square_y(n):
                act.wait_ge(sems["ycen_in"], n + 1)
                nc.scalar.activation(ysq[:, :, :], yb[:, :, :], ACT.Square).then_inc(sems["ysq_in"], 1)

            def root_y(n):
                act.wait_ge(sems["var_in"], n + 1)
                nc.scalar.activation(hl[:, :], hv[:, :], ACT.Ln, scale=1.0 / DV, bias=eps[:, :]).then_inc(sems["lv_in"], 1)
                act.wait_ge(sems["lv_in"], n + 1)
                nc.scalar.activation(hy[:, :], hl[:, :], ACT.Exp, scale=-0.5).then_inc(sems["root_in"], 1)

            def gate_y(n):
                act.wait_ge(sems["z_in"], n + 1)
                nc.scalar.activation(ysq[:, :, :], ya[:, :, :], ACT.Exp, scale=-1.0).then_inc(sems["silu_step"], 1)
                act.wait_ge(sems["silu_step"], 2 * n + 1)
                nc.scalar.activation(ysq[:, :, :], ysq[:, :, :], ACT.Ln, bias=1.0).then_inc(sems["silu_step"], 1)
                act.wait_ge(sems["silu_step"], 2 * n + 2)
                nc.scalar.activation(ysq[:, :, :], ysq[:, :, :], ACT.Exp, scale=-1.0).then_inc(sems["ez_in"], 1)

            act.preload_act_table_set("natural_log_exp_and_others")
            turned("xnT_ps", "xnT_in", 0, 4)
            act.wait_ge(padded, 3)
            turned_low(0, 6)
            magnitude(0)
            decay(0)
            turned("xnT_ps", "xnT_in", 1, 2)
            turned_low(1, 7)
            act.wait_ge(fills, 2)
            for n in range(NT):
                if n + 1 < NT:
                    magnitude(n + 1)
                act.wait_ge(sems["bt_ps"], n + 1)
                if n:
                    act.wait_ge(sems["eb_used"], n)
                cum = bank[:, 2:4, :].rearrange("p a (h t) -> p (a h) t", t=P)
                nc.scalar.activation(eN, cum, ACT.Exp, scale=-1.0).then_inc(sems["en_in"], 1)
                if n >= 2:
                    turned_y(n - 2)
                nc.scalar.activation(eB, cum, ACT.Exp).then_inc(sems["eb_in"], 1)
                if n + 1 < NT:
                    decay(n + 1)
                else:
                    part_high(2, 0)
                act.wait_ge(sems["vg_ps"], n + 1)
                if n:
                    act.wait_ge(sems["y1_in"], n)
                nc.scalar.activation(vgS[:, :], bank[:, 6, :], ACT.Copy).then_inc(sems["vg_in"], 1)
                if n:
                    square_y(n - 1)
                for hb in range(2):
                    act.wait_ge(sems["qt_ps"], 2 * n + hb + 1)
                    nc.scalar.activation(qS[:, hb * HH:(hb + 1) * HH, :].rearrange("p h t -> p (h t)"),
                                         bank[:, 4 + hb, :], ACT.Copy).then_inc(sems["q_in"], 1)
                if n:
                    root_y(n - 1)
                for hb in range(2):
                    act.wait_ge(sems["tr_ps"], 2 * n + hb + 1)
                    nc.scalar.activation(kkT[:, hb * HH:(hb + 1) * HH, :].rearrange("p h t -> p (h t)"),
                                         bank[:, 4 + hb, :], ACT.Copy).then_inc(sems["kkT_in"], 1)
                if n:
                    gate_y(n - 1)
                if n == 0:
                    act.wait_ge(w_ffn, 64)
                    for j, (raw, _w, rows, a, b) in enumerate(raw_parts):
                        if j:
                            act.wait_ge(summed, j)
                        nc.scalar.activation(junk[0:rows, 0:b - a], raw.rearrange("p k n -> p (k n)")[0:rows, a:b],
                                             ACT.Abs, accum_out=asum[0:rows, j:j + 1]).then_inc(summed, 1)

            def sigmoid(s, g):
                r = rows_of(g % FT)
                act.wait_ge(sems[f"up_ps{s}"], g + 1)
                if g >= 2:
                    act.wait_ge(sems[f"hid_in{s}"], g - 1)
                nc.scalar.activation(sg[0:r, g % 2, :], bank[0:r, up_bank(g), :], ACT.Sigmoid,
                                     scale=1.0 / XS).then_inc(sems[f"sig_in{s}"], 1)

            def high(s, g):
                c, m, r = g // FT, g % FT, rows_of(g % FT)
                act.wait_ge(sems[f"hid_in{s}"], g + 1)
                nc.scalar.activation(hTh[0:r, m, c * HT:(c + 1) * HT], hf[0:r, g % 2, :],
                                     ACT.Copy).then_inc(sems[f"hh_in{s}"], 1)

            turned_y(NT - 2)
            sigmoid(2, 0)
            sigmoid(2, 1)
            square_y(NT - 1)
            high(2, 0)
            sigmoid(2, 2)
            high(2, 1)
            sigmoid(2, 3)
            high(2, 2)
            act.wait_ge(sems["z_in"], NT)
            nc.scalar.activation(ysq[:, :, :], ya[:, :, :], ACT.Sigmoid).then_inc(sems["ez_in"], 1)
            turned_y(NT - 1)
            sigmoid(2, 4)
            high(2, 3)
            sigmoid(2, 5)
            high(2, 4)
            high(2, 5)
            part_high(2, 1)
            for g in range(FT, UPS):
                sigmoid(2, g)
                if g > FT:
                    high(2, g - 1)
            high(2, UPS - 1)

            def qkv_in(t):
                act.wait_ge(sems["qkv_ps"], t + 1)
                if t >= 2:
                    act.wait_ge(sems["rope_used"], t - 1)
                    act.wait_ge(sems["rope_b"], t - 1)
                    act.wait_ge(sems["vs_in"], t - 1)
                src = bank[:, 2 + t % 2, :]
                nc.scalar.activation(qk[:, t % 2, :, :].rearrange("p h d -> p (h d)"), src[:, 0:QK],
                                     ACT.Copy).then_inc(sems["qk_in"], 1)
                nc.scalar.activation(vf[:, t % 2, :, :], src[:, QK:].rearrange("p (h d) -> p h d", d=HD),
                                     ACT.Copy).then_inc(sems["v_in"], 1)

            def stacked(t):
                act.wait_ge(sems["stk_ps"], 3 * t + 1)
                nc.scalar.activation(qkT[:, 0:8, t * P:(t + 1) * P],
                                     bank[0:SK, 4, :].bitcast(BF16).rearrange("p (h q) -> p h q", q=P),
                                     ACT.Copy).then_inc(sems["qT_in"], 1)

            turned("xT3_ps", "xT3_in", 0, 0)
            qkv_in(0)
            for t in range(NT):
                s2, q2, r2 = stk[:, t % 2], ra[:, t % 2], rb[:, t % 2]
                act.wait_ge(sems["rot_in"], t + 1)
                if t >= 2:
                    act.wait_ge(sems["stk_ps"], 3 * (t - 1))
                nc.scalar.activation(s2[:, 0:QH, 0:3, :], q2[:, 0:QH, None, :].broadcast_to([P, QH, 3, HD]), ACT.Copy)
                nc.scalar.activation(s2[:, QH:, 0:4:3, :], q2[:, QH:, None, :].broadcast_to([P, VH, 2, HD]), ACT.Copy)
                nc.scalar.activation(s2[:, QH:, 5, :], q2[:, QH:, :], ACT.Copy).then_inc(sems["hi_in"], 1)
                if t == 3:
                    turned("xT3_ps", "xT3_in", 1, 0)
                if t + 1 < NT:
                    qkv_in(t + 1)
                if t:
                    stacked(t - 1)
                act.wait_ge(sems["mid_in"], t + 1)
                nc.scalar.activation(s2[:, 0:QH, 3:5, :], r2[:, 0:QH, None, :].broadcast_to([P, QH, 2, HD]), ACT.Copy)
                nc.scalar.activation(s2[:, QH:, 1:5:3, :], r2[:, QH:, None, :].broadcast_to([P, VH, 2, HD]),
                                     ACT.Copy).then_inc(sems["lo_in"], 1)
            stacked(NT - 1)

            def turned_o(b):
                act.wait_ge(sems["oT_ps"], b + 1)
                nc.scalar.activation(oT[:, :, :, :].rearrange("p a k t -> p (a k t)"), bank[:, 0, :],
                                     ACT.Copy).then_inc(sems["oT_in"], 1)

            for u in range(UNITS):
                b, g = u // VH, u % VH
                act.wait_ge(sems["sc_ps"], u + 1)
                if u >= 2:
                    act.wait_ge(sems["pl_in"], u - 1)
                b0 = 2 + 2 * (u % 2)
                nc.scalar.activation(prob[:, u % 2, :, :, :].rearrange("p k h q -> p (k h q)"),
                                     bank[:, b0:b0 + 2, :].rearrange("p a n -> p (a n)"), ACT.Exp,
                                     bias=shift[:, :], scale=HD ** -0.5).then_inc(sems["prob_in"], 1)
                if u >= 3:
                    act.wait_ge(sems["pv_ps"], u - 2)
                act.wait_ge(sems["prob_in"], u + 1)
                nc.scalar.activation(prob_h[:, u % 3, :, :, :].rearrange("p k h q -> p (k h q)"),
                                     prob[:, u % 2, :, :, :].rearrange("p k h q -> p (k h q)"),
                                     ACT.Copy).then_inc(sems["ph_in"], 1)
                if b and g == 3:
                    turned_o(b - 1)
                if u == TURN_AT:
                    part_high(4, 0)
            sigmoid(4, 0)
            turned_o(B - 1)
            for g in range(1, UPS):
                sigmoid(4, g)
                high(4, g - 1)
                if g == FT - 2:
                    part_high(4, 1)
            high(4, UPS - 1)

        @block.vector
        def _(dve):
            links = [0]

            def link(ins):
                links[0] += 1
                ins.then_inc(sems["vec"], 1)
                dve.wait_ge(sems["vec"], links[0])

            steps = {}

            def norm_steps(s, c, count):
                src = X[s - 1]
                var = mv[:, c * HTT:(c + 1) * HTT, 1]
                for _ in range(count):
                    i, waited = steps.get((s, c), (0, 0))
                    if i >= NORM_STEPS:
                        return
                    if i >= HTT:
                        dve.wait_ge(sems["vec"], waited)
                    if i < HTT:
                        t = c * HTT + i
                        if s == 1:
                            dve.wait_ge(sems[f"x_in{min(t, HTT)}"], 16)
                        elif s == 2:
                            dve.wait_ge(sems["res_in1"], ORDER.index(t) + 1)
                        else:
                            dve.wait_ge(sems[f"res_in{s - 1}"], t + 1)
                        last = nc.vector.bn_stats(st6[:, t, :], src[:, t, :])
                    elif i == HTT:
                        for t in range(c * HTT, (c + 1) * HTT):
                            last = nc.vector.bn_aggr(mv[:, t, :], st6[:, t, :])
                    elif i == HTT + 1:
                        last = nc.vector.tensor_scalar(nv[:, :], var, LN_EPS, None, ALU.add)
                    elif i == HTT + 2:
                        last = nc.vector.tensor_scalar(nh[:, :], nv[:, :].bitcast(I32), 1, None,
                                                       ALU.logical_shift_right)
                    elif i == HTT + 3:
                        last = nc.vector.tensor_scalar(ny[:, :].bitcast(I32), nh[:, :], -1.0, float(0x5F3759DF),
                                                       ALU.mult, ALU.add)
                    elif i < HTT + 13 and (i - HTT) % 3 == 1:
                        last = nc.vector.tensor_tensor(na[:, :], ny[:, :], ny[:, :], ALU.mult)
                    elif i < HTT + 13 and (i - HTT) % 3 == 2:
                        last = nc.vector.scalar_tensor_tensor(out=na[:, :], in0=na[:, :], scalar=-0.5, in1=nv[:, :],
                                                              op0=ALU.mult, op1=ALU.mult)
                    elif i < HTT + 13:
                        last = nc.vector.scalar_tensor_tensor(out=ny[:, :], in0=na[:, :], scalar=1.5, in1=ny[:, :],
                                                              op0=ALU.add, op1=ALU.mult)
                    else:
                        j = i - HTT - 13
                        t = c * HTT + j
                        last = nc.vector.tensor_scalar(xn[:, t, :], src[:, t, :], mv[:, t, 0:1], ny[:, j:j + 1],
                                                       ALU.subtract, ALU.mult)
                    if i >= HTT + 13:
                        last.then_inc(sems[f"xn_in{s}"], 1)
                        steps[s, c] = (i + 1, waited)
                    else:
                        last.then_inc(sems["vec"], 1)
                        links[0] += 1
                        steps[s, c] = (i + 1, links[0])

            def log_gate(n):
                dve.wait_ge(sems["lng_in"], n + 1)
                if n:
                    dve.wait_ge(sems["bt_ps"], n)
                nc.vector.scalar_tensor_tensor(out=gS, in0=bank[:, 0:2, :].rearrange("p a n -> p (a n)"),
                                               scalar=0.0, in1=absb, op0=ALU.min,
                                               op1=ALU.subtract).then_inc(sems["g_in"], 1)

            def residual_y(n):
                dve.wait_ge(sems["wo_ps"], n + 1)
                t = ORDER[n]
                nc.vector.tensor_tensor(X[1][:, t, :], bank[:, 7, 0:D], X[0][:, t, :],
                                        ALU.add).then_inc(sems["res_in1"], 1)

            def head_bc(v):
                return v[:, :, None].broadcast_to([P, H, DV])

            def add_state(n):
                dve.wait_ge(sems["o_ps"], n + 1)
                dve.wait_ge(sems["y1_in"], n + 1)
                o = bank[:, 7, :].rearrange("p (h c e) -> p h c e", h=H, c=2)
                for c in range(2):
                    r = slice(c * CH, (c + 1) * CH)
                    last = nc.vector.tensor_tensor(ya[r, :, :], o[r, :, c, :], y1[r, :, :], ALU.add)
                last.then_inc(sems["o_used"], 1)
                dve.wait_ge(sems["o_used"], n + 1)

            def centre_y(n):
                link(nc.vector.tensor_reduce(hm[:, :], ya[:, :, :], AX_X, ALU.add))
                nc.vector.scalar_tensor_tensor(out=yb[:, :, :], in0=head_bc(hm), scalar=-1.0 / DV, in1=ya[:, :, :],
                                               op0=ALU.mult, op1=ALU.add).then_inc(sems["ycen_in"], 1)

            def variance_y(n):
                dve.wait_ge(sems["ysq_in"], n + 1)
                nc.vector.tensor_reduce(hv[:, :], ysq[:, :, :], AX_X, ALU.add).then_inc(sems["var_in"], 1)

            def scale_y(n):
                if n + 1 < NT:
                    dve.wait_ge(sems["root_in"], n + 1)
                link(nc.vector.tensor_tensor(yb[:, :, :], yb[:, :, :], head_bc(hy), ALU.mult))
                link(nc.vector.tensor_tensor(yb[:, :, :], yb[:, :, :],
                                             lnw[:, None, :].broadcast_to([P, H, DV]), ALU.mult))
                nc.vector.tensor_tensor(ya[:, :, :], yb[:, :, :],
                                        lnb[:, None, :].broadcast_to([P, H, DV]), ALU.add).then_inc(sems["z_in"], 1)

            def silu_y(n):
                dve.wait_ge(sems["ez_in"], n + 1)
                nc.vector.tensor_tensor(yS[:, :, :], ya[:, :, :], ysq[:, :, :], ALU.mult).then_inc(sems["ys_in"], 1)
                dve.wait_ge(sems["ys_in"], n + 1)

            def part_low(s, c):
                for k in range(KC):
                    dve.wait_ge(sems[f"xh_in{s}"], KC * c + k + 1)
                    tok = slice(c * HT, (c + 1) * HT)
                    nc.vector.scalar_tensor_tensor(out=xl[:, k, tok], in0=bank[:, k, :], scalar=XS, in1=xh[:, k, tok],
                                                   op0=ALU.mult, op1=ALU.subtract).then_inc(sems[f"xl_in{s}"], 1)

            def state(n):
                dve.wait_ge(sems["u_state"], n + 1)
                if n:
                    dve.wait_ge(sems["o_ps"], n)
                u = bank[:, 6, :].rearrange("p (h c e) -> p h c e", h=H, c=2)
                Sb = S[n % 2]
                for c in range(2):
                    el = head_bc(eL[:, :, c])
                    if n % 4 < 2 and c == 0:
                        link(nc.vector.tensor_tensor(Sb[:, :, :], u[:, :, c, :], el, ALU.mult))
                    else:
                        link(nc.vector.tensor_tensor(su[:, :, :], u[:, :, c, :], Sb[:, :, :], ALU.add))
                        link(nc.vector.tensor_tensor(Sb[:, :, :], su[:, :, :], el, ALU.mult))
                    last = nc.vector.tensor_tensor(eS[:, :, c, :], Sb[:, :, :], el, ALU.mult)
                last.then_inc(sems["es_in"], 1)
                dve.wait_ge(sems["es_in"], n + 1)

            def thresholds_of_weights():
                dve.wait_ge(totals, 1)
                for k in range(6):
                    s = -0.5 if k > 2 else 0.5
                    last = nc.vector.tensor_scalar(thr[:, k:k + 1], bank[:, 7, k % 3:k % 3 + 1], s / (F * D), s * QEPS,
                                                   ALU.mult, ALU.add)
                link(last)
                for k in (2, 5):
                    s = -0.5 if k > 2 else 0.5
                    last = nc.vector.scalar_tensor_tensor(
                        out=thr[:, k:k + 1], in0=bank[:, 7, 3:4], scalar=s / (F * D),
                        in1=thr[:, k:k + 1], op0=ALU.mult, op1=ALU.add)
                last.then_inc(thresholds, 1)
                dve.wait_ge(thresholds, 1)

            def quantise(j):
                raw, w, rows, a, b = raw_parts[j]
                k = min(j, 2)
                r = raw.rearrange("p k n -> p (k n)")[0:rows, a:b]
                q = w[:, :, :].rearrange("p k n -> p (k n)")[0:rows, a:b]
                below = qtmp[0:rows, 0:b - a]
                link(nc.vector.tensor_scalar(below, r, thr[0:rows, 3 + k:4 + k], None, ALU.is_lt))
                nc.vector.scalar_tensor_tensor(out=q, in0=r, scalar=thr[0:rows, k:k + 1], in1=below,
                                               op0=ALU.is_gt, op1=ALU.subtract).then_inc(ternary, 1)
                dve.wait_ge(ternary, j + 1)

            norm_steps(1, 0, NORM_STEPS)
            norm_steps(1, 1, NORM_STEPS)
            dve.wait_ge(w_const, 16)
            nc.vector.tensor_copy(identb[:, :], ident).then_inc(identity_b, 1)
            nc.vector.memset(shift[:, :], PSHIFT).then_inc(fills, 1)
            nc.vector.memset(eps[:, :], LN_EPS).then_inc(fills, 1)
            log_gate(0)
            dve.wait_ge(w_gla, 48)
            for n in range(NT):
                dve.wait_ge(sems["en_in"], n + 1)
                if n:
                    dve.wait_ge(sems["p_ps"], n)
                for hb in range(2):
                    dve.wait_ge(sems["kt_ps"], 2 * n + hb + 1)
                    r = slice(hb * HH, (hb + 1) * HH)
                    nc.vector.tensor_tensor(kk[:, r, :], bank[:, 4 + hb, :].rearrange("p (h t) -> p h t", t=P),
                                            eN[:, r, :], ALU.mult).then_inc(sems["kk_in"], 1)
                    if n >= 2 and hb == 0:
                        residual_y(n - 2)
                if n == 1:
                    thresholds_of_weights()
                if n + 1 < NT:
                    log_gate(n + 1)
                else:
                    part_low(2, 0)
                if n:
                    add_state(n - 1)
                    centre_y(n - 1)
                dve.wait_ge(sems["eb_in"], n + 1)
                for hb in range(2):
                    dve.wait_ge(sems["q_in"], 2 * n + hb + 1)
                    r = slice(hb * HH, (hb + 1) * HH)
                    nc.vector.tensor_tensor(qq[:, r, :], qS[:, r, :], eB[:, r, :], ALU.mult).then_inc(sems["qq_in"], 1)
                    if n and hb == 0:
                        variance_y(n - 1)
                    if HTT < n < NT - 1:
                        norm_steps(2, 0, 4)
                nc.vector.tensor_copy(eL[:, :, :], eB[:, :, CH - 1:P:CH]).then_inc(sems["eb_used"], 1)
                dve.wait_ge(sems["eb_used"], n + 1)
                if n:
                    scale_y(n - 1)
                dve.wait_ge(sems["p_ps"], n + 1)
                link(nc.vector.tensor_tensor(pm, bank[:, 2:4, :].rearrange("p a (h t) -> p (a h) t", t=P),
                                             submask[:, None, :].broadcast_to([P, H, P]), ALU.mult))
                if n:
                    dve.wait_ge(sems["y1_in"], n)
                nc.vector.tensor_reduce(cs[:, :], pm, AX_X, ALU.add).then_inc(sems["cs_in"], 1)
                dve.wait_ge(sems["cs_in"], n + 1)
                if n:
                    silu_y(n - 1)
                state(n)
                if 1 <= n <= len(raw_parts):
                    quantise(n - 1)
                if n == NT - 2:
                    norm_steps(2, 0, NORM_STEPS)

            def hidden(s, g):
                r = rows_of(g % FT)
                dve.wait_ge(sems[f"sig_in{s}"], g + 1)
                if g >= 2:
                    dve.wait_ge(sems[f"hl_in{s}"], g - 1)
                nc.vector.scalar_tensor_tensor(
                    out=hf[0:r, g % 2, :], in0=bank[0:r, up_bank(g) + 1, :], scalar=HS / XS,
                    in1=sg[0:r, g % 2, :], op0=ALU.mult, op1=ALU.mult).then_inc(sems[f"hid_in{s}"], 1)

            def low(s, g):
                c, m, r = g // FT, g % FT, rows_of(g % FT)
                dve.wait_ge(sems[f"hh_in{s}"], g + 1)
                tok = slice(c * HT, (c + 1) * HT)
                nc.vector.tensor_tensor(hTl[0:r, m, tok], hf[0:r, g % 2, :], hTh[0:r, m, tok],
                                        ALU.subtract).then_inc(sems[f"hl_in{s}"], 1)

            def residual(s, t):
                dve.wait_ge(sems[f"down_ps{s}"], t + 1)
                nc.vector.scalar_tensor_tensor(
                    out=X[s][:, t, :], in0=bank[:, 6 + t % 2, 0:D], scalar=1.0 / HS,
                    in1=X[s - 1][:, t, :], op0=ALU.mult, op1=ALU.add).then_inc(sems[f"res_in{s}"], 1)

            hidden(2, 0)
            residual_y(NT - 2)
            add_state(NT - 1)
            centre_y(NT - 1)
            hidden(2, 1)
            low(2, 0)
            variance_y(NT - 1)
            dve.wait_ge(sems["var_in"], NT)
            link(nc.vector.tensor_scalar(hv[:, :], hv[:, :], 1.0 / DV, LN_EPS, ALU.mult, ALU.add))
            rsqrt(link, hv[:, :], hh, hy[:, :], ha[:, :])
            hidden(2, 2)
            low(2, 1)
            scale_y(NT - 1)
            hidden(2, 3)
            low(2, 2)
            silu_y(NT - 1)
            norm_steps(2, 1, HTT - 1)
            hidden(2, 4)
            low(2, 3)
            residual_y(NT - 1)
            norm_steps(2, 1, 4)
            hidden(2, 5)
            low(2, 4)
            norm_steps(2, 1, 4)
            low(2, 5)
            norm_steps(2, 1, NORM_STEPS)
            residual(2, 0)
            residual(2, 1)
            part_low(2, 1)
            residual(2, 2)
            residual(2, 3)
            for g in range(FT, UPS):
                hidden(2, g)
                if g > FT:
                    low(2, g - 1)
                norm_steps(3, 0, 4)
            low(2, UPS - 1)

            def rope_a(t):
                dve.wait_ge(sems["qk_in"], t + 1)
                if t >= 2:
                    dve.wait_ge(sems["stk_in"], t - 1)
                nc.vector.tensor_tensor(ra[:, t % 2, :, :], qk[:, t % 2, :, :],
                                        cosT[:, t % TT, None, :].broadcast_to([P, QH + VH, HD]),
                                        ALU.mult).then_inc(sems["rope_used"], 1)

            def rotate(t):
                dve.wait_ge(sems["rope_used"], t + 1)
                dve.wait_ge(sems["rope_b"], t + 1)
                nc.vector.tensor_tensor(ra[:, t % 2, :, :], ra[:, t % 2, :, :], rb[:, t % 2, :, :],
                                        ALU.add).then_inc(sems["rot_in"], 1)

            def split_values(t):
                dve.wait_ge(sems["v_in"], t + 1)
                if t == 0:
                    dve.wait_ge(padded, 3)
                vt = vf[:, t % 2, :, :]
                link(nc.vector.tensor_copy(v3[:, t, :, 0:HD], vt))
                link(nc.vector.tensor_tensor(vr[:, :, :], vt, v3[:, t, :, 0:HD], ALU.subtract))
                link(nc.vector.tensor_copy(v3[:, t, :, HD:2 * HD], vr[:, :, :]))
                nc.vector.tensor_tensor(v3[:, t, :, 2 * HD:3 * HD], vr[:, :, :], v3[:, t, :, HD:2 * HD],
                                        ALU.subtract).then_inc(sems["vs_in"], 1)
                dve.wait_ge(sems["vs_in"], t + 1)

            def middle(t):
                dve.wait_ge(sems["hi_in"], t + 1)
                q2, r2, s2 = ra[:, t % 2], rb[:, t % 2], stk[:, t % 2]
                nc.vector.tensor_tensor(r2[:, 0:QH, :], q2[:, 0:QH, :], s2[:, 0:QH, 0, :], ALU.subtract)
                nc.vector.tensor_tensor(r2[:, QH:, :], q2[:, QH:, :], s2[:, QH:, 0, :],
                                        ALU.subtract).then_inc(sems["mid_in"], 1)

            def last_part(t):
                dve.wait_ge(sems["mid_in"], t + 1)
                dve.wait_ge(sems["lo_in"], t + 1)
                r2, s2 = rb[:, t % 2], stk[:, t % 2]
                nc.vector.tensor_tensor(s2[:, 0:QH, 5, :], r2[:, 0:QH, :], s2[:, 0:QH, 3, :], ALU.subtract)
                nc.vector.tensor_tensor(s2[:, QH:, 2, :], r2[:, QH:, :], s2[:, QH:, 1, :],
                                        ALU.subtract).then_inc(sems["stk_in"], 1)

            def stacked(t, j):
                dve.wait_ge(sems["stk_ps"], 3 * t + j + 1)
                nc.vector.tensor_copy(qkT[:, 8 * j:8 * j + 8, t * P:(t + 1) * P],
                                      bank[0:SK, 4 + j, :].bitcast(BF16).rearrange("p (h q) -> p h q", q=P)
                                      ).then_inc(sems["qkT_in"], 1)

            def row_max(a):
                g = a % 8
                dve.wait_ge(sems["row_ps"], a + 1)
                nc.vector.tensor_reduce(nmx[:, a // 8, 2 * g:2 * g + 2],
                                        bank[:, a % 2, :].rearrange("p (h k) -> p h k", h=2), AX_X, ALU.max,
                                        negate=True).then_inc(sems["max_in"], 1)

            def split_max(b):
                dve.wait_ge(sems["max_in"], ROWS * (b + 1))
                src = nmx[:, b * TT:(b + 1) * TT, :]
                if b:
                    dve.wait_ge(sems["mT_ps"], b)
                link(nc.vector.tensor_copy(nm3[:, :, 0, :], src))
                link(nc.vector.tensor_tensor(nmr[:, :, :], src, nm3[:, :, 0, :], ALU.subtract))
                link(nc.vector.tensor_copy(nm3[:, :, 1, :], nmr[:, :, :]))
                nc.vector.tensor_tensor(nm3[:, :, 2, :], nmr[:, :, :], nm3[:, :, 1, :],
                                        ALU.subtract).then_inc(sems["nm3_in"], 1)

            def turned_max(b):
                dve.wait_ge(sems["mT_ps"], b + 1)
                nc.vector.tensor_copy(mT[:, b, :], bank[0:3 * QH, 0, :].bitcast(BF16)[:, 0:T]).then_inc(sems["mT_in"], 1)

            def normalise(w):
                b, hw = w // 2, w % 2
                dve.wait_ge(sems["pv_ps"], VH // 2 * (w + 1))
                if b and hw == 0:
                    dve.wait_ge(sems["oT_ps"], b)
                ov = bank[:, 6:8, 0:QH // 2 * VW].rearrange("p a (h e) -> p a h e", e=VW)
                nc.vector.reciprocal(rden[:, :, :], ov[:, :, :, VW - 1])
                for qt in range(TT):
                    last = nc.vector.tensor_reduce(
                        osum[:, qt, :, :], ov[:, qt, :, 0:3 * HD].rearrange("p h (s e) -> p h e s", s=3), AX_X, ALU.add)
                link(last)
                for qt in range(TT):
                    last = nc.vector.tensor_tensor(
                        oS[:, qt, hw * D // 2:(hw + 1) * D // 2].rearrange("p (h e) -> p h e", e=HD),
                        osum[:, qt, :, :], rden[:, qt, :, None].broadcast_to([P, QH // 2, HD]), ALU.mult)
                last.then_inc(sems["oS_in"], 1)
                dve.wait_ge(sems["oS_in"], w + 1)

            def prob_low(u):
                dve.wait_ge(sems["ph_in"], u + 1)
                nc.vector.tensor_tensor(prob_l[:, u % 3, :, :, :].rearrange("p k h q -> p (k h q)"),
                                        prob[:, u % 2, :, :, :].rearrange("p k h q -> p (k h q)"),
                                        prob_h[:, u % 3, :, :, :].rearrange("p k h q -> p (k h q)"),
                                        ALU.subtract).then_inc(sems["pl_in"], 1)

            def residual_o(b):
                dve.wait_ge(sems["bo_ps"], b + 1)
                for qt in range(TT):
                    t = b * TT + qt
                    nc.vector.tensor_tensor(X[3][:, t, :], bank[:, 1, qt * D:(qt + 1) * D], X[2][:, t, :],
                                            ALU.add).then_inc(sems["res_in3"], 1)

            residual(2, 4)
            residual(2, 5)
            rope_a(0)
            residual(2, 6)
            rotate(0)
            residual(2, 7)
            for t in range(NT):
                split_values(t)
                middle(t)
                if t < 2:
                    norm_steps(3, 1, NORM_STEPS if t else 10)
                if t + 1 < NT:
                    rope_a(t + 1)
                if t:
                    stacked(t - 1, 1)
                last_part(t)
                if t:
                    stacked(t - 1, 2)
                if t + 1 < NT:
                    rotate(t + 1)
                for a in rows_at(t):
                    if a == ROWS:
                        split_max(0)
                        turned_max(0)
                    row_max(a)
            stacked(NT - 1, 1)
            stacked(NT - 1, 2)
            for u in range(UNITS):
                b, g = u // VH, u % VH
                if b and g == 4:
                    residual_o(b - 1)
                more = next_row(u) < B * ROWS
                if more:
                    row_max(next_row(u))
                prob_low(u)
                if u and u % 4 == 0:
                    normalise(u // 4 - 1)
                if more:
                    row_max(next_row(u) + 1)
                    if next_row(u + 1) % ROWS == 0:
                        split_max(next_row(u) // ROWS)
                        turned_max(next_row(u) // ROWS)
                if 2 * VH + 4 < u < TURN_AT:
                    norm_steps(4, 0, 4)
                if u == TURN_AT:
                    part_low(4, 0)
            normalise(2 * B - 1)
            hidden(4, 0)
            hidden(4, 1)
            low(4, 0)
            residual_o(B - 1)
            for g in range(2, UPS):
                hidden(4, g)
                low(4, g - 1)
                norm_steps(4, 1, 7)
                if g == FT - 2:
                    part_low(4, 1)
                if FT + 1 <= g < FT + 3:
                    residual(4, g - FT - 1)
            low(4, UPS - 1)
            for t in range(2, NT):
                residual(4, t)

        @block.gpsimd
        def _(gp):
            nc.gpsimd.memset(Wg2[:, :], 0.0).then_inc(padded, 1)
            nc.gpsimd.memset(uT[:, :], 0.0)
            nc.gpsimd.memset(asum[:, :], 0.0)
            nc.gpsimd.memset(ones[:, :], 1.0)
            nc.gpsimd.memset(vbd[:, :, :, :], 0.0).then_inc(padded, 1)
            gp.wait_ge(padded, 2)
            nc.gpsimd.memset(uT[ONE_ROW:ONE_ROW + 1, :], 1.0).then_inc(padded, 1)
            gp.wait_ge(padded, 3)

            for n in range(NT):
                gp.wait_ge(sems["vg_in"], n + 1)
                if n:
                    gp.wait_ge(sems["u_state"], n)
                v = vgS[:, 0:VD].rearrange("p (h e) -> p h e", h=H)
                g = vgS[:, VD:].rearrange("p (h e) -> p h e", h=H)
                for c in range(2):
                    r = slice(c * CH, (c + 1) * CH)
                    last = nc.gpsimd.tensor_copy(vbd[r, :, c, :], v[r, :, :])
                last.then_inc(sems["vbd_in"], 1)
                gp.wait_ge(sems["vbd_in"], n + 1)
                gp.wait_ge(sems["cs_in"], n + 1)
                if n:
                    gp.wait_ge(sems["y1_in"], n)
                nc.gpsimd.tensor_tensor(y0[:, :, :], v, cs[:, :, None].broadcast_to([P, H, DV]),
                                        ALU.mult).then_inc(sems["pool_step"], 1)
                gp.wait_ge(sems["pool_step"], n + 1)
                if n:
                    gp.wait_ge(sems["o_used"], n)
                nc.gpsimd.tensor_tensor(y1[:, :, :], y0[:, :, :], g, ALU.add).then_inc(sems["y1_in"], 1)
                if n == 0:
                    gp.wait_ge(sems["y1_in"], 1)
                    nc.gpsimd.memset(v3[:, :, :, :], 1.0)
                    nc.gpsimd.memset(sel, 0.0).then_inc(sel_step, 1)
                    gp.wait_ge(sel_step, 1)
                    for part in range(3):
                        nc.gpsimd.affine_select(out=sel, in_=sel, compare_op=ALU.not_equal, fill=1.0,
                                                base=-part * QH, pattern=[[-1, QH], [0, P]],
                                                channel_multiplier=1).then_inc(sel_step, 1)
                        gp.wait_ge(sel_step, part + 2)
            gp.wait_ge(w_const, 16)
            for t in range(NT):
                gp.wait_ge(sems["qk_in"], t + 1)
                if t >= 2:
                    gp.wait_ge(sems["stk_in"], t - 1)
                for e in range(2):
                    last = nc.gpsimd.tensor_tensor(
                        rb[:, t % 2, :, e:HD:2], qk[:, t % 2, :, 1 - e:HD:2],
                        sinT[:, t % TT, None, e:HD:2].broadcast_to([P, QH + VH, HD // 2]), ALU.mult)
                last.then_inc(sems["rope_b"], 1)


def constants():
    r, c = np.arange(P)[:, None], np.arange(P)[None, :]
    tril = ((c >= r) & (c // CH == r // CH)).astype(np.float32) * np.float32(GATE)
    sub = ((c >= r) & (c // SC == r // SC)).astype(np.float32)
    inv = (1.0 / np.float32(10000.0) ** (np.arange(0, HD, 2, dtype=np.float32) / np.float32(HD))).astype(np.float32)
    ang = np.arange(T, dtype=np.float32)[:, None] * inv[None, :]
    cos = np.repeat(np.cos(ang), 2, axis=1).reshape(TT, P, HD).transpose(1, 0, 2).reshape(P, TT * HD)
    sin = np.stack([-np.sin(ang), np.sin(ang)], -1).reshape(TT, P, HD).transpose(1, 0, 2).reshape(P, TT * HD)
    eye = np.eye(P, dtype=np.float32)
    cf = np.concatenate([eye, tril, sub, cos, sin], axis=1).astype(np.float32)
    return cf


def kernel(**inputs):
    import numpy as _np
    import concourse.bacc as _bacc
    from concourse import mybir as _mybir
    from concourse.bass_utils import run_bass_kernel_spmd as _run

    nc = _bacc.Bacc("TRN2", target_bir_lowering=False, num_devices=1)
    a = {k: _np.ascontiguousarray(v) for k, v in inputs.items()}
    cf = constants()
    p, q, f = "L0_attn_a_", "L0_attn_b_", "L0_ffn_"
    arrays = {
        "x": a[p + "hidden_states"], "wq": a[p + "Wq"], "wk": a[p + "Wk"], "wv": a[p + "Wv"], "wg": a[p + "Wg"],
        "wgk1": a[p + "Wgk1"], "wgk2": a[p + "Wgk2"], "bgk2": a[p + "bgk2"], "wo": a[p + "Wo"],
        "ln_w": a[p + "ln_w"], "ln_b": a[p + "ln_b"],
        "w1t": _np.ascontiguousarray(a[f + "w1"].T), "w2t": _np.ascontiguousarray(a[f + "w2"].T),
        "w3t": _np.ascontiguousarray(a[f + "w3"].T),
        "bwq": a[q + "wq"], "bwk": a[q + "wk"], "bwv": a[q + "wv"], "bwo": a[q + "wo"],
        "const_f": cf,
    }
    args = [nc.dram_tensor(f"in_{n}", v.shape, _mybir.dt.from_np(v.dtype), kind="ExternalInput").ap()
            for n, v in arrays.items()]
    y = nc.dram_tensor("out_0", a[p + "hidden_states"].shape, _mybir.dt.float32, kind="ExternalOutput").ap()
    build(nc, *args, y)
    r = _run(nc, [{f"in_{n}": v for n, v in arrays.items()}], core_ids=[0])
    return r.results[0]["out_0"]
```

```python
from contextlib import ExitStack

import numpy as np

import concourse.bass as bass
from concourse import mybir

F32 = mybir.dt.float32
F16 = mybir.dt.float16
BF16 = mybir.dt.bfloat16
I32 = mybir.dt.int32
ALU = mybir.AluOpType
ACT = mybir.ActivationFunctionType
AX_X = mybir.AxisListType.X

P = 128
B, T, D = 4, 256, 256
KC = D // P
TT = T // P
NT = B * TT
NTOK = NT * P
HT = NTOK // 2
HTT = HT // P
LN_EPS = 1e-5

H, DK, DV = 8, 128, 32
KD, VD = H * DK, H * DV
CH, SC, LOW = 64, 16, 16
GATE = 1.0 / 16.0
GS = 6 * LOW
ONE_ROW, UK = 32, 64
HH = H // 2
GP = GS // LOW

F = 704
FT = -(-F // P)
QEPS = 1e-8
XS, HS = 2048.0, 128.0

QH, VH, HD = 16, 8, 16
QK = (QH + VH) * HD
PARTS = 6
SK = PARTS * HD
SM = SK + 3
VW = 3 * HD + 1
PSHIFT = 9.0

ORDER = [0, 2, 1, 3, 4, 6, 5, 7]


def build(nc, x, wq, wk, wv, wg, wgk1, wgk2, bgk2, wo, ln_w, ln_b, w1t, w2t, w3t,
          bwq, bwk, bwv, bwo, const_f, out):
    ctx = ExitStack()
    with ctx:
        def sb(name, shape, dt=F32):
            return ctx.enter_context(nc.sbuf_tensor(name, shape, dt))

        sems = {}

        def sem(name):
            sems[name] = ctx.enter_context(nc.semaphore(name))
            return sems[name]

        Wq = sb("Wq", [P, KC, KD])
        Wk = sb("Wk", [P, KC, KD])
        Wvg = sb("Wvg", [P, KC, 2 * VD])
        Wg1 = sb("Wg1", [P, KC, LOW])
        Wg2 = sb("Wg2", [UK, KD])
        Wg1s = sb("Wg1s", [P, KC, GP, LOW])
        Wg2s = sb("Wg2s", [GS + 3, KD], BF16)
        Wo = sb("Wo", [P, KC, D])
        lnw = sb("lnw", [P, DV])
        lnb = sb("lnb", [P, DV])
        RAW = 2 * KC * F + FT * D
        region = sb("region", [P, (QH + VH) * NTOK // 2])
        raw1 = region[:, 0:KC * F].rearrange("p (k n) -> p k n", k=KC)
        raw2 = region[:, KC * F:2 * KC * F].rearrange("p (k n) -> p k n", k=KC)
        raw3 = region[:, 2 * KC * F:RAW].rearrange("p (k n) -> p k n", k=FT)
        qtmp = region[:, RAW:RAW + KC * F]
        junk = region[:, RAW + KC * F:RAW + 2 * KC * F]
        HID = FT * NTOK // 2
        hTh = region[:, 0:HID].bitcast(F16).rearrange("p (m t) -> p m t", m=FT)
        hTl = region[:, HID:2 * HID].bitcast(F16).rearrange("p (m t) -> p m t", m=FT)
        qkT = region[0:SM, :].bitcast(BF16).rearrange("p (h t) -> p h t", t=NTOK)
        W1 = sb("W1", [P, KC, F], F16)
        W2 = sb("W2", [P, KC, F], F16)
        W3 = sb("W3", [P, FT, D], F16)
        Wqkv = sb("Wqkv", [P, KC, QK + VH * HD])
        Wob = sb("Wob", [P, KC, D])
        cf = sb("cf", [P, 3 * P + 2 * TT * HD + 4])
        ident = cf[:, 0:P]
        tril = cf[:, P:2 * P]
        submask = cf[:, 2 * P:3 * P]
        cosT = cf[:, 3 * P:3 * P + TT * HD].rearrange("p (t d) -> p t d", t=TT)
        sinT = cf[:, 3 * P + TT * HD:3 * P + 2 * TT * HD].rearrange("p (t d) -> p t d", t=TT)
        off_u, off_w = (cf[0:GS + 3, 3 * P + 2 * TT * HD + j:3 * P + 2 * TT * HD + j + 2] for j in (0, 2))
        identb = sb("identb", [P, P], BF16)
        ones = sb("ones", [P, P])
        asum = sb("asum", [P, 4])
        thr = sb("thr", [P, 6])
        shift = sb("shift", [P, 1])
        eps = sb("eps", [P, 1])

        Xe, Xo = sb("Xe", [P, NT, D]), sb("Xo", [P, NT, D])
        X = [Xe, Xo, Xe, Xo, Xe]
        rawg = Xo[0:GS + 3, 0:NT // 2, :].rearrange("p t d -> p (t d)")
        resg = Xo[0:GS + 3, NT // 2:, :].rearrange("p t d -> p (t d)")
        xn = sb("xn", [P, NT, D])
        xnT = sb("xnT", [P, KC, NTOK])
        xh = xnT[:, 0, :].bitcast(F16).rearrange("p (k t) -> p k t", k=KC)
        xl = xnT[:, 1, :].bitcast(F16).rearrange("p (k t) -> p k t", k=KC)
        st6 = sb("st6", [P, NT, 6])
        mv = sb("mv", [P, NT, 2])
        nv = sb("nv", [P, HTT])
        nh = sb("nh", [P, HTT], I32)
        ny = sb("ny", [P, HTT])
        na = sb("na", [P, HTT])
        uT = sb("uT", [UK, HT])
        uS = sb("uS", [GS + 3, NTOK], BF16)
        scratch = sb("scratch", [P, 10, KD])
        absb, expb, gS = scratch[:, 0, :], scratch[:, 1, :], scratch[:, 2, :]

        def heads(j):
            return scratch[:, j, :].rearrange("p (h t) -> p h t", t=P)

        eN, eB, kk, qq, qS, kkT, pm = (heads(j) for j in range(3, 10))
        prob = scratch[:, 0:3, :].rearrange("p s (k h q) -> p s k h q", k=TT, h=2)
        prob_h, prob_l = (scratch[:, j:j + 2, :].rearrange("p a n -> p (a n)").bitcast(F16).rearrange(
            "p (s k h q) -> p s k h q", s=4, k=TT, h=2) for j in (3, 5))
        sg = scratch[:, 6, :].rearrange("p (s t) -> p s t", s=2)
        hf = scratch[:, 3, :].rearrange("p (s t) -> p s t", s=2)
        stk = scratch[:, 0:3, :].rearrange("p a n -> p (a n)").bitcast(BF16)[:, 0:2 * PARTS * QK]
        stk = stk.rearrange("p (a h s d) -> p a h s d", a=2, s=PARTS, d=HD)
        qk, ra, rb = (scratch[:, j, 0:2 * QK].rearrange("p (a h d) -> p a h d", a=2, d=HD) for j in (3, 4, 5))
        osum = scratch[:, 8, 0:D].rearrange("p (t h d) -> p t h d", t=TT, d=HD)
        oS = scratch[:, 9, 0:TT * D].rearrange("p (t n) -> p t n", t=TT)
        oT = scratch[:, 9, TT * D:2 * TT * D].rearrange("p (t k q) -> p t k q", t=TT, k=KC)
        eL = sb("eL", [P, H, 2])
        cs = sb("cs", [P, H])
        vgS = sb("vgS", [P, 2 * VD])
        vbd = sb("vbd", [P, H, 2, DV])
        y0 = sb("y0", [P, H, DV])
        y1 = sb("y1", [P, H, DV])
        S = [sb(f"S{b}", [P, H, DV]) for b in range(2)]
        su = sb("su", [P, H, DV])
        eS = sb("eS", [P, H, 2, DV])
        ya = sb("ya", [P, H, DV])
        yb = sb("yb", [P, H, DV])
        ysq = sb("ysq", [P, H, DV])
        yS = sb("yS", [P, H, DV])
        hm = sb("hm", [P, H])
        hv = sb("hv", [P, H])
        hl = sb("hl", [P, H])
        hh = hl[:, :].bitcast(I32)
        ha = sb("ha", [P, H])
        hy = sb("hy", [P, H])
        yT = sb("yT", [P, KC, P])
        vf = sb("vf", [P, 2, VH, HD])
        vr = sb("vr", [P, VH, HD])
        v3 = sb("v3", [P, NT, VH, VW], BF16)
        nmx = sb("nmx", [P, NT, QH])
        nmr = sb("nmr", [P, TT, QH])
        nm3 = sb("nm3", [P, TT, 3, QH], BF16)
        mT = sb("mT", [3 * QH, B, T], BF16)
        rden = sb("rden", [P, TT, QH // 2])

        bank = ctx.enter_context(nc.psum_tensor("bank", [P, 8, 512], F32))

        w_gate = sem("w_gate")
        w_stack = sem("w_stack")
        w_k = sem("w_k")
        w_q = sem("w_q")
        w_vg = sem("w_vg")
        w_gla = sem("w_gla")
        w_const = sem("w_const")
        identity_b = sem("identity_b")
        fills = sem("fills")
        w_ffn = sem("w_ffn")
        w_att = sem("w_att")
        padded = sem("padded")
        summed = sem("summed")
        totals = sem("totals")
        thresholds = sem("thresholds")
        ternary = sem("ternary")
        stored = sem("stored")

        for n in (
                "x_in0 x_in1 x_in2 x_in3 x_in4 vec xnT_ps xnT_in u_ps u_in wg1s_in wg2s_in us_in gk_ps "
                "abs_in expg_in lng_in g_in bt_ps en_in eb_in eb_used "
                "kt_ps kk_in qt_ps q_in qq_in vg_ps vg_in vbd_in tr_ps kkT_in p_ps cs_in pool_step y1_in "
                "u_state es_in o_ps o_used "
                "ycen_in ysq_in var_in lv_in root_in z_in silu_step ez_in ys_in ytr_ps yT_in wo_ps "
                "qkv_ps qk_in v_in rope_b rope_used rot_in hi_in mid_in lo_in stk_in stk_ps qT_in kT_in "
                "v_step vs_in unit_rows "
                "row_ps max_in nm3_in mT_ps mT_in row_parts sc_ps prob_in ph_in pl_in pl_pool pv_ps "
                "oS_in oT_ps oT_in bo_ps").split():
            sem(n)
        for s in (1, 2, 3, 4):
            for n in ("xn_in", "res_in"):
                sem(f"{n}{s}")
        for s in (2, 4):
            for n in ("xT_ps", "xh_in", "xl_in", "up_ps", "sig_in", "hid_in", "hh_in", "hl_in", "down_ps"):
                sem(f"{n}{s}")
        sem("xT3_ps")
        sem("xT3_in")

        def rsqrt(link, v, half, y, a, rounds):
            link(nc.vector.tensor_scalar(half, v.bitcast(I32), 1, None, ALU.logical_shift_right))
            link(nc.vector.tensor_scalar(y.bitcast(I32), half, -1.0, float(0x5F3759DF), ALU.mult, ALU.add))
            newton(link, v, y, a, rounds)

        def newton(link, v, y, a, rounds):
            for _ in range(rounds):
                link(nc.vector.tensor_tensor(a, y, y, ALU.mult))
                link(nc.vector.scalar_tensor_tensor(out=a, in0=a, scalar=-0.5, in1=v, op0=ALU.mult, op1=ALU.mult))
                link(nc.vector.scalar_tensor_tensor(out=y, in0=a, scalar=1.5, in1=y, op0=ALU.add, op1=ALU.mult))

        x_v = x.rearrange("b (t p) d -> p (b t) d", p=P)
        out_v = out.rearrange("b (t p) d -> p (b t) d", p=P)
        FULL = (FT - 1) * P
        raw_parts = ((raw1, W1, P, 0, KC * F), (raw2, W2, P, 0, KC * F),
                     (raw3, W3, P, 0, (FT - 1) * D), (raw3, W3, F - FULL, (FT - 1) * D, FT * D))

        def rows_of(m):
            return min(P, F - m * P)

        UNITS = B * VH
        ROWS = TT * VH
        ROWS_EARLY = ROWS + 4
        TURN_AT = UNITS - 3
        POOL_EVERY, POOL_UNTIL = 2, (B * ROWS - ROWS_EARLY) // 2

        def rows_at(t):
            return range(4 * (t - 3), 4 * (t - 2)) if t >= 3 else ()

        def pool_low(u):
            return u % POOL_EVERY == 1 and u < POOL_UNTIL

        def pool_lows(u):
            return sum(pool_low(v) for v in range(u))

        def lows(u):
            return u - pool_lows(u)

        def next_row(u):
            return min(B * ROWS, ROWS_EARLY + 2 * u)

        NORM_STEPS = 2 * HTT + 13
        LOW_PARTS = ((6, slice(0, P)), (7, slice(P, HT)), (7, slice(HT, NTOK)))
        UPS = 2 * FT

        def up_bank(g):
            return 4 - 2 * (g % 2)

        block = ctx.enter_context(nc.Block())

        @block.sync
        def _(sp):
            def chunks(w):
                return w.rearrange("(k p) n -> p k n", p=P)

            for t in range(HTT):
                sp.dma_start(X[0][:, t, :], x_v[:, t, :]).then_inc(sems[f"x_in{t}"], 16)
            sp.dma_start(cf[:, :], const_f).then_inc(w_const, 16)
            sp.dma_start(Wg1[:, :, :], chunks(wgk1)).then_inc(w_gate, 16)
            sp.wait_ge(padded, 1)
            sp.dma_start(Wg2[0:LOW, :], wgk2).then_inc(w_gate, 16)
            sp.dma_start(Wg2[ONE_ROW:ONE_ROW + 1, :], bgk2.rearrange("(a n) -> a n", a=1)).then_inc(w_gate, 16)
            sp.dma_start(X[0][:, HTT:, :], x_v[:, HTT:, :]).then_inc(sems[f"x_in{HTT}"], 16)
            sp.dma_start(Wk[:, :, :], chunks(wk)).then_inc(w_k, 16)
            for part in range(GP):
                sp.dma_start(rawg[part * LOW:(part + 1) * LOW, :], wgk2).then_inc(w_stack, 16)
            for part in range(3):
                sp.dma_start(rawg[GS + part:GS + part + 1, :],
                             bgk2.rearrange("(a n) -> a n", a=1)).then_inc(w_stack, 16)
            sp.dma_start(Wq[:, :, :], chunks(wq)).then_inc(w_q, 16)
            sp.dma_start(Wvg[:, :, 0:VD], chunks(wv)).then_inc(w_vg, 16)
            sp.dma_start(Wvg[:, :, VD:], chunks(wg)).then_inc(w_vg, 16)
            sp.dma_start(Wo[:, :, :], chunks(wo)).then_inc(w_gla, 16)
            sp.dma_start(lnw[:, :], ln_w.partition_broadcast(P)).then_inc(w_gla, 16)
            sp.dma_start(lnb[:, :], ln_b.partition_broadcast(P)).then_inc(w_gla, 16)
            sp.dma_start(raw1, chunks(w1t)).then_inc(w_ffn, 16)
            sp.dma_start(raw2, chunks(w2t)).then_inc(w_ffn, 16)
            sp.dma_start(raw3[:, 0:FT - 1, :], chunks(w3t[0:FULL, :])).then_inc(w_ffn, 16)
            sp.dma_start(raw3[0:F - FULL, FT - 1, :], w3t[FULL:F, :]).then_inc(w_ffn, 16)
            for w, a, b in ((bwq, 0, QH * HD), (bwk, QH * HD, QK), (bwv, QK, QK + VH * HD)):
                sp.dma_start(Wqkv[:, :, a:b], chunks(w)).then_inc(w_att, 16)
            sp.dma_start(Wob[:, :, :], chunks(bwo)).then_inc(w_att, 16)
            for b in range(B):
                sp.wait_ge(sems["mT_in"], b + 1)
                for part in range(3):
                    sp.dma_start(qkT[SK + part:SK + part + 1, 0:QH, b * T:(b + 1) * T],
                                 mT[part * QH:(part + 1) * QH, b, :]).then_inc(sems["row_parts"], 16)
            for t in range(NT):
                sp.wait_ge(sems["res_in4"], t + 1)
                sp.dma_start(out_v[:, t, :], X[4][:, t, :]).then_inc(stored, 16)
            sp.wait_ge(stored, 16 * NT)

        @block.tensor
        def _(pe):
            def turn(s, c, b0, name):
                for t in range(HTT):
                    pe.wait_ge(sems[f"xn_in{s}"], c * HTT + t + 1)
                    for k in range(KC):
                        last = nc.tensor.transpose(bank[:, b0 + k, t * P:(t + 1) * P],
                                                   xn[:, c * HTT + t, k * P:(k + 1) * P], ident)
                last.then_inc(sems[name], 1)

            def low_rank(i):
                b, tok = LOW_PARTS[i]
                pe.wait_ge(sems["xnT_in"], KC * (2 if i == 2 else 1))
                if i == 1:
                    pe.wait_ge(sems["wg1s_in"], 1)
                if i == 2:
                    pe.wait_ge(sems["us_in"], 1)
                for k in range(KC):
                    w = Wg1s[:, k, :, :].rearrange("p s r -> p (s r)") if i else Wg1[:, k, :]
                    last = nc.tensor.matmul(bank[0:GS if i else LOW, b, 0:tok.stop - tok.start], w, xnT[:, k, tok],
                                            start=(k == 0), stop=(k == KC - 1))
                last.then_inc(sems["u_ps"], 1)

            def gate(n):
                t = ORDER[n]
                if n < 2:
                    pe.wait_ge(sems["u_in"], n + 1)
                else:
                    pe.wait_ge(sems["us_in"], n // HTT + 1)
                    pe.wait_ge(sems["wg2s_in"], 1)
                    pe.wait_ge(padded, 4)
                if n:
                    pe.wait_ge(sems["g_in"], n)
                for j in range(2):
                    cols = slice(j * 512, (j + 1) * 512)
                    if n < 2:
                        last = nc.tensor.matmul(bank[:, j, :], uT[:, t * P:(t + 1) * P], Wg2[:, cols],
                                                start=True, stop=True)
                    else:
                        last = nc.tensor.matmul(bank[:, j, :], uS[:, t * P:(t + 1) * P], Wg2s[:, cols],
                                                start=True, stop=True)
                last.then_inc(sems["gk_ps"], 1)

            def cumsum(n):
                pe.wait_ge(sems["g_in"], n + 1)
                if n:
                    pe.wait_ge(sems["cs_in"], n)
                for h in range(H):
                    last = nc.tensor.matmul(bank[:, 2 + h // HH, (h % HH) * P:(h % HH + 1) * P],
                                            gS[:, h * DK:(h + 1) * DK], tril, start=True, stop=True)
                last.then_inc(sems["bt_ps"], 1)

            def project(n, w, hb, done):
                t = ORDER[n]
                for h in range(hb * HH, hb * HH + HH):
                    for k in range(KC):
                        last = nc.tensor.matmul(bank[:, 4 + hb, (h % HH) * P:(h % HH + 1) * P],
                                                w[:, k, h * DK:(h + 1) * DK], xnT[:, k, t * P:(t + 1) * P],
                                                start=(k == 0), stop=(k == KC - 1))
                last.then_inc(sems[done], 1)

            def read_state(n):
                pe.wait_ge(sems["es_in"], n + 1)
                if n:
                    pe.wait_ge(sems["res_in1"], n)
                else:
                    pe.wait_ge(thresholds, 1)
                for h in range(H):
                    last = nc.tensor.matmul(bank[:, 7, h * 2 * DV:(h + 1) * 2 * DV], qS[:, h, :],
                                            eS[:, h, :, :].rearrange("p c e -> p (c e)"), start=True, stop=True)
                last.then_inc(sems["o_ps"], 1)

            def turn_y(n):
                pe.wait_ge(sems["ys_in"], n + 1)
                yf = yS[:, :, :].rearrange("p h e -> p (h e)")
                for k in range(KC):
                    last = nc.tensor.transpose(bank[:, 7, k * P:(k + 1) * P], yf[:, k * P:(k + 1) * P], ident)
                last.then_inc(sems["ytr_ps"], 1)

            def project_y(n):
                pe.wait_ge(sems["yT_in"], n + 1)
                for k in range(KC):
                    last = nc.tensor.matmul(bank[:, 7, 0:D], yT[:, k, :], Wo[:, k, :],
                                            start=(k == 0), stop=(k == KC - 1))
                last.then_inc(sems["wo_ps"], 1)

            pe.wait_ge(w_const, 16)
            turn(1, 0, 4, "xnT_ps")
            pe.wait_ge(w_gate, 48)
            pe.wait_ge(padded, 2)
            low_rank(0)
            gate(0)
            low_rank(1)
            pe.wait_ge(w_k, 16)
            pe.wait_ge(sems["xnT_in"], KC)
            project(0, Wk, 0, "kt_ps")
            project(0, Wk, 1, "kt_ps")
            pe.wait_ge(w_q, 16)
            pe.wait_ge(w_vg, 32)
            pe.wait_ge(w_gla, 48)
            for n in range(NT):
                t = ORDER[n]
                if n == 0:
                    cumsum(n)
                if n + 1 < NT:
                    gate(n + 1)
                if n:
                    pe.wait_ge(sems["kkT_in"], 2 * n - 1)
                    project(n, Wk, 0, "kt_ps")
                    cumsum(n)
                if n == NT - 1:
                    turn(2, 0, 0, "xT_ps2")
                if n == 1:
                    pe.wait_ge(summed, len(raw_parts))
                    pe.wait_ge(sems["us_in"], 2)
                    nc.tensor.matmul(bank[:, 7, 0:4], ones[:, :], asum[:, :],
                                     start=True, stop=True).then_inc(totals, 1)
                if n >= 2:
                    turn_y(n - 2)
                if n:
                    pe.wait_ge(sems["kkT_in"], 2 * n)
                    project(n, Wk, 1, "kt_ps")
                if n >= 2:
                    project_y(n - 2)
                for hb in range(2):
                    pe.wait_ge(sems["kk_in"], 2 * n + hb + 1)
                    project(n, Wq, hb, "qt_ps")
                    if n and hb == 0:
                        read_state(n - 1)
                if n:
                    pe.wait_ge(sems["es_in"], n)
                for k in range(KC):
                    last = nc.tensor.matmul(bank[:, 6, :], xnT[:, k, t * P:(t + 1) * P], Wvg[:, k, :],
                                            start=(k == 0), stop=(k == KC - 1))
                last.then_inc(sems["vg_ps"], 1)
                if n == 0:
                    pe.wait_ge(sems["eb_in"], 1)
                    turn(1, 1, 2, "xnT_ps")
                for hb in range(2):
                    pe.wait_ge(sems["q_in"], 2 * n + hb + 1)
                    for h in range(hb * HH, hb * HH + HH):
                        last = nc.tensor.transpose(bank[:, 4 + hb, (h % HH) * P:(h % HH + 1) * P], kk[:, h, :], ident)
                    last.then_inc(sems["tr_ps"], 1)
                if n == 0:
                    low_rank(2)
                pe.wait_ge(sems["qq_in"], 2 * n + 2)
                pe.wait_ge(sems["eb_in"], n + 1)
                for h in range(H):
                    last = nc.tensor.matmul(bank[:, 2 + h // HH, (h % HH) * P:(h % HH + 1) * P],
                                            kk[:, h, :], qq[:, h, :], start=True, stop=True)
                last.then_inc(sems["p_ps"], 1)
                pe.wait_ge(sems["vg_in"], n + 1)
                pe.wait_ge(sems["vbd_in"], n + 1)
                pe.wait_ge(sems["kkT_in"], 2 * n + 2)
                for h in range(H):
                    last = nc.tensor.matmul(bank[:, 6, h * 2 * DV:(h + 1) * 2 * DV], kkT[:, h, :],
                                            vbd[:, h, :, :].rearrange("p c e -> p (c e)"), start=True, stop=True)
                last.then_inc(sems["u_state"], 1)

            def up(s, g):
                c, m = g // FT, g % FT
                r = rows_of(m)
                pe.wait_ge(sems[f"xl_in{s}"], KC * (c + 1))
                if g >= 2:
                    pe.wait_ge(sems[f"hid_in{s}"], g - 1)
                for j, w in enumerate((W1, W2)):
                    for k in range(KC):
                        for part, xp in enumerate((xh, xl)):
                            last = nc.tensor.matmul(bank[0:r, up_bank(g) + j, :],
                                                    w[:, k, m * P:m * P + r], xp[:, k, c * HT:(c + 1) * HT],
                                                    start=(k == 0 and part == 0), stop=(k == KC - 1 and part == 1))
                last.then_inc(sems[f"up_ps{s}"], 1)

            def down(s, t):
                pe.wait_ge(sems[f"hl_in{s}"], FT * (t // HTT + 1))
                if t >= 2:
                    pe.wait_ge(sems[f"res_in{s}"], t - 1)
                for m in range(FT):
                    r = rows_of(m)
                    for part, hp in enumerate((hTh, hTl)):
                        last = nc.tensor.matmul(bank[:, 6 + t % 2, 0:D], hp[0:r, m, t * P:(t + 1) * P],
                                                W3[0:r, m, :], start=(m == 0 and part == 0),
                                                stop=(m == FT - 1 and part == 1))
                last.then_inc(sems[f"down_ps{s}"], 1)

            pe.wait_ge(ternary, len(raw_parts))
            turn_y(NT - 2)
            up(2, 0)
            project_y(NT - 2)
            read_state(NT - 1)
            pe.wait_ge(sems["cs_in"], NT)
            up(2, 1)
            for g in range(2, FT):
                up(2, g)
            turn_y(NT - 1)
            project_y(NT - 1)
            pe.wait_ge(sems["res_in1"], NT)
            down(2, 0)
            down(2, 1)
            turn(2, 1, 0, "xT_ps2")
            down(2, 2)
            down(2, 3)
            for g in range(FT, UPS):
                up(2, g)

            def qkv(t):
                pe.wait_ge(sems["xT3_in"], KC * (t // HTT + 1))
                if t >= 2:
                    pe.wait_ge(sems["v_in"], t - 1)
                else:
                    pe.wait_ge(sems["hid_in2"], UPS)
                for k in range(KC):
                    last = nc.tensor.matmul(bank[:, 2 + t % 2, :], xnT[:, k, t * P:(t + 1) * P], Wqkv[:, k, :],
                                            start=(k == 0), stop=(k == KC - 1))
                last.then_inc(sems["qkv_ps"], 1)

            def turn_stack(t):
                pe.wait_ge(sems["stk_in"], t + 1)
                if t == 0:
                    pe.wait_ge(sems["res_in2"], NT)
                for j in range(3):
                    if t and j < 2:
                        pe.wait_ge(sems["qT_in"], 2 * (t - 1) + j + 1)
                    elif t:
                        pe.wait_ge(sems["kT_in"], t)
                    pb = bank[0:SK, 4 + j, :].bitcast(BF16)
                    for h in range(8):
                        last = nc.tensor.transpose(
                            pb[:, h * P:(h + 1) * P],
                            stk[:, t % 2, 8 * j + h, :, :].rearrange("p s d -> p (s d)"), identb[:, :])
                    last.then_inc(sems["stk_ps"], 1)

            def row_scores(a):
                b, qt, g = a // 16, a // 8 % 2, a % 8
                if a >= 2:
                    pe.wait_ge(sems["max_in"], a - 1)
                else:
                    pe.wait_ge(sems["xT3_in"], 2 * KC)
                if a and a % ROWS == 0:
                    pe.wait_ge(sems["mT_in"], a // ROWS)
                k0 = b * T
                pe.wait_ge(sems["qT_in"], 2 * TT * (b + 1))
                pe.wait_ge(sems["kT_in"], TT * (b + 1))
                for h2 in range(2):
                    last = nc.tensor.matmul(bank[:, a % 2, h2 * T:(h2 + 1) * T],
                                            qkT[0:SK, 2 * g + h2, k0 + qt * P:k0 + (qt + 1) * P],
                                            qkT[0:SK, QH + g, k0:k0 + T], start=True, stop=True)
                last.then_inc(sems["row_ps"], 1)

            def turn_max(b):
                pe.wait_ge(sems["nm3_in"], b + 1)
                pb = bank[0:3 * QH, 0, :].bitcast(BF16)
                for qt in range(TT):
                    last = nc.tensor.transpose(pb[:, qt * P:(qt + 1) * P],
                                               nm3[:, qt, :, :].rearrange("p s h -> p (s h)"), identb[:, :])
                last.then_inc(sems["mT_ps"], 1)

            def scores(u):
                b, g = u // VH, u % VH
                pe.wait_ge(sems["row_parts"], 48 * (b + 1))
                if u == 0:
                    pe.wait_ge(sems["unit_rows"], NT)
                if u >= 2:
                    pe.wait_ge(sems["prob_in"], u - 1)
                k0 = b * T
                for kt in range(TT):
                    dst = bank[:, 2 + 2 * (u % 2) + kt, :].rearrange("p (h q) -> p h q", h=2)
                    last = nc.tensor.matmul(dst, qkT[:, QH + g, k0 + kt * P:k0 + (kt + 1) * P],
                                            qkT[:, 2 * g:2 * g + 2, k0:k0 + T], start=True, stop=True)
                last.then_inc(sems["sc_ps"], 1)

            def values(u):
                b, g = u // VH, u % VH
                pe.wait_ge(sems["pl_in"], lows(u + 1))
                if pool_low(u):
                    pe.wait_ge(sems["pl_pool"], pool_lows(u + 1))
                pe.wait_ge(sems["vs_in"], TT * (b + 1))
                if u >= VH // 2 and g % (VH // 2) == 0:
                    pe.wait_ge(sems["oS_in"], u // (VH // 2))
                for h2 in range(2):
                    c = (2 * (g % (VH // 2)) + h2) * VW
                    for qt in range(TT):
                        for kt in range(TT):
                            for part, pr in enumerate((prob_h, prob_l)):
                                last = nc.tensor.matmul(bank[:, 6 + qt, c:c + VW],
                                                        pr[:, u % 4, kt, h2, qt * P:(qt + 1) * P],
                                                        v3[:, b * TT + kt, g, :], start=(kt == 0 and part == 0),
                                                        stop=(kt == TT - 1 and part == 1))
                last.then_inc(sems["pv_ps"], 1)

            def turn_o(b, rows):
                pe.wait_ge(sems["oS_in"], 2 * b + 2)
                pe.wait_ge(sems["max_in"], rows)
                for qt in range(TT):
                    for k in range(KC):
                        last = nc.tensor.transpose(bank[:, 0, (qt * KC + k) * P:(qt * KC + k + 1) * P],
                                                   oS[:, qt, k * P:(k + 1) * P], ident)
                last.then_inc(sems["oT_ps"], 1)

            def project_o(b):
                pe.wait_ge(sems["oT_in"], b + 1)
                for qt in range(TT):
                    for k in range(KC):
                        last = nc.tensor.matmul(bank[:, 1, qt * D:(qt + 1) * D], oT[:, qt, k, :], Wob[:, k, :],
                                                start=(k == 0), stop=(k == KC - 1))
                last.then_inc(sems["bo_ps"], 1)

            turn(3, 0, 0, "xT3_ps")
            down(2, 4)
            down(2, 5)
            pe.wait_ge(w_att, 64)
            pe.wait_ge(identity_b, 1)
            qkv(0)
            qkv(1)
            down(2, 6)
            down(2, 7)
            for t in range(NT):
                if t == 2:
                    pe.wait_ge(sems["xT3_in"], KC)
                    turn(3, 1, 0, "xT3_ps")
                if t + 2 < NT:
                    qkv(t + 2)
                if t < NT - 1:
                    for a in rows_at(t):
                        row_scores(a)
                turn_stack(t)
            turn_max(0)
            for a in rows_at(NT - 1):
                row_scores(a)
            pe.wait_ge(sems["qT_in"], 2 * NT)
            pe.wait_ge(sems["kT_in"], NT)
            for u in range(UNITS):
                b, g = u // VH, u % VH
                scores(u)
                if b and g == 4:
                    project_o(b - 1)
                    values(u - 2)
                    if next_row(u) < B * ROWS:
                        pe.wait_ge(sems["res_in3"], TT * b)
                if next_row(u) < B * ROWS:
                    row_scores(next_row(u))
                    row_scores(next_row(u) + 1)
                    if next_row(u + 1) % ROWS == 0:
                        turn_max(next_row(u) // ROWS)
                if u % 4 == 3:
                    values(u - 3)
                if u >= 2 and u % 4 != 2 and not (b and g == 4):
                    values(u - 2)
                if b and g == 3:
                    turn_o(b - 1, next_row(u + 1))
                if u == TURN_AT:
                    pe.wait_ge(sems["oT_in"], B - 1)
                    pe.wait_ge(sems["res_in3"], TT * (B - 1))
                    turn(4, 0, 0, "xT_ps4")
            values(UNITS - 2)
            values(UNITS - 1)
            pe.wait_ge(sems["prob_in"], UNITS)
            up(4, 0)
            pe.wait_ge(sems["xl_in4"], KC)
            turn_o(B - 1, B * ROWS)
            project_o(B - 1)
            for g in range(1, FT):
                up(4, g)
            pe.wait_ge(sems["res_in3"], NT)
            turn(4, 1, 0, "xT_ps4")
            pe.wait_ge(sems["oS_in"], 2 * B)
            down(4, 0)
            down(4, 1)
            for g in range(FT, UPS):
                up(4, g)
            for t in range(2, NT):
                down(4, t)

        @block.scalar
        def _(act):
            def turned(ps, done, c, b0):
                act.wait_ge(sems[ps], c + 1)
                for k in range(KC):
                    nc.scalar.activation(xnT[:, k, c * HT:(c + 1) * HT], bank[:, b0 + k, :],
                                         ACT.Copy).then_inc(sems[done], 1)

            def turned_low(i):
                b, tok = LOW_PARTS[i]
                act.wait_ge(sems["u_ps"], i + 1)
                nc.scalar.activation(uT[0:LOW, tok], bank[0:LOW, b, 0:tok.stop - tok.start],
                                     ACT.Copy).then_inc(sems["u_in"], 1)

            def magnitude(n):
                act.wait_ge(sems["gk_ps"], n + 1)
                if n:
                    act.wait_ge(sems["g_in"], n)
                nc.scalar.activation(absb, bank[:, 0:2, :].rearrange("p a n -> p (a n)"),
                                     ACT.Abs).then_inc(sems["abs_in"], 1)

            def decay(n):
                act.wait_ge(sems["abs_in"], n + 1)
                nc.scalar.activation(expb, absb, ACT.Exp, scale=-1.0).then_inc(sems["expg_in"], 1)
                act.wait_ge(sems["expg_in"], n + 1)
                nc.scalar.activation(absb, expb, ACT.Ln, bias=1.0).then_inc(sems["lng_in"], 1)

            def turned_y(n):
                act.wait_ge(sems["ytr_ps"], n + 1)
                nc.scalar.activation(yT[:, :, :].rearrange("p k t -> p (k t)"), bank[:, 7, 0:D],
                                     ACT.Copy).then_inc(sems["yT_in"], 1)

            def part_high(s, c):
                act.wait_ge(sems[f"xT_ps{s}"], c + 1)
                for k in range(KC):
                    nc.scalar.activation(xh[:, k, c * HT:(c + 1) * HT], bank[:, k, :],
                                         ACT.Copy, scale=XS).then_inc(sems[f"xh_in{s}"], 1)

            def square_y(n):
                act.wait_ge(sems["ycen_in"], n + 1)
                nc.scalar.activation(ysq[:, :, :], yb[:, :, :], ACT.Square).then_inc(sems["ysq_in"], 1)

            def root_y(n):
                act.wait_ge(sems["var_in"], n + 1)
                nc.scalar.activation(hl[:, :], hv[:, :], ACT.Ln, scale=1.0 / DV,
                                     bias=eps[:, :]).then_inc(sems["lv_in"], 1)
                act.wait_ge(sems["lv_in"], n + 1)
                nc.scalar.activation(hy[:, :], hl[:, :], ACT.Exp, scale=-0.5).then_inc(sems["root_in"], 1)

            def gate_y(n):
                act.wait_ge(sems["z_in"], n + 1)
                nc.scalar.activation(ysq[:, :, :], ya[:, :, :], ACT.Exp, scale=-1.0).then_inc(sems["silu_step"], 1)
                act.wait_ge(sems["silu_step"], 2 * n + 1)
                nc.scalar.activation(ysq[:, :, :], ysq[:, :, :], ACT.Ln, bias=1.0).then_inc(sems["silu_step"], 1)
                act.wait_ge(sems["silu_step"], 2 * n + 2)
                nc.scalar.activation(ysq[:, :, :], ysq[:, :, :], ACT.Exp, scale=-1.0).then_inc(sems["ez_in"], 1)

            act.preload_act_table_set("natural_log_exp_and_others")
            turned("xnT_ps", "xnT_in", 0, 4)
            act.wait_ge(padded, 3)
            turned_low(0)
            magnitude(0)
            decay(0)
            turned_low(1)
            act.wait_ge(fills, 2)
            for n in range(NT):
                if 0 < n < NT - 1:
                    magnitude(n + 1)
                act.wait_ge(sems["bt_ps"], n + 1)
                if n:
                    act.wait_ge(sems["eb_used"], n)
                cum = bank[:, 2:4, :].rearrange("p a (h t) -> p (a h) t", t=P)
                nc.scalar.activation(eN, cum, ACT.Exp, scale=-1.0).then_inc(sems["en_in"], 1)
                if n >= 2:
                    turned_y(n - 2)
                nc.scalar.activation(eB, cum, ACT.Exp).then_inc(sems["eb_in"], 1)
                if n == 0:
                    magnitude(1)
                if n + 1 < NT:
                    decay(n + 1)
                else:
                    part_high(2, 0)
                if n:
                    square_y(n - 1)
                for hb in range(2):
                    act.wait_ge(sems["qt_ps"], 2 * n + hb + 1)
                    nc.scalar.activation(qS[:, hb * HH:(hb + 1) * HH, :].rearrange("p h t -> p (h t)"),
                                         bank[:, 4 + hb, :], ACT.Copy).then_inc(sems["q_in"], 1)
                act.wait_ge(sems["vg_ps"], n + 1)
                if n:
                    act.wait_ge(sems["y1_in"], n)
                    act.wait_ge(sems["u_state"], n)
                else:
                    act.wait_ge(padded, 3)
                for c in range(2):
                    r = slice(c * CH, (c + 1) * CH)
                    last = nc.scalar.activation(vbd[r, :, c, :], bank[r, 6, 0:VD].rearrange("p (h e) -> p h e", h=H),
                                                ACT.Copy)
                last.then_inc(sems["vbd_in"], 1)
                nc.scalar.activation(vgS[:, :], bank[:, 6, :], ACT.Copy).then_inc(sems["vg_in"], 1)
                if n == 0:
                    turned("xnT_ps", "xnT_in", 1, 2)
                if n:
                    root_y(n - 1)
                for hb in range(2):
                    act.wait_ge(sems["tr_ps"], 2 * n + hb + 1)
                    nc.scalar.activation(kkT[:, hb * HH:(hb + 1) * HH, :].rearrange("p h t -> p (h t)"),
                                         bank[:, 4 + hb, :], ACT.Copy).then_inc(sems["kkT_in"], 1)
                if n:
                    gate_y(n - 1)
                if n == 0:
                    act.wait_ge(w_ffn, 64)
                    for j, (raw, _w, rows, a, b) in enumerate(raw_parts):
                        if j:
                            act.wait_ge(summed, j)
                        nc.scalar.activation(junk[0:rows, 0:b - a], raw.rearrange("p k n -> p (k n)")[0:rows, a:b],
                                             ACT.Abs, accum_out=asum[0:rows, j:j + 1]).then_inc(summed, 1)

            def sigmoid(s, g):
                r = rows_of(g % FT)
                act.wait_ge(sems[f"up_ps{s}"], g + 1)
                if g >= 2:
                    act.wait_ge(sems[f"hid_in{s}"], g - 1)
                nc.scalar.activation(sg[0:r, g % 2, :], bank[0:r, up_bank(g), :], ACT.Sigmoid,
                                     scale=1.0 / XS).then_inc(sems[f"sig_in{s}"], 1)

            def high(s, g):
                c, m, r = g // FT, g % FT, rows_of(g % FT)
                act.wait_ge(sems[f"hid_in{s}"], g + 1)
                nc.scalar.activation(hTh[0:r, m, c * HT:(c + 1) * HT], hf[0:r, g % 2, :],
                                     ACT.Copy).then_inc(sems[f"hh_in{s}"], 1)

            turned_y(NT - 2)
            sigmoid(2, 0)
            sigmoid(2, 1)
            square_y(NT - 1)
            high(2, 0)
            sigmoid(2, 2)
            high(2, 1)
            sigmoid(2, 3)
            high(2, 2)
            sigmoid(2, 4)
            act.wait_ge(sems["z_in"], NT)
            nc.scalar.activation(ysq[:, :, :], ya[:, :, :], ACT.Sigmoid).then_inc(sems["ez_in"], 1)
            high(2, 3)
            sigmoid(2, 5)
            high(2, 4)
            turned_y(NT - 1)
            high(2, 5)
            part_high(2, 1)
            for g in range(FT, UPS):
                sigmoid(2, g)
                if g > FT:
                    high(2, g - 1)
            high(2, UPS - 1)

            def qkv_in(t):
                act.wait_ge(sems["qkv_ps"], t + 1)
                if t >= 2:
                    act.wait_ge(sems["rope_used"], t - 1)
                    act.wait_ge(sems["rope_b"], t - 1)
                    act.wait_ge(sems["vs_in"], t - 1)
                src = bank[:, 2 + t % 2, :]
                nc.scalar.activation(qk[:, t % 2, :, :].rearrange("p h d -> p (h d)"), src[:, 0:QK],
                                     ACT.Copy).then_inc(sems["qk_in"], 1)
                nc.scalar.activation(vf[:, t % 2, :, :], src[:, QK:].rearrange("p (h d) -> p h d", d=HD),
                                     ACT.Copy).then_inc(sems["v_in"], 1)

            def stacked(t):
                for j in range(2):
                    act.wait_ge(sems["stk_ps"], 3 * t + j + 1)
                    nc.scalar.activation(qkT[0:SK, 8 * j:8 * j + 8, t * P:(t + 1) * P],
                                         bank[0:SK, 4 + j, :].bitcast(BF16).rearrange("p (h q) -> p h q", q=P),
                                         ACT.Copy).then_inc(sems["qT_in"], 1)

            act.preload_act_table_set("natural_log_exp_and_others")
            turned("xT3_ps", "xT3_in", 0, 0)
            qkv_in(0)
            for t in range(NT):
                s2, q2, r2 = stk[:, t % 2], ra[:, t % 2], rb[:, t % 2]
                act.wait_ge(sems["rot_in"], t + 1)
                if t >= 2:
                    act.wait_ge(sems["stk_ps"], 3 * (t - 1))
                nc.scalar.activation(s2[:, 0:QH, 0:3, :], q2[:, 0:QH, None, :].broadcast_to([P, QH, 3, HD]), ACT.Copy)
                nc.scalar.activation(s2[:, QH:, 0:4:3, :], q2[:, QH:, None, :].broadcast_to([P, VH, 2, HD]), ACT.Copy)
                nc.scalar.activation(s2[:, QH:, 5, :], q2[:, QH:, :], ACT.Copy).then_inc(sems["hi_in"], 1)
                if t == 2:
                    turned("xT3_ps", "xT3_in", 1, 0)
                if t + 1 < NT:
                    qkv_in(t + 1)
                act.wait_ge(sems["mid_in"], t + 1)
                nc.scalar.activation(s2[:, 0:QH, 3:5, :], r2[:, 0:QH, None, :].broadcast_to([P, QH, 2, HD]), ACT.Copy)
                nc.scalar.activation(s2[:, QH:, 1:5:3, :], r2[:, QH:, None, :].broadcast_to([P, VH, 2, HD]),
                                     ACT.Copy).then_inc(sems["lo_in"], 1)
                if t:
                    stacked(t - 1)
            stacked(NT - 1)

            def turned_o(b):
                act.wait_ge(sems["oT_ps"], b + 1)
                nc.scalar.activation(oT[:, :, :, :].rearrange("p a k t -> p (a k t)"), bank[:, 0, :],
                                     ACT.Copy).then_inc(sems["oT_in"], 1)

            for u in range(UNITS):
                b, g = u // VH, u % VH
                act.wait_ge(sems["sc_ps"], u + 1)
                if u >= 3:
                    act.wait_ge(sems["pl_in"], max(1, lows(u - 2)))
                    if pool_low(u - 3):
                        act.wait_ge(sems["pl_pool"], pool_lows(u - 2))
                b0 = 2 + 2 * (u % 2)
                nc.scalar.activation(prob[:, u % 3, :, :, :].rearrange("p k h q -> p (k h q)"),
                                     bank[:, b0:b0 + 2, :].rearrange("p a n -> p (a n)"), ACT.Exp,
                                     bias=shift[:, :], scale=HD ** -0.5).then_inc(sems["prob_in"], 1)
                if u >= 4:
                    act.wait_ge(sems["pv_ps"], u - 3)
                act.wait_ge(sems["prob_in"], u + 1)
                nc.scalar.activation(prob_h[:, u % 4, :, :, :].rearrange("p k h q -> p (k h q)"),
                                     prob[:, u % 3, :, :, :].rearrange("p k h q -> p (k h q)"),
                                     ACT.Copy).then_inc(sems["ph_in"], 1)
                if b and g == 3:
                    turned_o(b - 1)
                if u == TURN_AT:
                    part_high(4, 0)
            act.preload_act_table_set("sigmoid_and_others")
            sigmoid(4, 0)
            turned_o(B - 1)
            for g in range(1, UPS):
                sigmoid(4, g)
                if g != FT:
                    high(4, g - 1)
                if g == FT - 1:
                    high(4, g)
                    part_high(4, 1)
            high(4, UPS - 1)

        @block.vector
        def _(dve):
            links = [0]

            def link(ins):
                links[0] += 1
                ins.then_inc(sems["vec"], 1)
                dve.wait_ge(sems["vec"], links[0])

            steps = {}

            def norm_steps(s, c, count):
                src = X[s - 1]
                var = mv[:, c * HTT:(c + 1) * HTT, 1]
                for _ in range(count):
                    i, waited = steps.get((s, c), (0, 0))
                    if i >= NORM_STEPS:
                        return
                    if i >= HTT:
                        dve.wait_ge(sems["vec"], waited)
                    if i < HTT:
                        t = c * HTT + i
                        if s == 1:
                            dve.wait_ge(sems[f"x_in{min(t, HTT)}"], 16)
                        elif s == 2:
                            dve.wait_ge(sems["res_in1"], ORDER.index(t) + 1)
                        else:
                            dve.wait_ge(sems[f"res_in{s - 1}"], t + 1)
                        last = nc.vector.bn_stats(st6[:, t, :], src[:, t, :])
                    elif i == HTT:
                        for t in range(c * HTT, (c + 1) * HTT):
                            last = nc.vector.bn_aggr(mv[:, t, :], st6[:, t, :])
                    elif i == HTT + 1:
                        last = nc.vector.tensor_scalar(nv[:, :], var, LN_EPS, None, ALU.add)
                    elif i == HTT + 2:
                        last = nc.vector.tensor_scalar(nh[:, :], nv[:, :].bitcast(I32), 1, None,
                                                       ALU.logical_shift_right)
                    elif i == HTT + 3:
                        last = nc.vector.tensor_scalar(ny[:, :].bitcast(I32), nh[:, :], -1.0, float(0x5F3759DF),
                                                       ALU.mult, ALU.add)
                    elif i < HTT + 13 and (i - HTT) % 3 == 1:
                        last = nc.vector.tensor_tensor(na[:, :], ny[:, :], ny[:, :], ALU.mult)
                    elif i < HTT + 13 and (i - HTT) % 3 == 2:
                        last = nc.vector.scalar_tensor_tensor(out=na[:, :], in0=na[:, :], scalar=-0.5, in1=nv[:, :],
                                                              op0=ALU.mult, op1=ALU.mult)
                    elif i < HTT + 13:
                        last = nc.vector.scalar_tensor_tensor(out=ny[:, :], in0=na[:, :], scalar=1.5, in1=ny[:, :],
                                                              op0=ALU.add, op1=ALU.mult)
                    else:
                        j = i - HTT - 13
                        t = c * HTT + j
                        last = nc.vector.tensor_scalar(xn[:, t, :], src[:, t, :], mv[:, t, 0:1], ny[:, j:j + 1],
                                                       ALU.subtract, ALU.mult)
                    if i >= HTT + 13:
                        last.then_inc(sems[f"xn_in{s}"], 1)
                        steps[s, c] = (i + 1, waited)
                    else:
                        last.then_inc(sems["vec"], 1)
                        links[0] += 1
                        steps[s, c] = (i + 1, links[0])

            def log_gate(n):
                dve.wait_ge(sems["lng_in"], n + 1)
                if n:
                    dve.wait_ge(sems["bt_ps"], n)
                nc.vector.scalar_tensor_tensor(out=gS, in0=bank[:, 0:2, :].rearrange("p a n -> p (a n)"),
                                               scalar=0.0, in1=absb, op0=ALU.min,
                                               op1=ALU.subtract).then_inc(sems["g_in"], 1)

            def residual_y(n):
                dve.wait_ge(sems["wo_ps"], n + 1)
                t = ORDER[n]
                nc.vector.tensor_tensor(X[1][:, t, :], bank[:, 7, 0:D], X[0][:, t, :],
                                        ALU.add).then_inc(sems["res_in1"], 1)

            def head_bc(v):
                return v[:, :, None].broadcast_to([P, H, DV])

            def add_state(n):
                dve.wait_ge(sems["o_ps"], n + 1)
                dve.wait_ge(sems["y1_in"], n + 1)
                o = bank[:, 7, :].rearrange("p (h c e) -> p h c e", h=H, c=2)
                for c in range(2):
                    r = slice(c * CH, (c + 1) * CH)
                    last = nc.vector.tensor_tensor(ya[r, :, :], o[r, :, c, :], y1[r, :, :], ALU.add)
                last.then_inc(sems["o_used"], 1)
                dve.wait_ge(sems["o_used"], n + 1)

            def centre_y(n):
                link(nc.vector.tensor_reduce(hm[:, :], ya[:, :, :], AX_X, ALU.add))
                nc.vector.scalar_tensor_tensor(out=yb[:, :, :], in0=head_bc(hm), scalar=-1.0 / DV, in1=ya[:, :, :],
                                               op0=ALU.mult, op1=ALU.add).then_inc(sems["ycen_in"], 1)

            def variance_y(n):
                dve.wait_ge(sems["ysq_in"], n + 1)
                nc.vector.tensor_reduce(hv[:, :], ysq[:, :, :], AX_X, ALU.add).then_inc(sems["var_in"], 1)

            def scale_y(n):
                if n + 1 < NT:
                    dve.wait_ge(sems["root_in"], n + 1)
                link(nc.vector.tensor_tensor(yb[:, :, :], yb[:, :, :], head_bc(hy), ALU.mult))
                link(nc.vector.tensor_tensor(yb[:, :, :], yb[:, :, :],
                                             lnw[:, None, :].broadcast_to([P, H, DV]), ALU.mult))
                nc.vector.tensor_tensor(ya[:, :, :], yb[:, :, :],
                                        lnb[:, None, :].broadcast_to([P, H, DV]), ALU.add).then_inc(sems["z_in"], 1)

            def silu_y(n):
                dve.wait_ge(sems["ez_in"], n + 1)
                nc.vector.tensor_tensor(yS[:, :, :], ya[:, :, :], ysq[:, :, :], ALU.mult).then_inc(sems["ys_in"], 1)
                dve.wait_ge(sems["ys_in"], n + 1)

            def part_low(s, c):
                for k in range(KC):
                    dve.wait_ge(sems[f"xh_in{s}"], KC * c + k + 1)
                    tok = slice(c * HT, (c + 1) * HT)
                    nc.vector.scalar_tensor_tensor(out=xl[:, k, tok], in0=bank[:, k, :], scalar=XS, in1=xh[:, k, tok],
                                                   op0=ALU.mult, op1=ALU.subtract).then_inc(sems[f"xl_in{s}"], 1)

            def state(n):
                dve.wait_ge(sems["u_state"], n + 1)
                if n:
                    dve.wait_ge(sems["o_ps"], n)
                u = bank[:, 6, :].rearrange("p (h c e) -> p h c e", h=H, c=2)
                Sb = S[n % 2]
                for c in range(2):
                    el = head_bc(eL[:, :, c])
                    if n % 4 < 2 and c == 0:
                        link(nc.vector.tensor_tensor(Sb[:, :, :], u[:, :, c, :], el, ALU.mult))
                    else:
                        link(nc.vector.tensor_tensor(su[:, :, :], u[:, :, c, :], Sb[:, :, :], ALU.add))
                        link(nc.vector.tensor_tensor(Sb[:, :, :], su[:, :, :], el, ALU.mult))
                    last = nc.vector.tensor_tensor(eS[:, :, c, :], Sb[:, :, :], el, ALU.mult)
                last.then_inc(sems["es_in"], 1)
                dve.wait_ge(sems["es_in"], n + 1)

            def thresholds_of_weights():
                dve.wait_ge(totals, 1)
                for k in range(6):
                    s = -0.5 if k > 2 else 0.5
                    last = nc.vector.tensor_scalar(thr[:, k:k + 1], bank[:, 7, k % 3:k % 3 + 1],
                                                   s / (F * D), s * QEPS, ALU.mult, ALU.add)
                link(last)
                for k in (2, 5):
                    s = -0.5 if k > 2 else 0.5
                    last = nc.vector.scalar_tensor_tensor(
                        out=thr[:, k:k + 1], in0=bank[:, 7, 3:4], scalar=s / (F * D),
                        in1=thr[:, k:k + 1], op0=ALU.mult, op1=ALU.add)
                last.then_inc(thresholds, 1)
                dve.wait_ge(thresholds, 1)

            def quantise(j):
                raw, w, rows, a, b = raw_parts[j]
                k = min(j, 2)
                r = raw.rearrange("p k n -> p (k n)")[0:rows, a:b]
                q = w[:, :, :].rearrange("p k n -> p (k n)")[0:rows, a:b]
                below = qtmp[0:rows, 0:b - a]
                link(nc.vector.tensor_scalar(below, r, thr[0:rows, 3 + k:4 + k], None, ALU.is_lt))
                nc.vector.scalar_tensor_tensor(out=q, in0=r, scalar=thr[0:rows, k:k + 1], in1=below,
                                               op0=ALU.is_gt, op1=ALU.subtract).then_inc(ternary, 1)
                dve.wait_ge(ternary, j + 1)

            def split_rows(out, src, res, off):
                link(nc.vector.tensor_copy(out, src))
                link(nc.vector.scalar_tensor_tensor(out=res, in0=out, scalar=off[:, 0:1], in1=src,
                                                    op0=ALU.mult, op1=ALU.add))
                link(nc.vector.tensor_copy(out, res))
                return nc.vector.scalar_tensor_tensor(out=out, in0=out, scalar=off[:, 1:2], in1=res,
                                                      op0=ALU.mult, op1=ALU.add)

            def stack_low(i):
                b, tok = LOW_PARTS[i]
                size = tok.stop - tok.start
                dve.wait_ge(sems["u_ps"], i + 1)
                dve.wait_ge(sems["u_in"], 2)
                split_rows(uS[0:GS, tok], bank[0:GS, b, 0:size], resg[0:GS, 0:size],
                           off_u[0:GS, :]).then_inc(sems["us_in"], 1)
                dve.wait_ge(sems["us_in"], i)

            norm_steps(1, 0, NORM_STEPS)
            dve.wait_ge(w_gate, 48)
            nc.vector.tensor_copy(Wg1s[:, :, :, :], Wg1[:, :, None, :].broadcast_to(
                [P, KC, GP, LOW])).then_inc(sems["wg1s_in"], 1)
            norm_steps(1, 1, NORM_STEPS)
            dve.wait_ge(w_const, 16)
            dve.wait_ge(w_stack, 16 * (GP + 3))
            split_rows(Wg2s[:, :], rawg, resg, off_w).then_inc(sems["wg2s_in"], 1)
            dve.wait_ge(sems["wg2s_in"], 1)
            nc.vector.tensor_copy(identb[:, :], ident).then_inc(identity_b, 1)
            nc.vector.memset(shift[:, :], PSHIFT).then_inc(fills, 1)
            nc.vector.memset(eps[:, :], LN_EPS).then_inc(fills, 1)
            log_gate(0)
            stack_low(1)
            dve.wait_ge(w_gla, 48)
            for n in range(NT):
                dve.wait_ge(sems["en_in"], n + 1)
                if n:
                    dve.wait_ge(sems["p_ps"], n)
                for hb in range(2):
                    dve.wait_ge(sems["kt_ps"], 2 * n + hb + 1)
                    r = slice(hb * HH, (hb + 1) * HH)
                    nc.vector.tensor_tensor(kk[:, r, :], bank[:, 4 + hb, :].rearrange("p (h t) -> p h t", t=P),
                                            eN[:, r, :], ALU.mult).then_inc(sems["kk_in"], 1)
                if n >= 2:
                    residual_y(n - 2)
                if n == 1:
                    thresholds_of_weights()
                if n + 1 < NT:
                    log_gate(n + 1)
                else:
                    part_low(2, 0)
                if n == NT - 2:
                    norm_steps(2, 0, NORM_STEPS)
                if n:
                    add_state(n - 1)
                    centre_y(n - 1)
                dve.wait_ge(sems["eb_in"], n + 1)
                for hb in range(2):
                    dve.wait_ge(sems["q_in"], 2 * n + hb + 1)
                    r = slice(hb * HH, (hb + 1) * HH)
                    nc.vector.tensor_tensor(qq[:, r, :], qS[:, r, :], eB[:, r, :],
                                            ALU.mult).then_inc(sems["qq_in"], 1)
                    if n and hb == 0:
                        variance_y(n - 1)
                nc.vector.tensor_copy(eL[:, :, :], eB[:, :, CH - 1:P:CH]).then_inc(sems["eb_used"], 1)
                dve.wait_ge(sems["eb_used"], n + 1)
                if n:
                    scale_y(n - 1)
                if n == 0:
                    stack_low(2)
                dve.wait_ge(sems["p_ps"], n + 1)
                link(nc.vector.tensor_tensor(pm, bank[:, 2:4, :].rearrange("p a (h t) -> p (a h) t", t=P),
                                             submask[:, None, :].broadcast_to([P, H, P]), ALU.mult))
                if n:
                    dve.wait_ge(sems["y1_in"], n)
                nc.vector.tensor_reduce(cs[:, :], pm, AX_X, ALU.add).then_inc(sems["cs_in"], 1)
                dve.wait_ge(sems["cs_in"], n + 1)
                if n:
                    silu_y(n - 1)
                state(n)
                if 1 <= n <= len(raw_parts):
                    quantise(n - 1)
                if n == NT - 3:
                    norm_steps(2, 0, 10)

            def hidden(s, g):
                r = rows_of(g % FT)
                dve.wait_ge(sems[f"sig_in{s}"], g + 1)
                if g >= 2:
                    dve.wait_ge(sems[f"hl_in{s}"], g - 1)
                nc.vector.scalar_tensor_tensor(
                    out=hf[0:r, g % 2, :], in0=bank[0:r, up_bank(g) + 1, :], scalar=HS / XS,
                    in1=sg[0:r, g % 2, :], op0=ALU.mult, op1=ALU.mult).then_inc(sems[f"hid_in{s}"], 1)

            def low(s, g):
                c, m, r = g // FT, g % FT, rows_of(g % FT)
                dve.wait_ge(sems[f"hh_in{s}"], g + 1)
                tok = slice(c * HT, (c + 1) * HT)
                nc.vector.tensor_tensor(hTl[0:r, m, tok], hf[0:r, g % 2, :], hTh[0:r, m, tok],
                                        ALU.subtract).then_inc(sems[f"hl_in{s}"], 1)

            def residual(s, t):
                dve.wait_ge(sems[f"down_ps{s}"], t + 1)
                nc.vector.scalar_tensor_tensor(
                    out=X[s][:, t, :], in0=bank[:, 6 + t % 2, 0:D], scalar=1.0 / HS,
                    in1=X[s - 1][:, t, :], op0=ALU.mult, op1=ALU.add).then_inc(sems[f"res_in{s}"], 1)

            residual_y(NT - 2)
            hidden(2, 0)
            add_state(NT - 1)
            centre_y(NT - 1)
            hidden(2, 1)
            low(2, 0)
            variance_y(NT - 1)
            dve.wait_ge(sems["var_in"], NT)
            link(nc.vector.tensor_scalar(hv[:, :], hv[:, :], 1.0 / DV, LN_EPS, ALU.mult, ALU.add))
            hidden(2, 2)
            low(2, 1)
            rsqrt(link, hv[:, :], hh, hy[:, :], ha[:, :], 1)
            hidden(2, 3)
            newton(link, hv[:, :], hy[:, :], ha[:, :], 2)
            scale_y(NT - 1)
            low(2, 2)
            silu_y(NT - 1)
            hidden(2, 4)
            low(2, 3)
            norm_steps(2, 1, HTT - 1)
            hidden(2, 5)
            low(2, 4)
            residual_y(NT - 1)
            norm_steps(2, 1, 3)
            low(2, 5)
            norm_steps(2, 1, NORM_STEPS)
            residual(2, 0)
            residual(2, 1)
            part_low(2, 1)
            residual(2, 2)
            residual(2, 3)
            norm_steps(3, 0, 9)
            for g in range(FT, UPS):
                hidden(2, g)
                norm_steps(3, 0, 2)
                if g > FT:
                    low(2, g - 1)
                norm_steps(3, 0, 2)
            low(2, UPS - 1)

            def rope_a(t):
                dve.wait_ge(sems["qk_in"], t + 1)
                if t >= 2:
                    dve.wait_ge(sems["stk_in"], t - 1)
                nc.vector.tensor_tensor(ra[:, t % 2, :, :], qk[:, t % 2, :, :],
                                        cosT[:, t % TT, None, :].broadcast_to([P, QH + VH, HD]),
                                        ALU.mult).then_inc(sems["rope_used"], 1)

            def rotate(t):
                dve.wait_ge(sems["rope_used"], t + 1)
                dve.wait_ge(sems["rope_b"], t + 1)
                nc.vector.tensor_tensor(ra[:, t % 2, :, :], ra[:, t % 2, :, :], rb[:, t % 2, :, :],
                                        ALU.add).then_inc(sems["rot_in"], 1)

            def middle(t):
                dve.wait_ge(sems["hi_in"], t + 1)
                q2, r2, s2 = ra[:, t % 2], rb[:, t % 2], stk[:, t % 2]
                nc.vector.tensor_tensor(r2[:, 0:QH, :], q2[:, 0:QH, :], s2[:, 0:QH, 0, :], ALU.subtract)
                nc.vector.tensor_tensor(r2[:, QH:, :], q2[:, QH:, :], s2[:, QH:, 0, :],
                                        ALU.subtract).then_inc(sems["mid_in"], 1)

            def last_part(t):
                dve.wait_ge(sems["mid_in"], t + 1)
                dve.wait_ge(sems["lo_in"], t + 1)
                r2, s2 = rb[:, t % 2], stk[:, t % 2]
                nc.vector.tensor_tensor(s2[:, 0:QH, 5, :], r2[:, 0:QH, :], s2[:, 0:QH, 3, :], ALU.subtract)
                nc.vector.tensor_tensor(s2[:, QH:, 2, :], r2[:, QH:, :], s2[:, QH:, 1, :],
                                        ALU.subtract).then_inc(sems["stk_in"], 1)

            def stacked(t):
                dve.wait_ge(sems["stk_ps"], 3 * t + 3)
                nc.vector.tensor_copy(qkT[0:SK, QH:, t * P:(t + 1) * P],
                                      bank[0:SK, 6, :].bitcast(BF16).rearrange("p (h q) -> p h q", q=P)
                                      ).then_inc(sems["kT_in"], 1)

            def row_max(a):
                g = a % 8
                dve.wait_ge(sems["row_ps"], a + 1)
                nc.vector.tensor_reduce(nmx[:, a // 8, 2 * g:2 * g + 2],
                                        bank[:, a % 2, :].rearrange("p (h k) -> p h k", h=2), AX_X, ALU.max,
                                        negate=True).then_inc(sems["max_in"], 1)

            def split_max(b):
                dve.wait_ge(sems["max_in"], ROWS * (b + 1))
                src = nmx[:, b * TT:(b + 1) * TT, :]
                if b:
                    dve.wait_ge(sems["mT_ps"], b)
                link(nc.vector.tensor_copy(nm3[:, :, 0, :], src))
                link(nc.vector.tensor_tensor(nmr[:, :, :], src, nm3[:, :, 0, :], ALU.subtract))
                link(nc.vector.tensor_copy(nm3[:, :, 1, :], nmr[:, :, :]))
                nc.vector.tensor_tensor(nm3[:, :, 2, :], nmr[:, :, :], nm3[:, :, 1, :],
                                        ALU.subtract).then_inc(sems["nm3_in"], 1)

            def turned_max(b):
                dve.wait_ge(sems["mT_ps"], b + 1)
                nc.vector.tensor_copy(mT[:, b, :],
                                      bank[0:3 * QH, 0, :].bitcast(BF16)[:, 0:T]).then_inc(sems["mT_in"], 1)

            def normalise(w):
                b, hw = w // 2, w % 2
                dve.wait_ge(sems["pv_ps"], VH // 2 * (w + 1))
                if b and hw == 0:
                    dve.wait_ge(sems["oT_ps"], b)
                ov = bank[:, 6:8, 0:QH // 2 * VW].rearrange("p a (h e) -> p a h e", e=VW)
                nc.vector.reciprocal(rden[:, :, :], ov[:, :, :, VW - 1])
                for qt in range(TT):
                    last = nc.vector.tensor_reduce(
                        osum[:, qt, :, :], ov[:, qt, :, 0:3 * HD].rearrange("p h (s e) -> p h e s", s=3),
                        AX_X, ALU.add)
                link(last)
                for qt in range(TT):
                    last = nc.vector.tensor_tensor(
                        oS[:, qt, hw * D // 2:(hw + 1) * D // 2].rearrange("p (h e) -> p h e", e=HD),
                        osum[:, qt, :, :], rden[:, qt, :, None].broadcast_to([P, QH // 2, HD]), ALU.mult)
                last.then_inc(sems["oS_in"], 1)
                dve.wait_ge(sems["oS_in"], w + 1)

            def prob_low(u):
                if pool_low(u):
                    return
                dve.wait_ge(sems["ph_in"], u + 1)
                nc.vector.tensor_tensor(prob_l[:, u % 4, :, :, :].rearrange("p k h q -> p (k h q)"),
                                        prob[:, u % 3, :, :, :].rearrange("p k h q -> p (k h q)"),
                                        prob_h[:, u % 4, :, :, :].rearrange("p k h q -> p (k h q)"),
                                        ALU.subtract).then_inc(sems["pl_in"], 1)

            def residual_o(b):
                dve.wait_ge(sems["bo_ps"], b + 1)
                for qt in range(TT):
                    t = b * TT + qt
                    nc.vector.tensor_tensor(X[3][:, t, :], bank[:, 1, qt * D:(qt + 1) * D], X[2][:, t, :],
                                            ALU.add).then_inc(sems["res_in3"], 1)

            residual(2, 4)
            residual(2, 5)
            rope_a(0)
            residual(2, 6)
            rotate(0)
            residual(2, 7)
            for t in range(NT):
                middle(t)
                norm_steps(3, 1, 3)
                if t + 1 < NT:
                    rope_a(t + 1)
                norm_steps(3, 1, 3)
                if t + 1 < NT:
                    rotate(t + 1)
                last_part(t)
                norm_steps(3, 1, 3)
                norm_steps(3, 1, 3)
                if t:
                    stacked(t - 1)
                if t == 1:
                    norm_steps(3, 1, NORM_STEPS)
                for a in rows_at(t):
                    if a == ROWS:
                        split_max(0)
                        turned_max(0)
                    row_max(a)
            stacked(NT - 1)
            for u in range(UNITS):
                b, g = u // VH, u % VH
                if b and g == 4:
                    prob_low(u - 1)
                    residual_o(b - 1)
                if u % 4 == 2 and u > 2:
                    normalise(u // 4 - 1)
                if next_row(u) < B * ROWS:
                    row_max(next_row(u))
                    row_max(next_row(u) + 1)
                    if next_row(u + 1) % ROWS == 0:
                        split_max(next_row(u) // ROWS)
                if u and not (b and g == 4):
                    prob_low(u - 1)
                if next_row(u) < B * ROWS and next_row(u + 1) % ROWS == 0:
                    turned_max(next_row(u) // ROWS)
                if 2 * VH + 4 < u < TURN_AT:
                    norm_steps(4, 0, 4)
                if u == TURN_AT:
                    part_low(4, 0)
                    norm_steps(4, 1, TT)
            prob_low(UNITS - 1)
            normalise(2 * B - 1)
            hidden(4, 0)
            residual_o(B - 1)
            hidden(4, 1)
            low(4, 0)
            for g in range(2, UPS):
                hidden(4, g)
                norm_steps(4, 1, 3)
                if g != FT:
                    low(4, g - 1)
                norm_steps(4, 1, 3)
                if g == FT - 1:
                    low(4, g)
                    part_low(4, 1)
                    residual(4, 0)
                    residual(4, 1)
            low(4, UPS - 1)
            for t in range(2, NT):
                residual(4, t)

        @block.gpsimd
        def _(gp):
            nc.gpsimd.memset(Wg2[:, :], 0.0).then_inc(padded, 1)
            nc.gpsimd.memset(uT[:, :], 0.0)
            nc.gpsimd.memset(asum[:, :], 0.0)
            nc.gpsimd.memset(ones[:, :], 1.0)
            nc.gpsimd.memset(vbd[:, :, :, :], 0.0).then_inc(padded, 1)
            gp.wait_ge(padded, 2)
            nc.gpsimd.memset(uT[ONE_ROW:ONE_ROW + 1, :], 1.0).then_inc(padded, 1)
            gp.wait_ge(padded, 3)
            nc.gpsimd.memset(uS[GS:, :], 1.0).then_inc(padded, 1)
            gp.wait_ge(padded, 4)

            for n in range(NT):
                gp.wait_ge(sems["vg_in"], n + 1)
                v = vgS[:, 0:VD].rearrange("p (h e) -> p h e", h=H)
                g = vgS[:, VD:].rearrange("p (h e) -> p h e", h=H)
                gp.wait_ge(sems["cs_in"], n + 1)
                if n:
                    gp.wait_ge(sems["y1_in"], n)
                nc.gpsimd.tensor_tensor(y0[:, :, :], v, cs[:, :, None].broadcast_to([P, H, DV]),
                                        ALU.mult).then_inc(sems["pool_step"], 1)
                gp.wait_ge(sems["pool_step"], n + 1)
                if n:
                    gp.wait_ge(sems["o_used"], n)
                nc.gpsimd.tensor_tensor(y1[:, :, :], y0[:, :, :], g, ALU.add).then_inc(sems["y1_in"], 1)
                if n == 0:
                    gp.wait_ge(sems["y1_in"], 1)
                    nc.gpsimd.memset(v3[:, :, :, :], 1.0).then_inc(padded, 1)
                    gp.wait_ge(padded, 5)
            gp.wait_ge(w_const, 16)
            for t in range(NT):
                gp.wait_ge(sems["qk_in"], t + 1)
                if t >= 2:
                    gp.wait_ge(sems["stk_in"], t - 1)
                for e in range(2):
                    last = nc.gpsimd.tensor_tensor(
                        rb[:, t % 2, :, e:HD:2], qk[:, t % 2, :, 1 - e:HD:2],
                        sinT[:, t % TT, None, e:HD:2].broadcast_to([P, QH + VH, HD // 2]), ALU.mult)
                last.then_inc(sems["rope_b"], 1)
                gp.wait_ge(sems["v_in"], t + 1)
                vt = vf[:, t % 2, :, :]
                nc.gpsimd.tensor_copy(v3[:, t, :, 0:HD], vt).then_inc(sems["v_step"], 1)
                gp.wait_ge(sems["v_step"], 3 * t + 1)
                nc.gpsimd.tensor_tensor(vr[:, :, :], vt, v3[:, t, :, 0:HD], ALU.subtract).then_inc(sems["v_step"], 1)
                gp.wait_ge(sems["v_step"], 3 * t + 2)
                nc.gpsimd.tensor_copy(v3[:, t, :, HD:2 * HD], vr[:, :, :]).then_inc(sems["v_step"], 1)
                gp.wait_ge(sems["v_step"], 3 * t + 3)
                nc.gpsimd.tensor_tensor(v3[:, t, :, 2 * HD:3 * HD], vr[:, :, :], v3[:, t, :, HD:2 * HD],
                                        ALU.subtract).then_inc(sems["vs_in"], 1)
                gp.wait_ge(sems["vs_in"], t + 1)
                if t == 0:
                    gp.wait_ge(sems["res_in2"], NT)
                nc.gpsimd.memset(qkT[SK:SM, QH:, t * P:(t + 1) * P], 1.0).then_inc(sems["unit_rows"], 1)
                gp.wait_ge(sems["unit_rows"], t + 1)
            for u in range(POOL_UNTIL):
                if pool_low(u):
                    gp.wait_ge(sems["ph_in"], u + 1)
                    if u >= 4:
                        gp.wait_ge(sems["pv_ps"], u - 3)
                    nc.gpsimd.tensor_tensor(prob_l[:, u % 4, :, :, :].rearrange("p k h q -> p (k h q)"),
                                            prob[:, u % 3, :, :, :].rearrange("p k h q -> p (k h q)"),
                                            prob_h[:, u % 4, :, :, :].rearrange("p k h q -> p (k h q)"),
                                            ALU.subtract).then_inc(sems["pl_pool"], 1)
                    gp.wait_ge(sems["pl_pool"], pool_lows(u + 1))


def constants():
    r, c = np.arange(P)[:, None], np.arange(P)[None, :]
    tril = ((c >= r) & (c // CH == r // CH)).astype(np.float32) * np.float32(GATE)
    sub = ((c >= r) & (c // SC == r // SC)).astype(np.float32)
    inv = (1.0 / np.float32(10000.0) ** (np.arange(0, HD, 2, dtype=np.float32) / np.float32(HD))).astype(np.float32)
    ang = np.arange(T, dtype=np.float32)[:, None] * inv[None, :]
    cos = np.repeat(np.cos(ang), 2, axis=1).reshape(TT, P, HD).transpose(1, 0, 2).reshape(P, TT * HD)
    sin = np.stack([-np.sin(ang), np.sin(ang)], -1).reshape(TT, P, HD).transpose(1, 0, 2).reshape(P, TT * HD)
    eye = np.eye(P, dtype=np.float32)
    part = np.arange(P) // LOW
    bias = np.arange(P) - GS
    u_first, u_second = part >= 3, part == 5
    w_first = np.isin(part, (1, 2, 4)) & (bias < 0) | (bias >= 1)
    w_second = (part == 2) | (bias == 2)
    off = -np.stack([u_first, u_second, w_first, w_second], axis=1).astype(np.float32)
    cf = np.concatenate([eye, tril, sub, cos, sin, off], axis=1).astype(np.float32)
    return cf


def kernel(**inputs):
    import numpy as _np
    import concourse.bacc as _bacc
    from concourse import mybir as _mybir
    from concourse.bass_utils import run_bass_kernel_spmd as _run

    nc = _bacc.Bacc("TRN2", target_bir_lowering=False, num_devices=1)
    a = {k: _np.ascontiguousarray(v) for k, v in inputs.items()}
    cf = constants()
    p, q, f = "L0_attn_a_", "L0_attn_b_", "L0_ffn_"
    arrays = {
        "x": a[p + "hidden_states"], "wq": a[p + "Wq"], "wk": a[p + "Wk"], "wv": a[p + "Wv"], "wg": a[p + "Wg"],
        "wgk1": a[p + "Wgk1"], "wgk2": a[p + "Wgk2"], "bgk2": a[p + "bgk2"], "wo": a[p + "Wo"],
        "ln_w": a[p + "ln_w"], "ln_b": a[p + "ln_b"],
        "w1t": _np.ascontiguousarray(a[f + "w1"].T), "w2t": _np.ascontiguousarray(a[f + "w2"].T),
        "w3t": _np.ascontiguousarray(a[f + "w3"].T),
        "bwq": a[q + "wq"], "bwk": a[q + "wk"], "bwv": a[q + "wv"], "bwo": a[q + "wo"],
        "const_f": cf,
    }
    args = [nc.dram_tensor(f"in_{n}", v.shape, _mybir.dt.from_np(v.dtype), kind="ExternalInput").ap()
            for n, v in arrays.items()]
    y = nc.dram_tensor("out_0", a[p + "hidden_states"].shape, _mybir.dt.float32, kind="ExternalOutput").ap()
    build(nc, *args, y)
    r = _run(nc, [{f"in_{n}": v for n, v in arrays.items()}], core_ids=[0])
    return r.results[0]["out_0"]
```
